# Optimizing a Trainium2 kernel written in Bass

```python
import numpy as np
import jax
import jax.numpy as jnp

def _softmax(x, axis=-1):
    return jax.nn.softmax(x, axis=axis)

def _gelu(x):
    return jax.nn.gelu(x, approximate=True)

def _silu(x):
    return jax.nn.silu(x)

def _sigmoid(x):
    return jax.nn.sigmoid(x)

def _layernorm(x, axis=-1, eps=1e-05):
    m = jnp.mean(x, axis=axis, keepdims=True)
    v = jnp.var(x, axis=axis, keepdims=True)
    return (x - m) / jnp.sqrt(v + eps)

def _scatter_add(tgt, idx, src, axis=0):
    return tgt.at[idx].add(src)

def _segment_sum(src, seg, n):
    return jax.ops.segment_sum(src, seg, n)
kernel_name = 'mk_macaron_d1_jaxref_r8_fd63cd'

def setup_inputs(seed: int=0):
    np.random.seed(seed)
    _w = jnp.asarray

    def _L0_attn_setup():
        import jax, jax.numpy as jnp
        import numpy as np
        B, N, D = (2, 256, 128)
        H, FD, HD = (16, 16, 64)
        ENC = 64
        EPS = 1e-12
        RD = 4.0
        RRD = 2.0
        R2 = float(np.sqrt(2.0))

        def taylor_exp(x):
            x2 = (x[..., :, None] * x[..., None, :]).reshape(*x.shape[:-1], FD * FD) / R2
            return jnp.concatenate([jnp.ones_like(x[..., :1]), x / RRD, x2 / RD], axis=-1)
        key = jax.random.key(seed)
        ks = jax.random.split(key, 7)
        s = 1.0 / np.sqrt(D)
        x = jax.random.normal(ks[0], (B, N, D), dtype=jnp.float32)
        Wq = jax.random.normal(ks[1], (H * FD, D), dtype=jnp.float32) * s
        Wk = jax.random.normal(ks[2], (H * FD, D), dtype=jnp.float32) * s
        Wv = jax.random.normal(ks[3], (H * HD, D), dtype=jnp.float32) * s
        Wk_enc = jax.random.normal(ks[4], (H * FD, D), dtype=jnp.float32) * s
        Wv_enc = jax.random.normal(ks[5], (H * HD, D), dtype=jnp.float32) * s
        Wout = jax.random.normal(ks[6], (D, H * HD), dtype=jnp.float32) * s
        return {'x': x, 'Wq': Wq, 'Wk': Wk, 'Wv': Wv, 'Wk_enc': Wk_enc, 'Wv_enc': Wv_enc, 'Wout': Wout}
    _L0_attn_in = _L0_attn_setup()

    def _L0_ffn_setup():
        import jax, jax.numpy as jnp
        import numpy as np
        from math import ceil
        CAPACITY_FACTOR = 2.0
        MIN_CAPACITY = 4
        key = jax.random.key(seed)
        ks = jax.random.split(key, 4)
        B, S, D, Di, E = (4, 256, 128, 512, 8)
        x = jax.random.normal(ks[0], (B, S, D), dtype=jnp.float32)
        Wr = jax.random.normal(ks[1], (D, E), dtype=jnp.float32) * D ** (-0.5)
        W1 = jax.random.normal(ks[2], (E, D, Di), dtype=jnp.float32) * D ** (-0.5)
        b1 = jnp.zeros((E, Di), dtype=jnp.float32)
        W2 = jax.random.normal(ks[3], (E, Di, D), dtype=jnp.float32) * Di ** (-0.5)
        b2 = jnp.zeros((E, D), dtype=jnp.float32)
        return {'x': x, 'Wr': Wr, 'W1': W1, 'b1': b1, 'W2': W2, 'b2': b2}
    _L0_ffn_in = _L0_ffn_setup()
    _d = {'L0_attn_x': _L0_attn_in['x'], 'L0_attn_Wq': _L0_attn_in['Wq'], 'L0_attn_Wk': _L0_attn_in['Wk'], 'L0_attn_Wv': _L0_attn_in['Wv'], 'L0_attn_Wk_enc': _L0_attn_in['Wk_enc'], 'L0_attn_Wv_enc': _L0_attn_in['Wv_enc'], 'L0_attn_Wout': _L0_attn_in['Wout'], 'L0_ffn_Wr': _L0_ffn_in['Wr'], 'L0_ffn_W1': _L0_ffn_in['W1'], 'L0_ffn_b1': _L0_ffn_in['b1'], 'L0_ffn_W2': _L0_ffn_in['W2'], 'L0_ffn_b2': _L0_ffn_in['b2']}
    _x0 = _d['L0_attn_x']
    _d['L0_attn_x'] = jax.random.normal(jax.random.fold_in(jax.random.key(seed), 1), (16, 256, 128), dtype=_x0.dtype)
    del _x0
    return _d

def reference(L0_attn_x, L0_attn_Wq, L0_attn_Wk, L0_attn_Wv, L0_attn_Wk_enc, L0_attn_Wv_enc, L0_attn_Wout, L0_ffn_Wr, L0_ffn_W1, L0_ffn_b1, L0_ffn_W2, L0_ffn_b2):

    def _L0_attn_ref(x, Wq, Wk, Wv, Wk_enc, Wv_enc, Wout):
        import jax, jax.numpy as jnp
        import numpy as np
        B, N, D = (2, 256, 128)
        H, FD, HD = (16, 16, 64)
        ENC = 64
        EPS = 1e-12
        RD = 4.0
        RRD = 2.0
        R2 = float(np.sqrt(2.0))

        def taylor_exp(x):
            x2 = (x[..., :, None] * x[..., None, :]).reshape(*x.shape[:-1], FD * FD) / R2
            return jnp.concatenate([jnp.ones_like(x[..., :1]), x / RRD, x2 / RD], axis=-1)
        b, n, _ = x.shape
        q = (x @ Wq.T).reshape(b, n, H, FD).transpose(0, 2, 1, 3)
        k = (x @ Wk.T).reshape(b, n, H, FD).transpose(0, 2, 1, 3)
        v = (x @ Wv.T).reshape(b, n, H, HD).transpose(0, 2, 1, 3)
        x_enc = x[:, :ENC]
        k_enc = (x_enc @ Wk_enc.T).reshape(b, ENC, H, FD).transpose(0, 2, 1, 3)
        v_enc = (x_enc @ Wv_enc.T).reshape(b, ENC, H, HD).transpose(0, 2, 1, 3)
        k_enc_f = taylor_exp(k_enc)
        q_f = taylor_exp(q)
        k_f = taylor_exp(k)
        A_qk = jnp.einsum('bhnd,bhmd->bhnm', q_f, k_f)
        A_qk = jnp.tril(A_qk)
        y1 = jnp.einsum('bhnm,bhme->bhne', A_qk, v)
        A_qk2 = jnp.einsum('bhnd,bhmd->bhnm', q_f, k_enc_f)
        y2 = jnp.einsum('bhnm,bhme->bhne', A_qk2, v_enc)
        k_state = k_enc_f.sum(axis=2, keepdims=True) + jnp.cumsum(k_f, axis=2)
        z = 1.0 / ((q_f * k_state).sum(axis=-1) + EPS)
        out = (y1 + y2) * z[..., None]
        out = out.transpose(0, 2, 1, 3).reshape(b, n, H * HD)
        return out @ Wout.T

    def _L0_ffn_ref(x, Wr, W1, b1, W2, b2):
        import jax, jax.numpy as jnp
        import numpy as np
        from math import ceil
        CAPACITY_FACTOR = 2.0
        MIN_CAPACITY = 4
        B, S, D = x.shape
        E = Wr.shape[1]
        N = B * S
        k = max(MIN_CAPACITY, ceil(N * CAPACITY_FACTOR / E))
        xt = x.reshape(N, D)
        scores = jax.nn.softmax(xt @ Wr, axis=-1)
        G, idx = jax.lax.top_k(scores.T, k)
        X_in = xt[idx]
        h = jax.nn.gelu(jnp.einsum('ekd,edh->ekh', X_in, W1) + b1[:, None, :], approximate=False)
        X_e = jnp.einsum('ekh,ehd->ekd', h, W2) + b2[:, None, :]
        contrib = (G[..., None] * X_e).reshape(E * k, D)
        out = jnp.zeros((N, D), dtype=x.dtype).at[idx.reshape(-1)].add(contrib)
        return out.reshape(B, S, D)
    x = L0_attn_x
    x = x + 0.5 * _L0_ffn_ref(_layernorm(x, axis=-1), L0_ffn_Wr, L0_ffn_W1, L0_ffn_b1, L0_ffn_W2, L0_ffn_b2)
    x = x + _L0_attn_ref(_layernorm(x, axis=-1), L0_attn_Wq, L0_attn_Wk, L0_attn_Wv, L0_attn_Wk_enc, L0_attn_Wv_enc, L0_attn_Wout)
    x = x + 0.5 * _L0_ffn_ref(_layernorm(x, axis=-1), L0_ffn_Wr, L0_ffn_W1, L0_ffn_b1, L0_ffn_W2, L0_ffn_b2)
    return x

_drawn_inputs = setup_inputs


def setup_inputs(seed=0):
    import zlib

    import numpy as np

    out = dict(_drawn_inputs(seed))
    spreads = {'L0_ffn_b1': (0.0, 0.1), 'L0_ffn_b2': (0.0, 0.1)}
    factors = {}
    for name, (base, spread) in spreads.items():
        noise = np.random.default_rng([zlib.crc32(name.encode()), seed]).standard_normal(out[name].shape)
        drawn = base * np.exp(spread * noise) if base else spread * noise
        out[name] = jnp.asarray(drawn.astype(out[name].dtype))
    for name, factor in factors.items():
        out[name] = (out[name] * factor).astype(out[name].dtype)
    return out
```

```python
from contextlib import ExitStack

import concourse.bass as bass
from concourse import mybir

F32 = mybir.dt.float32
BF16 = mybir.dt.bfloat16
I32 = mybir.dt.int32
ALU = mybir.AluOpType
ACT = mybir.ActivationFunctionType
AX_X = mybir.AxisListType.X

P = 128
B, N, D = 16, 256, 128
T = B * N
C = T // P
E = 8
K = T * 2 // E
HID = 512
HC = HID // P
SL = K // P
ROW = D + E
H, FD, HD = 16, 16, 64
ENC = 64
PAIRS = H // 2
LN_EPS = 1e-5
Z_EPS = 1e-12
HEAD_SCALE = 1.0 / (2 * 4.0 ** 2) ** 0.5
HEAD_SHIFT = 0.25 / (2 * HEAD_SCALE)
HALF = 1.0 - HEAD_SHIFT ** 2
BITS = 30


class Steps:

    def __init__(self, engine, sem, start=0):
        self.engine, self.sem, self.n = engine, sem, start

    def done(self, instruction):
        instruction.then_inc(self.sem, 1)
        self.n = self.n + 1
        return self.n

    def after(self, value=None):
        self.engine.wait_ge(self.sem, self.n if value is None else value)



def wait_unless_first(engine, sem, value):
    if not (isinstance(value, int) and value == 0):
        engine.wait_ge(sem, value)


def ffn_stage(nc, name, consts, weights, psum, x_src, x_acc, copy_residual, table):
    src = x_src.rearrange("(c p) d -> p c d", p=P)
    acc = x_acc.rearrange("(c p) d -> p c d", p=P)
    QT = 4
    ident = consts["ident"]

    with ExitStack() as ctx:
        def sem(n):
            return ctx.enter_context(nc.semaphore(f"{name}_{n}"))

        def sb(n, shape, dt=F32):
            return ctx.enter_context(nc.sbuf_tensor(f"{name}_{n}", shape, dt))

        flat = C * E
        buf = {
            "xt": sb("xt", [P, C, D]), "rows": sb("rows", [P, C, ROW]), "stats": sb("stats", [P, C, 6]),
            "mv": sb("mv", [P, C, 2]), "rstd": sb("rstd", [P, C]), "std": sb("std", [P, C]),
            "tmp32": sb("tmp32", [P, 4, C]), "xnT": sb("xnT", [D, 1024]), "scores": sb("scores", [P, flat]),
            "work": sb("work", [P, 4, flat]), "sT": sb("sT", [P, flat]), "thr": sb("thr", [P, 1], I32),
            "cand": sb("cand", [P, 1], I32), "take": sb("take", [P, 1], I32), "cmp": sb("cmp", [P, flat]),
            "count": sb("count", [P, 1]), "thr_wide": sb("thr_wide", [P, P]), "thr_row": sb("thr_row", [P, E]),
            "gt": sb("gt", [P, flat], BF16), "eq": sb("eq", [P, flat], BF16), "sel": sb("sel", [P, flat], BF16),
            "before": sb("before", [P, flat], BF16), "need": sb("need", [P, E]), "need2": sb("need2", [P, E]),
            "need3": sb("need3", [P, E]), "slot_i": sb("slot_i", [P, flat], I32), "hi_i": sb("hi_i", [P, flat], I32),
            "lo_i": sb("lo_i", [P, flat], I32), "hi": sb("hi", [P, flat], BF16), "lo": sb("lo", [P, flat], BF16),
            "hi_hot": sb("hi_hot", [P, C, P], BF16), "lo_hot": sb("lo_hot", [P, C, SL], BF16),
            "lo_val": sb("lo_val", [P, C, 2 * SL], BF16), "list": sb("list", [P, 2 * SL]),
            "idx": sb("idx", [P, E * SL], I32), "gather_idx": [sb(f"gather_idx{u}", [P, SL], I32) for u in range(2)],
            "scatter_idx": [sb(f"scatter_idx{u}", [P, SL], I32) for u in range(2)],
            "tok": [sb(f"tok{u}", [P, SL, ROW]) for u in range(2)], "tokT": sb("tokT", [D, K]),
            "hidden": sb("hidden", [P, HC, K]), "yb": sb("yb", [P, SL, D]), "y": sb("y", [P, SL, D])}
        xt, scores, xnT = buf["xt"], buf["scores"], buf["xnT"]
        stats, mv, rstd, tmp32 = buf["stats"], buf["mv"], buf["rstd"], buf["tmp32"]
        x_in = [sem(f"x_in{i}") for i in range(4)]
        residual_out = sem("residual_out")
        table_out = sem("table_out")
        xn_ready = sem("xn_ready")
        xnT_psum = sem("xnT_psum")
        xnT_ready = sem("xnT_ready")
        logits_ready = sem("logits_ready")
        var_ready = sem("var_ready")
        std_ready = sem("std_ready")
        shifted_ready = sem("shifted_ready")
        exp_ready = sem("exp_ready")
        scores_ready = sem("scores_ready")
        scoresT_psum = sem("scoresT_psum")
        counts_ready = sem("counts_ready")
        total_ready = sem("total_ready")
        thr_ready = sem("thr_ready")
        thrT_ready = sem("thrT_ready")
        gt_ready = sem("gt_ready")
        gt_count = sem("gt_count")
        eq_ready = sem("eq_ready")
        eq_rank = sem("eq_rank")
        sel_ready = sem("sel_ready")
        sel_rank = sem("sel_rank")
        dve_step = sem("dve_step")
        onehot_ready = sem("onehot_ready")
        list_ready = sem("list_ready")
        idx_ready = sem("idx_ready")
        w1_in = [sem("w1_in0"), sem("w1_in1")]
        gathered = [sem("gathered0"), sem("gathered1")]
        idx_copied = sem("idx_copied")
        act_turn = sem("act_turn")
        pool_turn = sem("pool_turn")
        tokT_psum = sem("tokT_psum")
        tokT_ready = sem("tokT_ready")
        hidden_psum = sem("hidden_psum")
        hidden_ready = sem("hidden_ready")
        y_psum = sem("y_psum")
        y_biased = sem("y_biased")
        y_ready = sem("y_ready")
        scattered = sem("scattered")
        block = ctx.enter_context(nc.Block())

        logits = psum[7][:, 0:C * E]
        scoresT = psum[6][:, 0:2 * P]
        total = psum[5][:, 0:1]
        thr_psum = psum[5][:, 0:P]
        rank_psum = psum[4][:, 0:C * E]
        list_psum = psum[7][:, 0:2 * SL]

        @block.sync
        def _(sp):
            def load_w1(e, u):
                sp.dma_start(weights["w1"][u][:, :], weights["w1_dram"][bass.ds(e, 1), :, :]
                             .rearrange("e d h -> d (e h)")).then_inc(w1_in[u], 16)

            for u in range(2):
                load_w1(u, u)
            for i in range(4):
                part = slice(8 * i, 8 * i + 8)
                sp.dma_start(xt[:, part, :], src[:, part, :]).then_inc(x_in[i], 16)
            if copy_residual:
                for i in range(4):
                    sp.wait_ge(x_in[i], 16)
                sp.dma_start(acc, xt[:]).then_inc(residual_out, 16)
                sp.wait_ge(residual_out, 16)
            sp.wait_ge(scores_ready, 2)
            sp.dma_start(table.rearrange("(c p) r -> p c r", p=P), buf["rows"][:]).then_inc(table_out, 16)
            sp.wait_ge(table_out, 16)
            with sp.Fori(0, E // 2 - 1) as g:
                for u in range(2):
                    sp.wait_ge(hidden_psum, (g * 2 + u) * (2 * HC) + 2 * HC)
                    load_w1(g * 2 + (2 + u), u)

        @block.vector
        def _(dve):
            own = Steps(dve, dve_step)
            rows = buf["rows"]
            for i in range(4):
                dve.wait_ge(x_in[i], 16)
                for c in range(8 * i, 8 * i + 8):
                    last = own.done(nc.vector.bn_stats(stats[:, c, :], xt[:, c, :]))
            own.after(last)
            for c in range(C):
                last = own.done(nc.vector.bn_aggr(mv[:, c, :], stats[:, c, :]))
            own.after(last)
            var = mv[:, :, 1]
            own.done(nc.vector.tensor_scalar(tmp32[:, 0, :], var, LN_EPS, None, ALU.add))
            own.after()
            nc.vector.tensor_copy(tmp32[:, 1, :], tmp32[:, 0, :]).then_inc(var_ready, 1)
            dve.wait_ge(std_ready, 1)
            own.done(nc.vector.reciprocal(tmp32[:, 2, :], buf["std"][:, :]))
            own.after()
            own.done(nc.vector.tensor_tensor(tmp32[:, 3, :], tmp32[:, 0, :], tmp32[:, 2, :], ALU.mult))
            own.after()
            own.done(nc.vector.tensor_tensor(tmp32[:, 2, :], tmp32[:, 3, :], buf["std"][:, :], ALU.add))
            own.after()
            own.done(nc.vector.tensor_scalar(tmp32[:, 3, :], tmp32[:, 2, :], 0.5, None, ALU.mult))
            own.after()
            own.done(nc.vector.reciprocal(rstd[:, :], tmp32[:, 3, :]))
            own.after()
            for c in range(C):
                nc.vector.tensor_scalar(rows[:, c, 0:D], xt[:, c, :], mv[:, c, 0:1], rstd[:, c:c + 1],
                                        ALU.subtract, ALU.mult).then_inc(xn_ready, 1)
            dve.wait_ge(logits_ready, 1)
            lg = logits.rearrange("p (c e) -> p c e", e=E)
            work = buf["work"]
            w3 = [work[:, i, :].rearrange("p (c e) -> p c e", e=E) for i in range(4)]
            own.done(nc.vector.tensor_reduce(tmp32[:, 0, :], lg, AX_X, ALU.max))
            own.after()
            nc.vector.tensor_tensor(w3[0], lg, tmp32[:, 0, :].unsqueeze(2).broadcast_to([P, C, E]),
                                    ALU.subtract).then_inc(shifted_ready, 1)
            dve.wait_ge(exp_ready, 1)
            own.done(nc.vector.tensor_reduce(tmp32[:, 1, :], w3[1], AX_X, ALU.add))
            own.after()
            own.done(nc.vector.reciprocal(tmp32[:, 2, :], tmp32[:, 1, :]))
            own.after()
            inv = tmp32[:, 2, :].unsqueeze(2).broadcast_to([P, C, E])
            s3 = scores[:, :].rearrange("p (c e) -> p c e", e=E)
            nc.vector.tensor_tensor(s3, w3[1], inv, ALU.mult).then_inc(scores_ready, 1)
            nc.vector.tensor_tensor(rows[:, :, D:ROW], w3[1], inv, ALU.mult).then_inc(scores_ready, 1)
            sT = buf["sT"]
            own.done(nc.vector.memset(buf["thr"][:, :], 0))
            dve.wait_ge(scoresT_psum, 1)
            own.done(nc.vector.tensor_copy(sT[:, :], scoresT))
            own.after()
            start = own.n
            PER_BIT = 3
            with dve.Fori(0, BITS) as i:
                bit = Steps(dve, dve_step, i * PER_BIT + start)
                ib = consts["bits_i"][:, bass.ds(i, 1)]
                bit.done(nc.vector.tensor_tensor(buf["cand"][:, :], buf["thr"][:, :], ib, ALU.bitwise_or))
                bit.after()
                nc.vector.tensor_scalar(buf["cmp"][:, :], sT[:, :], buf["cand"][:, :].bitcast(F32), 0.0,
                                        ALU.is_ge, ALU.add, accum_out=buf["count"][:, :]).then_inc(counts_ready, 1)
                dve.wait_ge(total_ready, i + 1)
                bit.done(nc.vector.tensor_scalar(buf["take"][:, :], total, float(K),
                                                 consts["bits_f"][:, bass.ds(i, 1)], ALU.is_ge, ALU.mult))
                bit.after()
                bit.done(nc.vector.tensor_tensor(buf["thr"][:, :], buf["thr"][:, :], buf["take"][:, :],
                                                 ALU.bitwise_or))
                bit.after()
            own = Steps(dve, dve_step, start + BITS * PER_BIT)
            thr = buf["thr"][:, :].bitcast(F32)
            nc.vector.tensor_copy(buf["thr_wide"][:, :], thr.broadcast_to([P, P])).then_inc(thr_ready, 1)
            dve.wait_ge(thrT_ready, 1)
            own.done(nc.vector.tensor_copy(buf["thr_row"][:, :], thr_psum[:, 0:E]))
            own.after()
            s_ec = scores[:, :].rearrange("p (c e) -> p e c", e=E)
            thr_ec = buf["thr_row"][:, :].unsqueeze(2).broadcast_to([P, E, C])

            def ec(t):
                return t[:, :].rearrange("p (e c) -> p e c", e=E)

            nc.vector.tensor_tensor(ec(buf["gt"]), s_ec, thr_ec, ALU.is_gt).then_inc(gt_ready, 1)
            own.done(nc.vector.tensor_tensor(ec(buf["eq"]), s_ec, thr_ec, ALU.is_equal))
            own.after()

            def ec_psum(t):
                return t.rearrange("p (e c) -> p e c", e=E)

            def earlier_tiles(mask):
                own.done(nc.vector.tensor_tensor_scan(work[:, 0, :], consts["restart"][:, :], mask[:, :], 0.0,
                                                      ALU.mult, ALU.add))
                own.after()
                return nc.vector.tensor_tensor(buf["before"][:, :], work[:, 0, :], mask[:, :], ALU.subtract)

            earlier_tiles(buf["eq"]).then_inc(eq_ready, 1)
            dve.wait_ge(gt_count, 1)
            own.done(nc.vector.tensor_reduce(buf["need"][:, :], ec_psum(rank_psum), AX_X, ALU.add))
            own.after()
            own.done(nc.vector.tensor_scalar(buf["need2"][:, :], buf["need"][:, :], -1.0, float(K), ALU.mult, ALU.add))
            own.after()
            nc.vector.tensor_copy(buf["need3"][:, :], buf["need2"][:, :]).then_inc(eq_ready, 1)
            dve.wait_ge(eq_rank, 1)
            own.done(nc.vector.tensor_tensor(work[:, 1, :].rearrange("p (e c) -> p e c", e=E), ec_psum(rank_psum),
                                             buf["need2"][:, :].unsqueeze(2).broadcast_to([P, E, C]), ALU.is_le))
            own.after()
            own.done(nc.vector.tensor_tensor(work[:, 2, :], work[:, 1, :], buf["eq"][:, :], ALU.mult))
            own.after()
            own.done(nc.vector.tensor_tensor(buf["sel"][:, :], work[:, 2, :], buf["gt"][:, :], ALU.add))
            own.after()
            earlier_tiles(buf["sel"]).then_inc(sel_ready, 1)
            dve.wait_ge(sel_rank, 1)
            own.done(nc.vector.tensor_tensor(work[:, 1, :], rank_psum, buf["sel"][:, :], ALU.mult))
            own.after()
            own.done(nc.vector.tensor_scalar(buf["slot_i"][:, :], work[:, 1, :], -1.0, None, ALU.add))
            own.after()
            own.done(nc.vector.tensor_scalar(buf["hi_i"][:, :], buf["slot_i"][:, :], 3, None, ALU.arith_shift_right))
            own.done(nc.vector.tensor_scalar(buf["lo_i"][:, :], buf["slot_i"][:, :], SL - 1, None, ALU.bitwise_and))
            own.after()
            own.done(nc.vector.tensor_copy(buf["hi"][:, :], buf["hi_i"][:, :]))
            own.done(nc.vector.tensor_copy(buf["lo"][:, :], buf["lo_i"][:, :]))
            own.after()
            start = own.n
            PER_LIST = 2

            def build_list(e):
                own = Steps(dve, dve_step, e * PER_LIST + start)
                hi = buf["hi"][:, bass.ds(e * C, C)].unsqueeze(2).broadcast_to([P, C, P])
                lo = buf["lo"][:, bass.ds(e * C, C)].unsqueeze(2).broadcast_to([P, C, SL])
                own.done(nc.vector.tensor_tensor(buf["lo_hot"][:, :, :], consts["iota_f"][:, 0:SL].unsqueeze(1)
                                                 .broadcast_to([P, C, SL]), lo, ALU.is_equal))
                nc.vector.tensor_tensor(buf["hi_hot"][:, :, :], consts["iota_f"][:, :].unsqueeze(1)
                                        .broadcast_to([P, C, P]), hi, ALU.is_equal).then_inc(onehot_ready, 1)
                own.after()
                nc.vector.tensor_scalar(buf["lo_val"][:, :, 0:SL], buf["lo_hot"][:, :, :], consts["part"][:, 0:1],
                                        None, ALU.mult).then_inc(onehot_ready, 1)
                nc.vector.tensor_tensor(buf["lo_val"][:, :, SL:2 * SL], buf["lo_hot"][:, :, :],
                                        consts["iota_f"][:, 0:C].unsqueeze(2).broadcast_to([P, C, SL]),
                                        ALU.mult).then_inc(onehot_ready, 1)
                dve.wait_ge(list_ready, e + 1)
                own.done(nc.vector.tensor_copy(buf["list"][:, :], list_psum))
                own.after()
                nc.vector.scalar_tensor_tensor(buf["idx"][:, bass.ds(e * SL, SL)], buf["list"][:, SL:2 * SL], float(P),
                                               buf["list"][:, 0:SL], ALU.mult, ALU.add).then_inc(idx_ready, 1)

            def expert(e, u, more):
                for half in range(2):
                    dve.wait_ge(tokT_psum, e * 2 + half + 1)
                    nc.vector.tensor_copy(buf["tokT"][:, 512 * half:512 * half + 512],
                                          psum[half][:, :]).then_inc(tokT_ready, 1)
                if more:
                    build_list(e + 1)
                for half in range(2):
                    dve.wait_ge(y_psum, e * 2 + half + 1)
                    y4 = psum[4 + half][:, :].rearrange("p (j d) -> p j d", d=D)
                    bias = weights["b2"][:, bass.ds(e * D, D)].unsqueeze(1).broadcast_to([P, 4, D])
                    nc.vector.tensor_tensor(buf["yb"][:, 4 * half:4 * half + 4, :], y4, bias,
                                            ALU.add).then_inc(y_biased, 1)
                    dve.wait_ge(y_biased, e * 2 + half + 1)
                    if half == 0:
                        wait_unless_first(dve, scattered, e * (16 * SL))
                    gate = buf["tok"][u][:, 4 * half:4 * half + 4, bass.ds(e + D, 1)].broadcast_to([P, 4, D])
                    nc.vector.scalar_tensor_tensor(buf["y"][:, 4 * half:4 * half + 4, :],
                                                   buf["yb"][:, 4 * half:4 * half + 4, :], 0.5, gate,
                                                   ALU.mult, ALU.mult).then_inc(y_ready, 1)

            build_list(0)
            expert(0, 0, True)
            expert(1, 1, True)
            with dve.Fori(1, E // 2 - 1) as g:
                expert(g * 2, 0, True)
                expert(g * 2 + 1, 1, True)
            expert(E - 2, 0, True)
            expert(E - 1, 1, False)

        @block.scalar
        def _(act):
            act.wait_ge(var_ready, 1)
            nc.scalar.activation(buf["std"][:, :], tmp32[:, 1, :], ACT.Sqrt).then_inc(std_ready, 1)
            for i in range(C // QT):
                act.wait_ge(xnT_psum, i + 1)
                nc.scalar.copy(xnT[:, 512 * (i % 2):512 * (i % 2) + 512], psum[i % 2][:, :]).then_inc(xnT_ready, 1)
            act.wait_ge(shifted_ready, 1)
            nc.scalar.activation(buf["work"][:, 1, :], buf["work"][:, 0, :], ACT.Exp).then_inc(exp_ready, 1)
            with act.Fori(0, E) as e:
                for k in range(HC):
                    for half in range(2):
                        act.wait_ge(hidden_psum, e * (2 * HC) + (2 * k + half + 1))
                        act.sem_inc(act_turn, 1)
                        nc.scalar.activation(buf["hidden"][:, k, 512 * half:512 * half + 512], psum[2 + half][:, :],
                                             ACT.Gelu, bias=weights["b1"][:, bass.ds(e * HC + k, 1)]
                                             ).then_inc(hidden_ready, 1)

        @block.tensor
        def _(pe):
            def route(i):
                pe.wait_ge(xnT_ready, i + 1)
                for q in range(QT):
                    c = QT * i + q
                    mm = nc.tensor.matmul(logits[:, E * c:E * c + E],
                                          xnT[:, 512 * (i % 2) + P * q:512 * (i % 2) + P * q + P],
                                          weights["wr"][:, :], start=True, stop=True)
                return mm

            for i in range(C // QT):
                if i >= 2:
                    pe.wait_ge(xnT_ready, i - 1)
                for q in range(QT):
                    c = QT * i + q
                    pe.wait_ge(xn_ready, c + 1)
                    mm = nc.tensor.transpose(psum[i % 2][:, P * q:P * q + P], buf["rows"][:, c, 0:D], ident[:, :])
                mm.then_inc(xnT_psum, 1)
                if i >= 1:
                    route(i - 1)
            route(C // QT - 1).then_inc(logits_ready, 1)
            pe.wait_ge(scores_ready, 1)
            for half in range(2):
                mm = nc.tensor.transpose(scoresT[:, P * half:P * half + P], scores[:, P * half:P * half + P],
                                         ident[:, :])
            mm.then_inc(scoresT_psum, 1)
            with pe.Fori(0, BITS) as i:
                pe.wait_ge(counts_ready, i + 1)
                nc.tensor.matmul(total, consts["same_expert"][:, :], buf["count"][:, :], start=True,
                                 stop=True).then_inc(total_ready, 1)
            pe.wait_ge(thr_ready, 1)
            nc.tensor.transpose(thr_psum, buf["thr_wide"][:, :], ident[:, :]).then_inc(thrT_ready, 1)
            pe.wait_ge(gt_ready, 1)
            nc.tensor.matmul(rank_psum, consts["ones"][:, :], buf["gt"][:, :], start=True,
                             stop=True).then_inc(gt_count, 1)
            pe.wait_ge(eq_ready, 2)
            nc.tensor.matmul(rank_psum, consts["tri"][:, :], buf["eq"][:, :], start=True, stop=False)
            nc.tensor.matmul(rank_psum, consts["ones"][:, :], buf["before"][:, :], start=False,
                             stop=True).then_inc(eq_rank, 1)
            pe.wait_ge(sel_ready, 1)
            nc.tensor.matmul(rank_psum, consts["tri"][:, :], buf["sel"][:, :], start=True, stop=False)
            nc.tensor.matmul(rank_psum, consts["ones"][:, :], buf["before"][:, :], start=False,
                             stop=True).then_inc(sel_rank, 1)

            def token_list(e):
                pe.wait_ge(onehot_ready, e * 3 + 3)
                for c in range(C):
                    mm = nc.tensor.matmul(list_psum, buf["hi_hot"][:, c, :], buf["lo_val"][:, c, :],
                                          start=(c == 0), stop=(c == C - 1))
                mm.then_inc(list_ready, 1)

            def expert(e, u, more):
                pe.wait_ge(gathered[u], (e - u) * (8 * SL) + 16 * SL)
                for half in range(2):
                    for q in range(4):
                        mm = nc.tensor.transpose(psum[half][:, P * q:P * q + P], buf["tok"][u][:, 4 * half + q, 0:D],
                                                 ident[:, :])
                    mm.then_inc(tokT_psum, 1)
                pe.wait_ge(tokT_ready, e * 2 + 2)
                pe.wait_ge(w1_in[u], (e - u) * 8 + 16)
                for k in range(HC):
                    for half in range(2):
                        if k >= 1:
                            pe.wait_ge(hidden_ready, e * (2 * HC) + (2 * k + half - 1))
                        nc.tensor.matmul(psum[2 + half][:, :], weights["w1"][u][:, P * k:P * k + P],
                                         buf["tokT"][:, 512 * half:512 * half + 512], start=True,
                                         stop=True).then_inc(hidden_psum, 1)
                    if k == 1 and more:
                        token_list(e + 1)
                pe.wait_ge(hidden_ready, e * (2 * HC) + 2 * HC)
                wait_unless_first(pe, y_biased, e * 2)
                for half in range(2):
                    for q in range(4):
                        for k in range(HC):
                            mm = nc.tensor.matmul(psum[4 + half][:, P * q:P * q + P],
                                                  buf["hidden"][:, k, 512 * half + P * q:512 * half + P * q + P],
                                                  weights["w2"][:, bass.ds(e * HID + k * P, P)],
                                                  start=(k == 0), stop=(k == HC - 1))
                    mm.then_inc(y_psum, 1)

            token_list(0)
            expert(0, 0, True)
            expert(1, 1, True)
            with pe.Fori(1, E // 2 - 1) as g:
                expert(g * 2, 0, True)
                expert(g * 2 + 1, 1, True)
            expert(E - 2, 0, True)
            expert(E - 1, 1, False)

        @block.gpsimd
        def _(pool):
            pool.wait_ge(table_out, 16)
            if copy_residual:
                pool.wait_ge(residual_out, 16)

            def gather(e, u):
                pool.wait_ge(idx_ready, e + 1)
                nc.gpsimd.tensor_copy(buf["gather_idx"][u][:, :], buf["idx"][:, bass.ds(e * SL, SL)]
                                      ).then_inc(idx_copied, 1)
                pool.wait_ge(idx_copied, e * 2 + 1)
                pool.sem_inc(pool_turn, 1)
                for j in range(SL):
                    nc.gpsimd.indirect_dma_start(
                        out=buf["tok"][u][:, j, :], out_offset=None, in_=table,
                        in_offset=bass.IndirectOffsetOnAxis(ap=buf["gather_idx"][u][:, j:j + 1], axis=0)
                    ).then_inc(gathered[u], 16)

            def expert(e, u, more):
                nc.gpsimd.tensor_copy(buf["scatter_idx"][u][:, :], buf["idx"][:, bass.ds(e * SL, SL)]
                                      ).then_inc(idx_copied, 1)
                if more:
                    wait_unless_first(pool, y_ready, e * 2)
                    gather(e + 1, 1 - u)
                pool.wait_ge(idx_copied, e * 2 + 2)
                wait_unless_first(pool, scattered, e * (16 * SL))
                pool.wait_ge(y_ready, e * 2 + 2)
                pool.sem_inc(pool_turn, 1)
                for j in range(SL):
                    nc.gpsimd.indirect_dma_start(
                        out=x_acc, out_offset=bass.IndirectOffsetOnAxis(ap=buf["scatter_idx"][u][:, j:j + 1], axis=0),
                        in_=buf["y"][:, j, :], in_offset=None, compute_op=ALU.add).then_inc(scattered, 16)

            gather(0, 0)
            expert(0, 0, True)
            expert(1, 1, True)
            with pool.Fori(1, E // 2 - 1) as g:
                expert(g * 2, 0, True)
                expert(g * 2 + 1, 1, True)
            expert(E - 2, 0, True)
            expert(E - 1, 1, False)
            pool.wait_ge(scattered, E * 16 * SL)


Q_PART = [0, 0, 1, 1, 0, 2, 1, 2]
K_PART = [0, 1, 0, 1, 2, 0, 2, 1]
SLOTS = len(Q_PART)
HALVES = 2
ROUNDS = B // HALVES
RT = HALVES * N
TILES = RT // P
KW = N + ENC
NCH = H * FD // P
STEPS = HALVES * PAIRS
LN_STEP, SQRT_STEP, TURN_STEP, QK_STEP, OUT_STEP = 0, 1, 3, 4, 10


def attention_weights(nc, psum, ident, wT, w_in):
    with ExitStack() as ctx:
        def sem(n):
            return ctx.enter_context(nc.semaphore(f"attn_weights_{n}"))

        def sb(n, shape):
            return ctx.enter_context(nc.sbuf_tensor(f"raw_{n}", shape, F32))

        rows = {n: sb(n, [P, w_in[n].shape[0] // P, D]) for n in ("wq", "wk", "wke", "wv", "wve")}
        rows["wout"] = sb("wout", [D, H * HD])
        loaded = sem("loaded")
        turned = sem("turned")
        copied = sem("copied")
        block = ctx.enter_context(nc.Block())
        blocks = []
        for n in ("wq", "wk", "wke", "wv", "wve"):
            blocks += [(rows[n][:, i, :], wT[n], P * i) for i in range(w_in[n].shape[0] // P)]
        blocks += [(rows["wout"][:, P * i:P * i + P], wT["wout"], P * i) for i in range(PAIRS)]

        @block.sync
        def _(sp):
            for n in ("wq", "wk", "wke", "wv", "wve"):
                sp.dma_start(rows[n][:], w_in[n].rearrange("(c p) d -> p c d", p=P)).then_inc(loaded, 16)
            sp.dma_start(rows["wout"][:, :], w_in["wout"]).then_inc(loaded, 16)

        @block.tensor
        def _(pe):
            pe.wait_ge(loaded, 6 * 16)
            for i, (source, _, _) in enumerate(blocks):
                if i >= 8 and i % 2 == 0:
                    pe.wait_ge(copied, i // 2 - 3)
                mm = nc.tensor.transpose(psum[i // 2 % 4][:, P * (i % 2):P * (i % 2) + P], source, ident[:, :])
                if i % 2:
                    mm.then_inc(turned, 1)

        @block.vector
        def _(dve):
            for i in range(0, len(blocks), 2):
                dve.wait_ge(turned, i // 2 + 1)
                _, destination, column = blocks[i]
                nc.vector.tensor_copy(destination[:, column:column + 2 * P],
                                      psum[i // 2 % 4][:, 0:2 * P]).then_inc(copied, 1)


def attention(nc, psum, consts, wT, x, scratch):
    with ExitStack() as ctx:
        def sem(n):
            return ctx.enter_context(nc.semaphore(f"attn_{n}"))

        def sb(n, shape, dt=F32):
            return ctx.enter_context(nc.sbuf_tensor(f"attn_{n}", shape, dt))

        x_ln, xn, x_res = sb("x_ln", [P, TILES, D]), sb("xn", [P, TILES, D]), sb("x_res", [P, TILES, D])
        x_new = sb("x_new", [P, TILES, D])
        xnT = sb("xnT", [D, RT])
        stats, mv = sb("stats", [P, TILES, 6]), sb("mv", [P, TILES, 2])
        var, std = sb("var", [P, TILES]), sb("std", [P, TILES])
        ln_tmp, rstd = sb("ln_tmp", [P, 3, TILES]), sb("rstd", [P, TILES])
        q_parts = sb("q_parts", [P, 3, NCH, RT], BF16)
        k_parts = sb("k_parts", [P, 3, NCH, HALVES, KW], BF16)
        rest = [sb(f"rest{u}", [P, RT]) for u in range(2)]
        q_stack = [sb(f"q_stack{a}", [P, H, N], BF16) for a in range(HALVES)]
        k_stack = [sb(f"k_stack{a}", [P, H, KW], BF16) for a in range(HALVES)]
        v = sb("v", [P, TILES, H * HD])
        v_enc = sb("v_enc", [P, HALVES, PAIRS, P])
        att = [sb(f"att{u}", [P, 4 * N]) for u in range(2)]
        den, z = ([sb(f"{n}{u}", [P, N]) for u in range(2)] for n in ("den", "z"))
        yT = [sb(f"yT{a}", [P, PAIRS, N]) for a in range(HALVES)]
        q_dram, k_dram = scratch

        x_ln_in = sem("x_ln_in")
        x_res_in = sem("x_res_in")
        var_ready = sem("var_ready")
        std_ready = sem("std_ready")
        xn_ready = sem("xn_ready")
        turned = sem("turned")
        xnT_ready = sem("xnT_ready")
        qk_psum = sem("qk_psum")
        part1_ready = sem("part1_ready")
        parts_ready = sem("parts_ready")
        parts_out = sem("parts_out")
        stack_in = [sem(f"stack_in{a}") for a in range(HALVES)]
        v_psum = sem("v_psum")
        v_ready = sem("v_ready")
        v_enc_ready = sem("v_enc_ready")
        scores_psum = sem("scores_psum")
        squares_ready = sem("squares_ready")
        att_ready = sem("att_ready")
        y_psum = sem("y_psum")
        den_ready = sem("den_ready")
        z_ready = sem("z_ready")
        yT_ready = sem("yT_ready")
        out_psum = sem("out_psum")
        x_new_ready = sem("x_new_ready")
        x_out = sem("x_out")
        dve_step = sem("dve_step")
        dve_turn = sem("dve_turn")
        sp_turn = sem("sp_turn")
        split_step = sem("split_step")
        v_enc_clear = sem("v_enc_clear")
        block = ctx.enter_context(nc.Block())

        S, SE, Y, PR, TR = psum[0:2], psum[2], psum[3:5], psum[5:7], psum[7]
        NQK = 2 * NCH + 1
        LN_STEPS = 2 * TILES + 5
        VN = TILES * 2

        def x_round(i):
            return x[bass.ds(i * RT, RT), :].rearrange("(t p) d -> p t d", p=P)

        def head_blocks(u):
            return att[u][:, 0:6 * P].rearrange("p (a w) -> p a w", a=2)

        def qk_tile(j):
            bank = PR[j % 2]
            if j < NCH:
                return (lambda s: q_parts[:, s, j, :]), bank[:, :]
            if j < 2 * NCH:
                return ((lambda s: k_parts[:, s, j - NCH, :, 0:N]),
                        bank[:, :].rearrange("p (a n) -> p a n", a=HALVES))
            return ((lambda s: k_parts[:, s, :, :, N:KW].rearrange("p c a n -> p (c a) n")),
                    bank[:, 0:NCH * HALVES * ENC].rearrange("p (g n) -> p g n", n=ENC))

        @block.sync
        def _(sp):
            def load_ln(i):
                sp.dma_start(x_ln[:], x_round(i)).then_inc(x_ln_in, 16)

            def store_parts(i):
                sp.wait_ge(part1_ready, i * NQK + NQK)
                sp.wait_ge(parts_ready, i * NQK + NQK)
                sp.dma_start(q_dram.rearrange("s c p t -> p s c t"), q_parts[:]).then_inc(parts_out, 16)
                sp.dma_start(k_dram.rearrange("s c p t -> p s c t"),
                             k_parts[:].rearrange("p s c a w -> p s c (a w)")).then_inc(parts_out, 16)
                sp.wait_ge(parts_out, i * 32 + 32)

            def load_stack(a):
                for s in range(SLOTS):
                    sp.dma_start(q_stack[a][FD * s:FD * s + FD, :, :],
                                 q_dram[Q_PART[s]].rearrange("c (h f) t -> f (c h) t", f=FD)[:, :, N * a:N * a + N]
                                 ).then_inc(stack_in[a], 16)
                    sp.dma_start(k_stack[a][FD * s:FD * s + FD, :, :],
                                 k_dram[K_PART[s]].rearrange("c (h f) t -> f (c h) t", f=FD)[:, :, KW * a:KW * a + KW]
                                 ).then_inc(stack_in[a], 16)

            def round_(i, more):
                sp.dma_start(x_res[:], x_round(i)).then_inc(x_res_in, 16)
                if more:
                    sp.wait_ge(xn_ready, i * TILES + TILES)
                    sp.sem_inc(sp_turn, 1)
                    load_ln(i + 1)
                    sp.wait_ge(stack_in[1], i * (32 * SLOTS) + 32 * SLOTS)
                    store_parts(i + 1)
                    sp.wait_ge(scores_psum, i * (2 * STEPS) + STEPS)
                    load_stack(0)
                sp.wait_ge(x_new_ready, i * 2 + 1)
                sp.sem_inc(sp_turn, 1)
                sp.dma_start(x_round(i)[:, 0:2, :], x_new[:, 0:2, :]).then_inc(x_out, 16)
                if more:
                    sp.wait_ge(scores_psum, i * (2 * STEPS) + 2 * STEPS)
                    load_stack(1)
                sp.wait_ge(x_new_ready, i * 2 + 2)
                sp.sem_inc(sp_turn, 1)
                sp.dma_start(x_round(i)[:, 2:4, :], x_new[:, 2:4, :]).then_inc(x_out, 16)
                sp.wait_ge(x_out, i * 32 + 32)
                sp.sem_inc(sp_turn, 1)

            load_ln(0)
            store_parts(0)
            load_stack(0)
            load_stack(1)
            with sp.Fori(0, ROUNDS - 1) as i:
                round_(i, True)
            round_(ROUNDS - 1, False)

        @block.vector
        def _(dve):
            def layernorm_a(i):
                own = Steps(dve, dve_step, i * LN_STEPS)
                dve.wait_ge(x_ln_in, i * 16 + 16)
                for t in range(TILES):
                    own.done(nc.vector.bn_stats(stats[:, t, :], x_ln[:, t, :]))
                own.after()
                dve.sem_inc(dve_turn, 1)
                for t in range(TILES):
                    own.done(nc.vector.bn_aggr(mv[:, t, :], stats[:, t, :]))
                own.after()
                nc.vector.tensor_scalar(var[:, :], mv[:, :, 1], LN_EPS, None, ALU.add).then_inc(var_ready, 1)

            def layernorm_b(i):
                own = Steps(dve, dve_step, i * LN_STEPS + 2 * TILES)
                dve.wait_ge(std_ready, i + 1)
                own.done(nc.vector.reciprocal(ln_tmp[:, 0, :], std[:, :]))
                own.after()
                own.done(nc.vector.tensor_tensor(ln_tmp[:, 1, :], var[:, :], ln_tmp[:, 0, :], ALU.mult))
                own.after()
                own.done(nc.vector.tensor_tensor(ln_tmp[:, 2, :], ln_tmp[:, 1, :], std[:, :], ALU.add))
                own.after()
                own.done(nc.vector.tensor_scalar(ln_tmp[:, 0, :], ln_tmp[:, 2, :], 0.5, None, ALU.mult))
                own.after()
                own.done(nc.vector.reciprocal(rstd[:, :], ln_tmp[:, 0, :]))
                own.after()
                for t in range(TILES):
                    nc.vector.tensor_scalar(xn[:, t, :], x_ln[:, t, :], mv[:, t, 0:1], rstd[:, t:t + 1],
                                            ALU.subtract, ALU.mult).then_inc(xn_ready, 1)

            def split(i, j):
                own = Steps(dve, split_step, i * (2 * NQK) + 2 * j)
                tile, bank = qk_tile(j)
                dve.wait_ge(part1_ready, i * NQK + j + 1)
                r = rest[j % 2][:, 0:tile(0).shape[1] * (tile(0).shape[2] if len(tile(0).shape) == 3 else 1)]
                if len(tile(0).shape) == 3:
                    r = r.rearrange("p (a w) -> p a w", a=tile(0).shape[1])
                own.done(nc.vector.tensor_tensor(r, bank, tile(0), ALU.subtract))
                own.after()
                own.done(nc.vector.tensor_copy(tile(1), r))
                own.after()
                nc.vector.tensor_tensor(tile(2), r, tile(1), ALU.subtract).then_inc(parts_ready, 1)

            def mask(i, s):
                u, n = s % 2, i * (3 * STEPS) + 3 * s
                blocks = head_blocks(u)
                dve.wait_ge(squares_ready, n + 2)
                nc.vector.scalar_tensor_tensor(blocks[:, :, 0:2 * P], blocks[:, :, 0:2 * P], HALF,
                                               consts["causal"][:, :].unsqueeze(1).broadcast_to([P, 2, 2 * P]),
                                               ALU.add, ALU.mult).then_inc(att_ready, 1)
                nc.vector.tensor_scalar(blocks[:, :, 2 * P:3 * P], blocks[:, :, 2 * P:3 * P], HALF, None,
                                        ALU.add).then_inc(att_ready, 1)
                dve.wait_ge(squares_ready, n + 3)
                nc.vector.tensor_scalar(att[u][:, 6 * P:8 * P], att[u][:, 6 * P:8 * P], HALF, None,
                                        ALU.add).then_inc(att_ready, 1)

            def normalise(i, s):
                u, a, p = s % 2, s // PAIRS, s % PAIRS
                dve.wait_ge(den_ready, i * STEPS + s + 1)
                nc.vector.reciprocal(z[u][:, :], den[u][:, :]).then_inc(z_ready, 1)
                dve.wait_ge(z_ready, i * STEPS + s + 1)
                nc.vector.tensor_tensor(yT[a][:, p, :], Y[u][:, 0:N], z[u][:, :], ALU.mult).then_inc(yT_ready, 1)

            def values_enc(i):
                for a in range(HALVES):
                    dve.wait_ge(v_psum, i * (VN + HALVES) + VN + a + 1)
                    for w in range(2):
                        rows = slice(ENC * w, ENC * w + ENC)
                        nc.vector.tensor_copy(v_enc[rows, a, :, HD * w:HD * w + HD],
                                              PR[a][rows, :].rearrange("p (g e) -> p g e", e=HD)
                                              ).then_inc(v_enc_ready, 1)

            def residual(i, a):
                dve.wait_ge(x_res_in, i * 16 + 16)
                dve.wait_ge(out_psum, i * 2 + a + 1)
                nc.vector.tensor_tensor(x_new[:, 2 * a:2 * a + 2, :], TR[:, 0:2 * D].rearrange("p (t d) -> p t d", d=D),
                                        x_res[:, 2 * a:2 * a + 2, :], ALU.add).then_inc(x_new_ready, 1)

            def round_(i, more):
                for s in range(STEPS):
                    mask(i, s)
                    if s >= 1:
                        normalise(i, s - 1)
                    if more and s == LN_STEP:
                        layernorm_a(i + 1)
                    if more and s == SQRT_STEP:
                        layernorm_b(i + 1)
                    if more and 0 <= s - QK_STEP < NQK:
                        split(i + 1, s - QK_STEP)
                    if s == OUT_STEP:
                        residual(i, 0)
                normalise(i, STEPS - 1)
                if more:
                    values_enc(i + 1)
                residual(i, 1)

            layernorm_a(0)
            layernorm_b(0)
            for j in range(NQK):
                split(0, j)
            dve.wait_ge(v_enc_clear, 1)
            values_enc(0)
            with dve.Fori(0, ROUNDS - 1) as i:
                round_(i, True)
            round_(ROUNDS - 1, False)

        @block.scalar
        def _(act):
            def square_root(i):
                act.wait_ge(var_ready, i + 1)
                nc.scalar.activation(std[:, :], var[:, :], ACT.Sqrt).then_inc(std_ready, 1)

            def turn(i):
                act.wait_ge(turned, i + 1)
                nc.scalar.copy(xnT[:, :], TR[:, :]).then_inc(xnT_ready, 1)

            def first_part(i, j):
                tile, bank = qk_tile(j)
                act.wait_ge(qk_psum, i * NQK + j + 1)
                nc.scalar.copy(tile(0), bank).then_inc(part1_ready, 1)

            def square(i, s):
                u, n = s % 2, i * (2 * STEPS) + 2 * s
                act.wait_ge(scores_psum, n + 1)
                for w in range(2):
                    nc.scalar.activation(att[u][:, 3 * P * w:3 * P * w + 3 * P], S[w][:, 0:3 * P], ACT.Square,
                                         bias=HEAD_SHIFT, scale=HEAD_SCALE).then_inc(squares_ready, 1)
                act.wait_ge(scores_psum, n + 2)
                nc.scalar.activation(att[u][:, 6 * P:8 * P], SE[:, 0:N], ACT.Square, bias=HEAD_SHIFT,
                                     scale=HEAD_SCALE).then_inc(squares_ready, 1)

            def denominator(i, s):
                u = s % 2
                act.wait_ge(y_psum, i * STEPS + s + 1)
                nc.scalar.activation(den[u][:, :], Y[u][:, N:2 * N], ACT.Identity,
                                     bias=Z_EPS).then_inc(den_ready, 1)

            def values(i):
                for m in range(VN):
                    act.wait_ge(v_psum, i * (VN + HALVES) + m + 1)
                    nc.scalar.copy(v[:, m // 2, 512 * (m % 2):512 * (m % 2) + 512], PR[m % 2][:, :]
                                   ).then_inc(v_ready, 1)

            def round_(i, more):
                for s in range(STEPS):
                    square(i, s)
                    if s >= 1:
                        denominator(i, s - 1)
                    if more and s == LN_STEP:
                        square_root(i + 1)
                    if more and s == TURN_STEP:
                        turn(i + 1)
                    if more and 0 <= s - QK_STEP < NQK:
                        if s == QK_STEP:
                            act.wait_ge(parts_out, i * 32 + 32)
                        first_part(i + 1, s - QK_STEP)
                denominator(i, STEPS - 1)
                if more:
                    values(i + 1)

            square_root(0)
            turn(0)
            for j in range(NQK):
                first_part(0, j)
            values(0)
            with act.Fori(0, ROUNDS - 1) as i:
                round_(i, True)
            round_(ROUNDS - 1, False)

        @block.tensor
        def _(pe):
            def turn(i):
                pe.wait_ge(xn_ready, i * TILES + TILES)
                for t in range(TILES):
                    mm = nc.tensor.transpose(TR[:, P * t:P * t + P], xn[:, t, :], consts["ident"][:, :])
                mm.then_inc(turned, 1)

            def project(i, j):
                if j >= 2:
                    pe.wait_ge(parts_ready, i * NQK + j - 1)
                bank = PR[j % 2]
                if j < 2 * NCH:
                    w, c = ("wq", "wk")[j // NCH], j % NCH
                    mm = nc.tensor.matmul(bank[:, :], wT[w][:, P * c:P * c + P], xnT[:, :], start=True, stop=True)
                else:
                    enc = xnT[:, :].rearrange("d (a n) -> d a n", a=HALVES)[:, :, 0:ENC]
                    for c in range(NCH):
                        mm = nc.tensor.matmul(bank[:, P * c:P * c + P], wT["wke"][:, P * c:P * c + P], enc,
                                              start=True, stop=True)
                mm.then_inc(qk_psum, 1)

            def values(i):
                pe.wait_ge(parts_ready, i * NQK + NQK)
                for m in range(VN + HALVES):
                    bank = PR[m % 2]
                    if m >= 2:
                        pe.wait_ge(v_ready, i * VN + m - 1)
                    if m < VN:
                        t, w = m // 2, m % 2
                        mm = nc.tensor.matmul(bank[:, :], xnT[:, P * t:P * t + P], wT["wv"][:, 512 * w:512 * w + 512],
                                              start=True, stop=True)
                    else:
                        a = m - VN
                        heads = wT["wve"][:, :].rearrange("d (g w e) -> d w g e", w=2, e=HD)
                        for w in range(2):
                            mm = nc.tensor.matmul(bank[ENC * w:ENC * w + ENC, :], xnT[:, N * a:N * a + ENC],
                                                  heads[:, w], start=True, stop=True)
                    mm.then_inc(v_psum, 1)

            def scores(i, s):
                a, p = s // PAIRS, s % PAIRS
                if p == 0:
                    pe.wait_ge(stack_in[a], i * (32 * SLOTS) + 32 * SLOTS)
                if s >= 1:
                    pe.wait_ge(squares_ready, i * (3 * STEPS) + 3 * s)
                for w in range(2):
                    h = 2 * p + w
                    nc.tensor.matmul(S[w][:, 0:P], k_stack[a][:, h, P:2 * P], q_stack[a][:, h, P:2 * P],
                                     start=True, stop=True)
                    mm = nc.tensor.matmul(S[w][:, P:3 * P], k_stack[a][:, h, 0:P], q_stack[a][:, h, :],
                                          start=True, stop=True)
                mm.then_inc(scores_psum, 1)
                for w in range(2):
                    h = 2 * p + w
                    mm = nc.tensor.matmul(SE[ENC * w:ENC * w + ENC, 0:N], k_stack[a][:, h, N:KW],
                                          q_stack[a][:, h, :], start=True, stop=True)
                mm.then_inc(scores_psum, 1)

            def weighted(i, s):
                u, a, p = s % 2, s // PAIRS, s % PAIRS
                blocks = head_blocks(u)
                pe.wait_ge(att_ready, i * (3 * STEPS) + 3 * s + 3)
                if s == 0:
                    pe.wait_ge(v_ready, i * VN + VN)
                    pe.wait_ge(v_enc_ready, i * (2 * HALVES) + 2 * HALVES)
                if s >= 2:
                    pe.wait_ge(yT_ready, i * STEPS + s - 1)
                for den_ in range(2):
                    base = N * den_
                    for late in range(2):
                        for w in range(2):
                            h = 2 * p + w
                            left = consts["ones_f"][:, 0:HD] if den_ else v[:, 2 * a + late, HD * h:HD * h + HD]
                            right = blocks[:, w, 0:P] if late else blocks[:, w, P:3 * P]
                            nc.tensor.matmul(Y[u][HD * w:HD * w + HD, base + P * late:base + N], left, right,
                                             start=(late == 0), stop=False, skip_group_check=True)
                    left = consts["pair_ones"][:, :] if den_ else v_enc[:, a, p, :]
                    mm = nc.tensor.matmul(Y[u][:, base:base + N], left, att[u][:, 6 * P:8 * P], start=False,
                                          stop=True, skip_group_check=True)
                mm.then_inc(y_psum, 1)

            def project_out(i, a):
                pe.wait_ge(yT_ready, i * STEPS + PAIRS * (a + 1))
                if a == 1:
                    pe.wait_ge(x_new_ready, i * 2 + 1)
                for t in range(2):
                    for p in range(PAIRS):
                        mm = nc.tensor.matmul(TR[:, D * t:D * t + D], yT[a][:, p, P * t:P * t + P],
                                              wT["wout"][:, D * p:D * p + D], start=(p == 0), stop=(p == PAIRS - 1))
                mm.then_inc(out_psum, 1)

            def round_(i, more):
                for s in range(STEPS):
                    scores(i, s)
                    if s >= 1:
                        weighted(i, s - 1)
                    if more and s == TURN_STEP:
                        turn(i + 1)
                    if more and 0 <= s - QK_STEP < NQK:
                        if s == QK_STEP:
                            pe.wait_ge(xnT_ready, i + 2)
                        project(i + 1, s - QK_STEP)
                    if s == OUT_STEP:
                        project_out(i, 0)
                weighted(i, STEPS - 1)
                if more:
                    values(i + 1)
                project_out(i, 1)

            turn(0)
            pe.wait_ge(xnT_ready, 1)
            for j in range(NQK):
                project(0, j)
            values(0)
            with pe.Fori(0, ROUNDS - 1) as i:
                round_(i, True)
            round_(ROUNDS - 1, False)

        @block.gpsimd
        def _(pool):
            nc.gpsimd.memset(v_enc[:], 0.0).then_inc(v_enc_clear, 1)


def make_constants(nc, consts, raw, psum, weights, stage, inputs):
    with ExitStack() as ctx:
        def sem(n):
            return ctx.enter_context(nc.semaphore(f"setup_{n}"))
        pool_step = sem("pool_step")
        iota_ready = sem("iota_ready")
        masks_ready = sem("masks_ready")
        converted = sem("converted")
        loaded = sem("loaded")
        b1_in = sem("b1_in")
        b1T_psum = sem("b1T_psum")
        block = ctx.enter_context(nc.Block())

        @block.sync
        def _(sp):
            sp.dma_start(stage["b1"][:, :], inputs["b1"].rearrange("e (k p) -> (e k) p", p=P)).then_inc(b1_in, 16)
            sp.dma_start(weights["wr"][:, :], inputs["wr"]).then_inc(loaded, 16)
            sp.dma_start(weights["w2"][:, :].rearrange("p (e k d) -> p e k d", e=E, k=HC),
                         inputs["w2"].rearrange("e (k p) d -> p e k d", p=P)).then_inc(loaded, 16)
            sp.dma_start(weights["b2"][:, :], inputs["b2"].rearrange("e d -> (e d)").unsqueeze(0)
                         .broadcast_to([P, E * D])).then_inc(loaded, 16)
            sp.wait_ge(loaded, 48)

        @block.gpsimd
        def _(pool):
            own = Steps(pool, pool_step)
            own.done(nc.gpsimd.memset(raw["ones"][:, :], 1.0))
            own.done(nc.gpsimd.iota(raw["column"][:, :], pattern=[[1, P]], base=0, channel_multiplier=0))
            own.done(nc.gpsimd.iota(raw["row"][:, :], pattern=[[0, 1]], base=0, channel_multiplier=1))
            own.done(nc.gpsimd.iota(raw["shift"][:, :], pattern=[[-1, BITS]], base=BITS - 1, channel_multiplier=0))
            own.done(nc.gpsimd.iota(raw["distance"][:, :], pattern=[[1, P]], base=P, channel_multiplier=-1))
            own.done(nc.gpsimd.memset(raw["one_i"][:, :], 1))
            own.after()
            nc.gpsimd.affine_select(out=consts["tri_f"][:, :], in_=raw["ones"][:, :], compare_op=ALU.is_ge, fill=0.0,
                                    base=0, pattern=[[1, P]], channel_multiplier=-1).then_inc(masks_ready, 1)
            nc.gpsimd.affine_select(out=consts["ident"][:, :], in_=raw["ones"][:, :], compare_op=ALU.is_equal,
                                    fill=0.0, base=0, pattern=[[1, P]], channel_multiplier=-1
                                    ).then_inc(masks_ready, 1)

        @block.vector
        def _(dve):
            own = Steps(dve, converted)
            dve.wait_ge(pool_step, 6)
            own.done(nc.vector.tensor_copy(consts["iota_f"][:, :], raw["column"][:, :]))
            own.done(nc.vector.tensor_copy(consts["part"][:, :], raw["row"][:, :]))
            own.done(nc.vector.tensor_copy(consts["ones"][:, :], raw["ones"][:, :]))
            own.done(nc.vector.tensor_tensor(consts["bits_i"][:, :], raw["one_i"][:, :], raw["shift"][:, :],
                                             ALU.logical_shift_left))
            own.done(nc.vector.memset(consts["restart"][:, :], 1.0))
            own.done(nc.vector.tensor_scalar(raw["phase"][:, :], raw["distance"][:, :], E - 1, None, ALU.bitwise_and))
            own.after()
            own.done(nc.vector.tensor_copy(consts["bits_f"][:, :], consts["bits_i"][:, :]))
            own.done(nc.vector.memset(consts["restart"][:, :].rearrange("p (e c) -> p e c", e=E)[:, :, 0:1], 0.0))
            own.done(nc.vector.tensor_scalar(consts["same_expert"][:, :], raw["phase"][:, :], 0.0, None,
                                             ALU.is_equal))
            own.done(nc.vector.tensor_copy(consts["ones_f"][:, :], raw["ones"][:, 0:HD]))
            own.done(nc.vector.memset(consts["pair_ones"][:, :], 0.0))
            own.after()
            for w in range(2):
                half = slice(HD * w, HD * w + HD)
                own.done(nc.vector.memset(consts["pair_ones"][half, half], 1.0))
            dve.wait_ge(masks_ready, 2)
            for w in range(2):
                own.done(nc.vector.tensor_copy(consts["causal"][:, P * w:P * w + P], consts["tri_f"][:, :]))
            own.done(nc.vector.tensor_copy(consts["tri"][:, :], consts["tri_f"][:, :]))
            dve.wait_ge(b1T_psum, 1)
            own.done(nc.vector.tensor_copy(weights["b1"][:, :], psum[0][:, 0:E * HC]))

        @block.tensor
        def _(pe):
            pe.wait_ge(b1_in, 16)
            pe.wait_ge(masks_ready, 2)
            nc.tensor.transpose(psum[0][:, 0:E * HC], stage["b1"][:, :], consts["ident"][0:E * HC, 0:E * HC]
                                ).then_inc(b1T_psum, 1)


def build(nc, x, wq, wk, wv, wke, wve, wout, wr, w1, b1, w2, b2, out):
    with ExitStack() as ctx:
        def sb(name, shape, dt=F32):
            return ctx.enter_context(nc.sbuf_tensor(name, shape, dt))

        psum = [ctx.enter_context(nc.psum_tensor(f"bank{i}", [P, 512], F32)) for i in range(8)]
        consts = {
            "tri_f": sb("tri_f", [P, P]), "ident": sb("ident", [P, P]), "iota_f": sb("iota_f", [P, P], BF16),
            "part": sb("part", [P, 1]), "ones": sb("ones", [P, P], BF16), "bits_i": sb("bits_i", [P, BITS], I32),
            "bits_f": sb("bits_f", [P, BITS]), "restart": sb("restart", [P, C * E]),
            "same_expert": sb("same_expert", [P, P]), "tri": sb("tri", [P, P], BF16),
            "causal": sb("causal", [P, 2 * P]), "ones_f": sb("ones_f", [P, HD]), "pair_ones": sb("pair_ones", [P, P])}
        weights = {"wr": sb("wr", [D, E]), "w1": [sb(f"w1_{u}", [D, HID]) for u in range(2)], "w1_dram": w1,
                   "w2": sb("w2", [P, E * HC * D]), "b2": sb("b2", [P, E * D]), "b1": sb("b1", [P, E * HC])}
        table = nc.dram_tensor("dispatch_table", [T, ROW], F32, kind="Internal").ap()
        q_dram = nc.dram_tensor("q_parts_dram", [3, NCH, P, RT], BF16, kind="Internal").ap()
        k_dram = nc.dram_tensor("k_parts_dram", [3, NCH, P, HALVES * KW], BF16, kind="Internal").ap()
        wT = {"wq": sb("wqT", [D, H * FD]), "wk": sb("wkT", [D, H * FD]), "wke": sb("wkeT", [D, H * FD]),
              "wv": sb("wvT", [D, H * HD]), "wve": sb("wveT", [D, H * HD]), "wout": sb("woutT", [P, PAIRS * D])}
        with ExitStack() as setup:
            def raw_sb(name, shape, dt=F32):
                return setup.enter_context(nc.sbuf_tensor(name, shape, dt))

            raw = {
                "ones": raw_sb("raw_ones", [P, P]), "column": raw_sb("raw_column", [P, P], I32),
                "row": raw_sb("raw_row", [P, 1], I32), "shift": raw_sb("raw_shift", [P, BITS], I32),
                "distance": raw_sb("raw_distance", [P, P], I32), "one_i": raw_sb("raw_one_i", [P, BITS], I32),
                "phase": raw_sb("raw_phase", [P, P], I32)}
            make_constants(nc, consts, raw, psum, weights, {"b1": raw_sb("b1_rows", [E * HC, P])},
                           {"wr": wr, "w1": w1, "b1": b1, "w2": w2, "b2": b2})
        attention_weights(nc, psum, consts["ident"], wT,
                          {"wq": wq, "wk": wk, "wke": wke, "wv": wv, "wve": wve, "wout": wout})
        x_flat = x.rearrange("b n d -> (b n) d")
        out_flat = out.rearrange("b n d -> (b n) d")
        ffn_stage(nc, "ffn1", consts, weights, psum, x_flat, out_flat, True, table)
        attention(nc, psum, consts, wT, out_flat, (q_dram, k_dram))
        ffn_stage(nc, "ffn2", consts, weights, psum, out_flat, out_flat, False, table)

_INS = ['L0_attn_x', 'L0_attn_Wq', 'L0_attn_Wk', 'L0_attn_Wv', 'L0_attn_Wk_enc', 'L0_attn_Wv_enc', 'L0_attn_Wout',
        'L0_ffn_Wr', 'L0_ffn_W1', 'L0_ffn_b1', 'L0_ffn_W2', 'L0_ffn_b2']
_OUTS = [((16, 256, 128), 'float32')]


def kernel(**inputs):
    import numpy as _np
    import concourse.bacc as _bacc
    from concourse import mybir as _mybir
    from concourse.bass_utils import run_bass_kernel_spmd as _run

    nc = _bacc.Bacc("TRN2", target_bir_lowering=False, num_devices=1)
    arrays, args = {}, []
    for name in _INS:
        a = _np.ascontiguousarray(inputs[name])
        arrays[f"in_{name}_dram"] = a
        args.append(nc.dram_tensor(f"in_{name}_dram", a.shape, _mybir.dt.from_np(a.dtype), kind="ExternalInput").ap())
    for i, (shape, dtype) in enumerate(_OUTS):
        dt = _mybir.dt.from_np(_np.dtype(dtype))
        args.append(nc.dram_tensor(f"out_{i}_dram", shape, dt, kind="ExternalOutput").ap())
    build(nc, *args)
    r = _run(nc, [arrays], core_ids=[0])
    got = tuple(r.results[0][f"out_{i}_dram"] for i in range(len(_OUTS)))
    return got[0]
```

```python
from contextlib import ExitStack

import concourse.bass as bass
from concourse import mybir

F32 = mybir.dt.float32
BF16 = mybir.dt.bfloat16
I32 = mybir.dt.int32
ALU = mybir.AluOpType
ACT = mybir.ActivationFunctionType
AX_X = mybir.AxisListType.X

P = 128
B, N, D = 16, 256, 128
T = B * N
C = T // P
E = 8
K = T * 2 // E
HID = 512
HC = HID // P
SL = K // P
ROW = D + E
H, FD, HD = 16, 16, 64
ENC = 64
PAIRS = H // 2
LN_EPS = 1e-5
Z_EPS = 1e-12
HEAD_SCALE = 1.0 / (2 * 4.0 ** 2) ** 0.5
HEAD_SHIFT = 0.25 / (2 * HEAD_SCALE)
HALF = 1.0 - HEAD_SHIFT ** 2
BITS = 30

UNROLL = 5


class Steps:

    def __init__(self, engine, sem, start=0):
        self.engine, self.sem, self.n = engine, sem, start

    def done(self, instruction):
        instruction.then_inc(self.sem, 1)
        self.n = self.n + 1
        return self.n

    def after(self, value=None):
        self.engine.wait_ge(self.sem, self.n if value is None else value)



def wait_unless_first(engine, sem, value):
    if not (isinstance(value, int) and value == 0):
        engine.wait_ge(sem, value)


def load_tokens(sp, xt, src, x_in):
    for i in range(4):
        part = slice(8 * i, 8 * i + 8)
        sp.dma_start(xt[:, part, :], src[:, part, :]).then_inc(x_in[i], 16)


def ffn_stage(nc, name, consts, weights, psum, x_src, x_acc, table, tokens=None, turn=None):
    src = x_src.rearrange("(c p) d -> p c d", p=P)
    acc = x_acc.rearrange("(c p) d -> p c d", p=P)
    QT = 4
    ident = consts["ident"]

    with ExitStack() as ctx:
        def sem(n):
            return ctx.enter_context(nc.semaphore(f"{name}_{n}"))

        def sb(n, shape, dt=F32):
            return ctx.enter_context(nc.sbuf_tensor(f"{name}_{n}", shape, dt))

        flat = C * E
        buf = {
            "rows": sb("rows", [P, C, ROW]), "stats": sb("stats", [P, C, 6]),
            "mv": sb("mv", [P, C, 2]), "rstd": sb("rstd", [P, C]), "std": sb("std", [P, C]),
            "tmp32": sb("tmp32", [P, 4, C]), "logitsT": sb("logitsT", [P, 2, 512]), "scores": sb("scores", [P, flat]),
            "work": sb("work", [P, 4, flat]), "sT": sb("sT", [P, flat]), "thr": sb("thr", [P, 1], I32),
            "cand": sb("cand", [P, 1], I32), "take": sb("take", [P, 1], I32), "cmp": sb("cmp", [P, flat]),
            "count": sb("count", [P, 1], BF16), "thr_wide": sb("thr_wide", [P, P]), "thr_row": sb("thr_row", [P, E]),
            "gt": sb("gt", [P, flat], BF16), "eq": sb("eq", [P, flat], BF16), "sel": sb("sel", [P, flat], BF16),
            "before": sb("before", [P, flat], BF16), "need": sb("need", [P, E]), "need2": sb("need2", [P, E]),
            "need3": sb("need3", [P, E]), "slot_i": sb("slot_i", [P, flat], I32), "hi_i": sb("hi_i", [P, flat], I32),
            "lo_i": sb("lo_i", [P, flat], I32), "hi": sb("hi", [P, flat], BF16), "lo": sb("lo", [P, flat], BF16),
            "hi_hot": sb("hi_hot", [P, C, P], BF16), "lo_hot": sb("lo_hot", [P, C, SL], BF16),
            "lo_val": sb("lo_val", [P, C, 2 * SL], BF16), "list": sb("list", [P, 2 * SL]),
            "idx": sb("idx", [P, E * SL], I32), "gather_idx": [sb(f"gather_idx{u}", [P, SL], I32) for u in range(2)],
            "scatter_idx": [sb(f"scatter_idx{u}", [P, SL], I32) for u in range(2)],
            "tok": [sb(f"tok{u}", [P, SL, ROW]) for u in range(2)], "tokT": sb("tokT", [D, K]),
            "hidden": sb("hidden", [P, HC, K]), "yb": sb("yb", [P, SL, D]), "gate": [sb(f"gate{u}", [P, SL]) for u in range(2)],
            "y": [sb(f"y{u}", [P, SL, D]) for u in range(2)]}
        scores, xnT = buf["scores"], buf["hidden"][:, :, :].rearrange("p k t -> p (k t)")
        stats, mv, rstd, tmp32 = buf["stats"], buf["mv"], buf["rstd"], buf["tmp32"]
        xt, x_in = tokens or (sb("xt", [P, C, D]), [sem(f"x_in{i}") for i in range(4)])
        residual_out = sem("residual_out")
        table_out = sem("table_out")
        xn_ready = sem("xn_ready")
        xn_pool_ready = sem("xn_pool_ready")
        rstd_ready = sem("rstd_ready")
        logitsT_psum = sem("logitsT_psum")
        logitsT_ready = sem("logitsT_ready")
        xnT_psum = sem("xnT_psum")
        xnT_ready = sem("xnT_ready")
        logits_ready = sem("logits_ready")
        var_ready = sem("var_ready")
        std_ready = sem("std_ready")
        shifted_ready = sem("shifted_ready")
        exp_ready = sem("exp_ready")
        scores_ready = sem("scores_ready")
        scoresT_psum = sem("scoresT_psum")
        counts_ready = sem("counts_ready")
        total_ready = sem("total_ready")
        thr_ready = sem("thr_ready")
        thrT_ready = sem("thrT_ready")
        gt_ready = sem("gt_ready")
        gt_count = sem("gt_count")
        eq_ready = sem("eq_ready")
        eq_rank = sem("eq_rank")
        sel_ready = sem("sel_ready")
        sel_rank = sem("sel_rank")
        dve_step = sem("dve_step")
        onehot_ready = sem("onehot_ready")
        list_ready = sem("list_ready")
        idx_ready = sem("idx_ready")
        w1_in = [sem("w1_in0"), sem("w1_in1")]
        gathered = [sem("gathered0"), sem("gathered1")]
        gather_idx_ready = sem("gather_idx_ready")
        scatter_idx_ready = sem("scatter_idx_ready")
        gate_ready = sem("gate_ready")
        act_turn = sem("act_turn")
        pool_turn = sem("pool_turn")
        tokT_psum = sem("tokT_psum")
        tokT_ready = sem("tokT_ready")
        hidden_psum = sem("hidden_psum")
        hidden_ready = sem("hidden_ready")
        y_psum = sem("y_psum")
        y_biased = sem("y_biased")
        y_ready = sem("y_ready")
        scattered = sem("scattered")
        weights_turned = sem("weights_turned")
        weights_ready = sem("weights_ready")
        block = ctx.enter_context(nc.Block())

        logitsT = psum[2:4]
        logits = [bank[:, :].rearrange("p (q g r) -> p g q r", q=4, g=4)[:, :, :, 0:E] for bank in (psum[7], psum[4])]
        scoresT = psum[6][:, 0:2 * P]
        total = psum[5][:, 0:1]
        thr_psum = psum[5][:, 0:P]
        rank_psum = psum[4][:, 0:C * E]
        list_psum = psum[7][:, 0:2 * SL]
        hidden_bank = [psum[2], psum[3], psum[6]]

        @block.sync
        def _(sp):
            def load_w1(e, u):
                sp.dma_start(weights["w1"][u][:, :], weights["w1_dram"][bass.ds(e, 1), :, :]
                             .rearrange("e d h -> d (e h)")).then_inc(w1_in[u], 16)

            if not tokens:
                load_tokens(sp, xt, src, x_in)
            for u in range(2):
                load_w1(u, u)
            if tokens:
                for i in range(4):
                    sp.wait_ge(x_in[i], 16)
                sp.dma_start(acc, xt[:]).then_inc(residual_out, 16)
                sp.wait_ge(residual_out, 16)
            sp.wait_ge(scores_ready, 2)
            sp.dma_start(table.rearrange("(c p) r -> p c r", p=P), buf["rows"][:]).then_inc(table_out, 16)
            sp.wait_ge(table_out, 16)
            with sp.Fori(0, E // 2 - 1) as g:
                for u in range(2):
                    sp.wait_ge(hidden_psum, (g * 2 + u) * (2 * HC) + 2 * HC)
                    load_w1(g * 2 + (2 + u), u)

        @block.vector
        def _(dve):
            own = Steps(dve, dve_step)
            rows = buf["rows"]
            for i in range(4):
                dve.wait_ge(x_in[i], 16)
                for c in range(8 * i, 8 * i + 8):
                    last = own.done(nc.vector.bn_stats(stats[:, c, :], xt[:, c, :]))
            own.after(last)
            for c in range(C):
                last = own.done(nc.vector.bn_aggr(mv[:, c, :], stats[:, c, :]))
            own.after(last)
            var = mv[:, :, 1]
            own.done(nc.vector.tensor_scalar(tmp32[:, 0, :], var, LN_EPS, None, ALU.add))
            own.after()
            nc.vector.tensor_copy(tmp32[:, 1, :], tmp32[:, 0, :]).then_inc(var_ready, 1)
            dve.wait_ge(std_ready, 1)
            own.done(nc.vector.reciprocal(tmp32[:, 2, :], buf["std"][:, :]))
            own.after()
            own.done(nc.vector.tensor_tensor(tmp32[:, 3, :], tmp32[:, 0, :], tmp32[:, 2, :], ALU.mult))
            own.after()
            own.done(nc.vector.tensor_tensor(tmp32[:, 2, :], tmp32[:, 3, :], buf["std"][:, :], ALU.add))
            own.after()
            own.done(nc.vector.tensor_scalar(tmp32[:, 3, :], tmp32[:, 2, :], 0.5, None, ALU.mult))
            own.after()
            nc.vector.reciprocal(rstd[:, :], tmp32[:, 3, :]).then_inc(rstd_ready, 1)
            dve.wait_ge(rstd_ready, 1)
            for c in range(C):
                if c % QT != QT - 1:
                    nc.vector.tensor_scalar(rows[:, c, 0:D], xt[:, c, :], mv[:, c, 0:1], rstd[:, c:c + 1],
                                            ALU.subtract, ALU.mult).then_inc(xn_ready, 1)
            work = buf["work"]
            w3 = [work[:, i, :].rearrange("p (c e) -> p c e", e=E) for i in range(4)]
            for half in range(2):
                dve.wait_ge(logits_ready, half + 1)
                tiles = slice(C // 2 * half, C // 2 * half + C // 2)
                highest = tmp32[:, 0, tiles].rearrange("p (g q) -> p g q", g=4)
                own.done(nc.vector.tensor_reduce(highest, logits[half], AX_X, ALU.max))
                own.after()
                nc.vector.tensor_tensor(w3[0][:, tiles, :].rearrange("p (g q) e -> p g q e", g=4), logits[half],
                                        highest.unsqueeze(3).broadcast_to([P, 4, 4, E]),
                                        ALU.subtract).then_inc(shifted_ready, 1)
            dve.wait_ge(exp_ready, 2)
            own.done(nc.vector.tensor_reduce(tmp32[:, 1, :], w3[1], AX_X, ALU.add))
            own.after()
            own.done(nc.vector.reciprocal(tmp32[:, 2, :], tmp32[:, 1, :]))
            own.after()
            inv = tmp32[:, 2, :].unsqueeze(2).broadcast_to([P, C, E])
            s3 = scores[:, :].rearrange("p (c e) -> p c e", e=E)
            nc.vector.tensor_tensor(s3, w3[1], inv, ALU.mult).then_inc(scores_ready, 1)
            nc.vector.tensor_tensor(rows[:, :, D:ROW], w3[1], inv, ALU.mult).then_inc(scores_ready, 1)
            sT = buf["sT"]
            thr, cand, take = buf["thr"], buf["cand"], buf["take"]
            own.done(nc.vector.memset(thr[:, :], 0))
            own.done(nc.vector.memset(take[:, :], 0))
            own.done(nc.vector.tensor_copy(cand[:, :], consts["bits_i"][:, 0:1]))
            dve.wait_ge(scoresT_psum, 1)
            own.done(nc.vector.tensor_copy(sT[:, :], scoresT))
            own.after()
            start = own.n
            PER_BIT = 3
            with dve.Fori(0, BITS // UNROLL) as r:
                for b in range(UNROLL):
                    i = r * UNROLL + b
                    bit = Steps(dve, dve_step, i * PER_BIT + start)
                    nc.vector.tensor_scalar(buf["cmp"][:, :], sT[:, :], cand[:, :].bitcast(F32), 0.0,
                                            ALU.is_ge, ALU.add, accum_out=buf["count"][:, :]).then_inc(counts_ready, 1)
                    bit.done(nc.vector.tensor_tensor(thr[:, :], thr[:, :], take[:, :], ALU.bitwise_or))
                    bit.after()
                    dve.wait_ge(total_ready, i + 1)
                    bit.done(nc.vector.tensor_scalar(take[:, :], total, float(K), consts["bits_f"][:, bass.ds(i, 1)],
                                                     ALU.is_ge, ALU.mult))
                    bit.after()
                    bit.done(nc.vector.scalar_tensor_tensor(cand[:, :], take[:, :], consts["bits_i"][:, bass.ds(i + 1, 1)],
                                                            thr[:, :], ALU.bitwise_or, ALU.bitwise_or))
                    bit.after()
            own = Steps(dve, dve_step, start + BITS * PER_BIT)
            own.after()
            thr = cand[:, :].bitcast(F32)
            nc.vector.tensor_copy(buf["thr_wide"][:, :], thr.broadcast_to([P, P])).then_inc(thr_ready, 1)
            dve.wait_ge(thrT_ready, 1)
            own.done(nc.vector.tensor_copy(buf["thr_row"][:, :], thr_psum[:, 0:E]))
            own.after()
            s_ec = scores[:, :].rearrange("p (c e) -> p e c", e=E)
            thr_ec = buf["thr_row"][:, :].unsqueeze(2).broadcast_to([P, E, C])

            def ec(t):
                return t[:, :].rearrange("p (e c) -> p e c", e=E)

            nc.vector.tensor_tensor(ec(buf["gt"]), s_ec, thr_ec, ALU.is_gt).then_inc(gt_ready, 1)
            own.done(nc.vector.tensor_tensor(ec(buf["eq"]), s_ec, thr_ec, ALU.is_equal))
            own.after()

            def ec_psum(t):
                return t.rearrange("p (e c) -> p e c", e=E)

            def earlier_tiles(mask):
                own.done(nc.vector.tensor_tensor_scan(work[:, 0, :], consts["restart"][:, :], mask[:, :], 0.0,
                                                      ALU.mult, ALU.add))
                own.after()
                return nc.vector.tensor_tensor(buf["before"][:, :], work[:, 0, :], mask[:, :], ALU.subtract)

            earlier_tiles(buf["eq"]).then_inc(eq_ready, 1)
            dve.wait_ge(gt_count, 1)
            own.done(nc.vector.tensor_reduce(buf["need"][:, :], ec_psum(rank_psum), AX_X, ALU.add))
            own.after()
            own.done(nc.vector.tensor_scalar(buf["need2"][:, :], buf["need"][:, :], -1.0, float(K), ALU.mult, ALU.add))
            own.after()
            nc.vector.tensor_copy(buf["need3"][:, :], buf["need2"][:, :]).then_inc(eq_ready, 1)
            dve.wait_ge(eq_rank, 1)
            own.done(nc.vector.tensor_tensor(work[:, 1, :].rearrange("p (e c) -> p e c", e=E), ec_psum(rank_psum),
                                             buf["need2"][:, :].unsqueeze(2).broadcast_to([P, E, C]), ALU.is_le))
            own.after()
            own.done(nc.vector.tensor_tensor(work[:, 2, :], work[:, 1, :], buf["eq"][:, :], ALU.mult))
            own.after()
            own.done(nc.vector.tensor_tensor(buf["sel"][:, :], work[:, 2, :], buf["gt"][:, :], ALU.add))
            own.after()
            earlier_tiles(buf["sel"]).then_inc(sel_ready, 1)
            dve.wait_ge(sel_rank, 1)
            own.done(nc.vector.tensor_tensor(work[:, 1, :], rank_psum, buf["sel"][:, :], ALU.mult))
            own.after()
            own.done(nc.vector.tensor_scalar(buf["slot_i"][:, :], work[:, 1, :], -1.0, None, ALU.add))
            own.after()
            own.done(nc.vector.tensor_scalar(buf["hi_i"][:, :], buf["slot_i"][:, :], 3, None, ALU.arith_shift_right))
            own.done(nc.vector.tensor_scalar(buf["lo_i"][:, :], buf["slot_i"][:, :], SL - 1, None, ALU.bitwise_and))
            own.after()
            own.done(nc.vector.tensor_copy(buf["hi"][:, :], buf["hi_i"][:, :]))
            own.done(nc.vector.tensor_copy(buf["lo"][:, :], buf["lo_i"][:, :]))
            own.after()
            start = own.n
            PER_LIST = 2

            def build_list(e):
                own = Steps(dve, dve_step, e * PER_LIST + start)
                hi = buf["hi"][:, bass.ds(e * C, C)].unsqueeze(2).broadcast_to([P, C, P])
                lo = buf["lo"][:, bass.ds(e * C, C)].unsqueeze(2).broadcast_to([P, C, SL])
                own.done(nc.vector.tensor_tensor(buf["lo_hot"][:, :, :], consts["iota_f"][:, 0:SL].unsqueeze(1)
                                                 .broadcast_to([P, C, SL]), lo, ALU.is_equal))
                nc.vector.tensor_tensor(buf["hi_hot"][:, :, :], consts["iota_f"][:, :].unsqueeze(1)
                                        .broadcast_to([P, C, P]), hi, ALU.is_equal).then_inc(onehot_ready, 1)
                own.after()
                nc.vector.tensor_scalar(buf["lo_val"][:, :, 0:SL], buf["lo_hot"][:, :, :], consts["part"][:, 0:1],
                                        None, ALU.mult).then_inc(onehot_ready, 1)
                nc.vector.tensor_tensor(buf["lo_val"][:, :, SL:2 * SL], buf["lo_hot"][:, :, :],
                                        consts["iota_f"][:, 0:C].unsqueeze(2).broadcast_to([P, C, SL]),
                                        ALU.mult).then_inc(onehot_ready, 1)
                dve.wait_ge(list_ready, e + 1)
                own.done(nc.vector.tensor_copy(buf["list"][:, :], list_psum))
                own.after()
                nc.vector.scalar_tensor_tensor(buf["idx"][:, bass.ds(e * SL, SL)], buf["list"][:, SL:2 * SL], float(P),
                                               buf["list"][:, 0:SL], ALU.mult, ALU.add).then_inc(idx_ready, 1)

            def take_tokens(e, u):
                for half in range(2):
                    dve.wait_ge(tokT_psum, e * 2 + half + 1)
                    nc.vector.tensor_copy(buf["tokT"][:, 512 * half:512 * half + 512],
                                          psum[half][:, :]).then_inc(tokT_ready, 1)
                if not isinstance(e, int) or e >= 2:
                    dve.wait_ge(y_ready, e * 2 - 2)
                nc.vector.tensor_scalar(buf["gate"][u][:, :], buf["tok"][u][:, :, bass.ds(e + D, 1)]
                                        .rearrange("p j o -> p (j o)"), 0.5, None, ALU.mult).then_inc(gate_ready, 1)

            def expert(e, u, lists, takes):
                if lists:
                    build_list(e + 2)
                if takes:
                    take_tokens(e + 1, 1 - u)
                for half in range(2):
                    slots = slice(4 * half, 4 * half + 4)
                    dve.wait_ge(y_psum, e * 2 + half + 1)
                    y4 = psum[4 + half][:, :].rearrange("p (j d) -> p j d", d=D)
                    bias = weights["b2"][:, bass.ds(e * D, D)].unsqueeze(1).broadcast_to([P, 4, D])
                    nc.vector.tensor_tensor(buf["yb"][:, slots, :], y4, bias, ALU.add).then_inc(y_biased, 1)
                    dve.wait_ge(y_biased, e * 2 + half + 1)
                    if half == 0:
                        if not isinstance(e, int) or e >= 2:
                            dve.wait_ge(scattered, (e - 1) * (16 * SL))
                        dve.wait_ge(gate_ready, e + 1)
                    gate = buf["gate"][u][:, slots].unsqueeze(2).broadcast_to([P, 4, D])
                    nc.vector.tensor_tensor(buf["y"][u][:, slots, :], buf["yb"][:, slots, :], gate,
                                            ALU.mult).then_inc(y_ready, 1)

            build_list(0)
            build_list(1)
            take_tokens(0, 0)
            dve.wait_ge(weights["b2_in"], 16)
            expert(0, 0, True, True)
            expert(1, 1, True, True)
            with dve.Fori(1, E // 2 - 1) as g:
                expert(g * 2, 0, True, True)
                expert(g * 2 + 1, 1, True, True)
            expert(E - 2, 0, False, True)
            expert(E - 1, 1, False, False)

        @block.scalar
        def _(act):
            if turn:
                for i, (_, destination, column) in enumerate(turn["blocks"]):
                    if i % 2 == 0:
                        act.wait_ge(weights_turned, i // 2 + 1)
                        nc.scalar.copy(destination[:, column:column + 2 * P], psum[i // 2 % 4][:, 0:2 * P]
                                       ).then_inc(weights_ready, 1)
            act.wait_ge(var_ready, 1)
            nc.scalar.activation(buf["std"][:, :], tmp32[:, 1, :], ACT.Sqrt).then_inc(std_ready, 1)
            for i in range(C // QT):
                act.wait_ge(xnT_psum, i + 1)
                nc.scalar.copy(xnT[:, 512 * i:512 * i + 512], psum[i % 2][:, :]).then_inc(xnT_ready, 1)
                if i % 4 == 3:
                    act.wait_ge(logitsT_psum, i // 4 + 1)
                    nc.scalar.copy(buf["logitsT"][:, i // 4, :], logitsT[i // 4][:, :]).then_inc(logitsT_ready, 1)
            for half in range(2):
                act.wait_ge(shifted_ready, half + 1)
                columns = slice(flat // 2 * half, flat // 2 * half + flat // 2)
                nc.scalar.activation(buf["work"][:, 1, columns], buf["work"][:, 0, columns], ACT.Exp
                                     ).then_inc(exp_ready, 1)

            def expert(e):
                for n in range(2 * HC):
                    k, half = n // 2, n % 2
                    act.wait_ge(hidden_psum, e * (2 * HC) + (n + 1))
                    act.sem_inc(act_turn, 1)
                    nc.scalar.activation(buf["hidden"][:, k, 512 * half:512 * half + 512], hidden_bank[n % 3][:, :],
                                         ACT.Gelu, bias=weights["b1"][:, bass.ds(e * HC + k, 1)]
                                         ).then_inc(hidden_ready, 1)

            expert(0)
            with act.Fori(1, E) as e:
                expert(e)

        @block.tensor
        def _(pe):
            if turn:
                pe.wait_ge(turn["loaded"], turn["loads"] * 16)
                for i, (source, _, _) in enumerate(turn["blocks"]):
                    if i >= 8 and i % 2 == 0:
                        pe.wait_ge(weights_ready, i // 2 - 3)
                    mm = nc.tensor.transpose(psum[i // 2 % 4][:, P * (i % 2):P * (i % 2) + P], source, ident[:, :])
                    if i % 2:
                        mm.then_inc(weights_turned, 1)
                pe.wait_ge(weights_ready, len(turn["blocks"]) // 2)

            def route(half):
                pe.wait_ge(xnT_ready, 4 * half + 4)
                for g in range(4):
                    i = 4 * half + g
                    mm = nc.tensor.matmul(logitsT[half][32 * g:32 * g + 32, :], weights["wr"][:, :],
                                          xnT[:, 512 * i:512 * i + 512], start=True, stop=True)
                mm.then_inc(logitsT_psum, 1)

            def turn_logits(half):
                pe.wait_ge(logitsT_ready, half + 1)
                bank = (psum[7], psum[4])[half]
                for q in range(4):
                    mm = nc.tensor.transpose(bank[:, P * q:P * q + P], buf["logitsT"][:, half, P * q:P * q + P],
                                             ident[:, :])
                mm.then_inc(logits_ready, 1)

            pe.wait_ge(weights["wr_in"], 16)
            for i in range(C // QT):
                if i >= 2:
                    pe.wait_ge(xnT_ready, i - 1)
                for q in range(QT):
                    if q == QT - 1:
                        pe.wait_ge(xn_pool_ready, i + 1)
                    else:
                        pe.wait_ge(xn_ready, i * (QT - 1) + q + 1)
                    mm = nc.tensor.transpose(psum[i % 2][:, P * q:P * q + P], buf["rows"][:, QT * i + q, 0:D],
                                             ident[:, :])
                mm.then_inc(xnT_psum, 1)
                if i == 4:
                    route(0)
                if i == 6:
                    turn_logits(0)
            route(1)
            turn_logits(1)
            pe.wait_ge(scores_ready, 1)
            for half in range(2):
                mm = nc.tensor.transpose(scoresT[:, P * half:P * half + P], scores[:, P * half:P * half + P],
                                         ident[:, :])
            mm.then_inc(scoresT_psum, 1)
            with pe.Fori(0, BITS // UNROLL) as r:
                for b in range(UNROLL):
                    pe.wait_ge(counts_ready, r * UNROLL + b + 1)
                    nc.tensor.matmul(total, consts["same_expert"][:, :], buf["count"][:, :], start=True,
                                     stop=True).then_inc(total_ready, 1)
            pe.wait_ge(thr_ready, 1)
            nc.tensor.transpose(thr_psum, buf["thr_wide"][:, :], ident[:, :]).then_inc(thrT_ready, 1)
            pe.wait_ge(gt_ready, 1)
            nc.tensor.matmul(rank_psum, consts["ones"][:, :], buf["gt"][:, :], start=True,
                             stop=True).then_inc(gt_count, 1)
            pe.wait_ge(eq_ready, 2)
            nc.tensor.matmul(rank_psum, consts["tri"][:, :], buf["eq"][:, :], start=True, stop=False)
            nc.tensor.matmul(rank_psum, consts["ones"][:, :], buf["before"][:, :], start=False,
                             stop=True).then_inc(eq_rank, 1)
            pe.wait_ge(sel_ready, 1)
            nc.tensor.matmul(rank_psum, consts["tri"][:, :], buf["sel"][:, :], start=True, stop=False)
            nc.tensor.matmul(rank_psum, consts["ones"][:, :], buf["before"][:, :], start=False,
                             stop=True).then_inc(sel_rank, 1)

            def token_list(e):
                pe.wait_ge(onehot_ready, e * 3 + 3)
                for c in range(C):
                    mm = nc.tensor.matmul(list_psum, buf["hi_hot"][:, c, :], buf["lo_val"][:, c, :],
                                          start=(c == 0), stop=(c == C - 1))
                mm.then_inc(list_ready, 1)

            def turn_tokens(e, u):
                pe.wait_ge(gathered[u], (e - u) * (8 * SL) + 16 * SL)
                for half in range(2):
                    for q in range(4):
                        mm = nc.tensor.transpose(psum[half][:, P * q:P * q + P], buf["tok"][u][:, 4 * half + q, 0:D],
                                                 ident[:, :])
                    mm.then_inc(tokT_psum, 1)

            def expert(e, u, lists, turns):
                pe.wait_ge(tokT_ready, e * 2 + 2)
                pe.wait_ge(w1_in[u], (e - u) * 8 + 16)
                for n in range(2 * HC):
                    k, half = n // 2, n % 2
                    if n >= 3:
                        pe.wait_ge(hidden_ready, e * (2 * HC) + (n - 2))
                    nc.tensor.matmul(hidden_bank[n % 3][:, :], weights["w1"][u][:, P * k:P * k + P],
                                     buf["tokT"][:, 512 * half:512 * half + 512], start=True,
                                     stop=True).then_inc(hidden_psum, 1)
                if lists:
                    token_list(e + 2)
                if turns:
                    turn_tokens(e + 1, 1 - u)
                pe.wait_ge(hidden_ready, e * (2 * HC) + 2 * HC)
                wait_unless_first(pe, y_biased, e * 2)
                for half in range(2):
                    for q in range(4):
                        for k in range(HC):
                            mm = nc.tensor.matmul(psum[4 + half][:, P * q:P * q + P],
                                                  buf["hidden"][:, k, 512 * half + P * q:512 * half + P * q + P],
                                                  weights["w2"][:, bass.ds(e * HID + k * P, P)],
                                                  start=(k == 0), stop=(k == HC - 1))
                    mm.then_inc(y_psum, 1)

            token_list(0)
            token_list(1)
            turn_tokens(0, 0)
            pe.wait_ge(weights["w2_in"], 16)
            expert(0, 0, True, True)
            expert(1, 1, True, True)
            with pe.Fori(1, E // 2 - 1) as g:
                expert(g * 2, 0, True, True)
                expert(g * 2 + 1, 1, True, True)
            expert(E - 2, 0, False, True)
            expert(E - 1, 1, False, False)

        @block.gpsimd
        def _(pool):
            pool.wait_ge(rstd_ready, 1)
            for c in range(QT - 1, C, QT):
                nc.gpsimd.tensor_scalar(buf["rows"][:, c, 0:D], xt[:, c, :], mv[:, c, 0:1], rstd[:, c:c + 1],
                                        ALU.subtract, ALU.mult).then_inc(xn_pool_ready, 1)
            pool.wait_ge(table_out, 16)
            if tokens:
                pool.wait_ge(residual_out, 16)

            def gather(e, u):
                pool.wait_ge(idx_ready, e + 1)
                if not isinstance(e, int) or e >= 2:
                    pool.wait_ge(gate_ready, e - 1)
                nc.gpsimd.tensor_copy(buf["gather_idx"][u][:, :], buf["idx"][:, bass.ds(e * SL, SL)]
                                      ).then_inc(gather_idx_ready, 1)
                pool.wait_ge(gather_idx_ready, e + 1)
                pool.sem_inc(pool_turn, 1)
                for j in range(SL):
                    nc.gpsimd.indirect_dma_start(
                        out=buf["tok"][u][:, j, :], out_offset=None, in_=table,
                        in_offset=bass.IndirectOffsetOnAxis(ap=buf["gather_idx"][u][:, j:j + 1], axis=0)
                    ).then_inc(gathered[u], 16)

            def expert(e, u, gathers):
                if gathers:
                    gather(e + 2, u)
                nc.gpsimd.tensor_copy(buf["scatter_idx"][u][:, :], buf["idx"][:, bass.ds(e * SL, SL)]
                                      ).then_inc(scatter_idx_ready, 1)
                pool.wait_ge(scatter_idx_ready, e + 1)
                wait_unless_first(pool, scattered, e * (16 * SL))
                for half in range(2):
                    pool.wait_ge(y_ready, e * 2 + half + 1)
                    pool.sem_inc(pool_turn, 1)
                    for j in range(4 * half, 4 * half + 4):
                        nc.gpsimd.indirect_dma_start(
                            out=x_acc, out_offset=bass.IndirectOffsetOnAxis(ap=buf["scatter_idx"][u][:, j:j + 1], axis=0),
                            in_=buf["y"][u][:, j, :], in_offset=None, compute_op=ALU.add).then_inc(scattered, 16)

            gather(0, 0)
            gather(1, 1)
            expert(0, 0, True)
            expert(1, 1, True)
            with pool.Fori(1, E // 2 - 1) as g:
                expert(g * 2, 0, True)
                expert(g * 2 + 1, 1, True)
            expert(E - 2, 0, False)
            expert(E - 1, 1, False)
            pool.wait_ge(scattered, E * 16 * SL)



Q_PART = [0, 0, 1, 1, 0, 2, 1, 2]
K_PART = [0, 1, 0, 1, 2, 0, 2, 1]
SLOTS = len(Q_PART)
HALVES = 2
ROUNDS = B // HALVES
RT = HALVES * N
TILES = RT // P
KW = N + ENC
ROW_GROUP = 32
NCH = H * FD // P
STEPS = HALVES * PAIRS
LN_STEP, SQRT_STEP, TURN_STEP, QK_STEP = 0, 1, 3, 4
LAG = 2
INVERT_STEP = PAIRS + 4
OUT_STEP, RESIDUAL_STEP = (0, 7), (1, 8)


def attention(nc, psum, consts, wT, x, scratch):
    with ExitStack() as ctx:
        def sem(n):
            return ctx.enter_context(nc.semaphore(f"attn_{n}"))

        def sb(n, shape, dt=F32):
            return ctx.enter_context(nc.sbuf_tensor(f"attn_{n}", shape, dt))

        x_ln, xn, x_res = sb("x_ln", [P, TILES, D]), sb("xn", [P, TILES, D]), sb("x_res", [P, TILES, D])
        x_new = sb("x_new", [P, TILES, D])
        xnT = sb("xnT", [D, RT])
        stats, mv = sb("stats", [P, TILES, 6]), sb("mv", [P, TILES, 2])
        var, std = sb("var", [P, TILES]), sb("std", [P, TILES])
        ln_tmp, rstd = sb("ln_tmp", [P, 3, TILES]), sb("rstd", [P, TILES])
        q_parts = sb("q_parts", [P, 3, NCH, RT], BF16)
        k_parts = sb("k_parts", [P, 3, NCH, HALVES, KW], BF16)
        rest = [sb(f"rest{u}", [P, RT]) for u in range(2)]
        q_stack = [sb(f"q_stack{a}", [P, H, N], BF16) for a in range(HALVES)]
        k_stack = [sb(f"k_stack{a}", [P, H, KW], BF16) for a in range(HALVES)]
        v = sb("v", [P, TILES, H * HD])
        v_enc = sb("v_enc", [P, HALVES, PAIRS, P])
        att = [sb(f"att{u}", [P, 2, 4 * P]) for u in range(4)]
        den, z = ([sb(f"{n}{a}", [P, N]) for a in range(HALVES)] for n in ("den", "z"))
        z_wide = [sb(f"z_wide{a}", [P, PAIRS * N]) for a in range(HALVES)]
        yT = [sb(f"yT{a}", [P, PAIRS, N]) for a in range(HALVES)]
        q_dram, k_dram, z_dram = scratch

        x_ln_in = sem("x_ln_in")
        x_res_in = [sem(f"x_res_in{a}") for a in range(HALVES)]
        var_ready = sem("var_ready")
        std_ready = sem("std_ready")
        xn_ready = sem("xn_ready")
        turned = sem("turned")
        xnT_ready = sem("xnT_ready")
        qk_psum = sem("qk_psum")
        part1_ready = sem("part1_ready")
        parts_ready = sem("parts_ready")
        parts_out = sem("parts_out")
        stack_in = [sem(f"stack_in{a}") for a in range(HALVES)]
        v_psum = sem("v_psum")
        v_ready = sem("v_ready")
        v_enc_ready = sem("v_enc_ready")
        scores_psum = sem("scores_psum")
        squares_ready = sem("squares_ready")
        att_ready = sem("att_ready")
        y_psum = sem("y_psum")
        y_copied = sem("y_copied")
        den_psum = sem("den_psum")
        den_ready = sem("den_ready")
        z_ready = sem("z_ready")
        z_out = sem("z_out")
        z_wide_in = sem("z_wide_in")
        yT_ready = sem("yT_ready")
        out_psum = sem("out_psum")
        x_new_ready = sem("x_new_ready")
        x_out = sem("x_out")
        dve_step = sem("dve_step")
        dve_turn = sem("dve_turn")
        sp_turn = sem("sp_turn")
        pool_turn = sem("pool_turn")
        split_step = sem("split_step")
        v_enc_clear = sem("v_enc_clear")
        block = ctx.enter_context(nc.Block())

        S, DEN, Y, PR, TR = psum[0:2], psum[2], psum[3:5], psum[5:7], psum[7]
        NQK = 2 * NCH + 1
        LN_STEPS = 2 * TILES + 5
        VN = TILES * 2

        def x_round(i):
            return x[bass.ds(i * RT, RT), :].rearrange("(t p) d -> p t d", p=P)

        LATE, EARLY, ENC_KEYS = slice(0, P), slice(P, 3 * P), slice(3 * P, 4 * P)
        MASKED, WHOLE = slice(0, 2 * P), slice(2 * P, 4 * P)

        def qk_tile(j):
            bank = PR[j % 2]
            if j < NCH:
                return (lambda s: q_parts[:, s, j, :]), bank[:, :]
            if j < 2 * NCH:
                return ((lambda s: k_parts[:, s, j - NCH, :, 0:N]),
                        bank[:, :].rearrange("p (a n) -> p a n", a=HALVES))
            return ((lambda s: k_parts[:, s, :, :, N:KW].rearrange("p c a n -> p (c a) n")),
                    bank[:, 0:NCH * HALVES * ENC].rearrange("p (g n) -> p g n", n=ENC))

        @block.sync
        def _(sp):
            def load_ln(i):
                sp.dma_start(x_ln[:], x_round(i)).then_inc(x_ln_in, 16)

            def store_parts(i):
                sp.wait_ge(part1_ready, i * NQK + NQK)
                sp.wait_ge(parts_ready, i * NQK + NQK)
                sp.dma_start(q_dram.rearrange("s c p t -> p s c t"), q_parts[:]).then_inc(parts_out, 16)
                sp.dma_start(k_dram.rearrange("s c p t -> p s c t"),
                             k_parts[:].rearrange("p s c a w -> p s c (a w)")).then_inc(parts_out, 16)
                sp.wait_ge(parts_out, i * 32 + 32)

            def load_stack(a):
                for s in range(SLOTS):
                    sp.dma_start(q_stack[a][FD * s:FD * s + FD, :, :],
                                 q_dram[Q_PART[s]].rearrange("c (h f) t -> f (c h) t", f=FD)[:, :, N * a:N * a + N]
                                 ).then_inc(stack_in[a], 16)
                    sp.dma_start(k_stack[a][FD * s:FD * s + FD, :, :],
                                 k_dram[K_PART[s]].rearrange("c (h f) t -> f (c h) t", f=FD)[:, :, KW * a:KW * a + KW]
                                 ).then_inc(stack_in[a], 16)

            def load_res(i, a):
                sp.dma_start(x_res[:, 2 * a:2 * a + 2, :], x_round(i)[:, 2 * a:2 * a + 2, :]
                             ).then_inc(x_res_in[a], 16)

            def store_out(i, a):
                n = i * 2 + a
                sp.wait_ge(x_new_ready, n + 1)
                sp.sem_inc(sp_turn, 1)
                sp.dma_start(x_round(i)[:, 2 * a:2 * a + 2, :], x_new[:, 2 * a:2 * a + 2, :]).then_inc(x_out, 16)
                sp.wait_ge(x_out, n * 16 + 16)
                sp.sem_inc(sp_turn, 1)

            def round_(i, first, more):
                if more:
                    sp.wait_ge(xn_ready, i * TILES + TILES)
                    sp.sem_inc(sp_turn, 1)
                    load_ln(i + 1)
                if not first:
                    for a in range(HALVES):
                        load_res(i - 1, a)
                    for a in range(HALVES):
                        store_out(i - 1, a)
                if more:
                    sp.wait_ge(stack_in[1], i * (32 * SLOTS) + 32 * SLOTS)
                    store_parts(i + 1)
                    for a in range(HALVES):
                        sp.wait_ge(scores_psum, i * (2 * STEPS) + STEPS * (a + 1))
                        load_stack(a)

            load_ln(0)
            store_parts(0)
            load_stack(0)
            load_stack(1)
            round_(0, True, True)
            with sp.Fori(1, ROUNDS - 1) as i:
                round_(i, False, True)
            round_(ROUNDS - 1, False, False)
            for a in range(HALVES):
                load_res(ROUNDS - 1, a)
            for a in range(HALVES):
                store_out(ROUNDS - 1, a)

        @block.vector
        def _(dve):
            def layernorm_a(i):
                own = Steps(dve, dve_step, i * LN_STEPS)
                dve.wait_ge(x_ln_in, i * 16 + 16)
                for t in range(TILES):
                    own.done(nc.vector.bn_stats(stats[:, t, :], x_ln[:, t, :]))
                own.after()
                dve.sem_inc(dve_turn, 1)
                for t in range(TILES):
                    own.done(nc.vector.bn_aggr(mv[:, t, :], stats[:, t, :]))
                own.after()
                nc.vector.tensor_scalar(var[:, :], mv[:, :, 1], LN_EPS, None, ALU.add).then_inc(var_ready, 1)

            def layernorm_b(i):
                own = Steps(dve, dve_step, i * LN_STEPS + 2 * TILES)
                dve.wait_ge(std_ready, i + 1)
                own.done(nc.vector.reciprocal(ln_tmp[:, 0, :], std[:, :]))
                own.after()
                own.done(nc.vector.tensor_tensor(ln_tmp[:, 1, :], var[:, :], ln_tmp[:, 0, :], ALU.mult))
                own.after()
                own.done(nc.vector.tensor_tensor(ln_tmp[:, 2, :], ln_tmp[:, 1, :], std[:, :], ALU.add))
                own.after()
                own.done(nc.vector.tensor_scalar(ln_tmp[:, 0, :], ln_tmp[:, 2, :], 0.5, None, ALU.mult))
                own.after()
                own.done(nc.vector.reciprocal(rstd[:, :], ln_tmp[:, 0, :]))
                own.after()
                for t in range(TILES):
                    nc.vector.tensor_scalar(xn[:, t, :], x_ln[:, t, :], mv[:, t, 0:1], rstd[:, t:t + 1],
                                            ALU.subtract, ALU.mult).then_inc(xn_ready, 1)

            def split(i, j):
                own = Steps(dve, split_step, i * (2 * NQK) + 2 * j)
                tile, bank = qk_tile(j)
                dve.wait_ge(part1_ready, i * NQK + j + 1)
                r = rest[j % 2][:, 0:tile(0).shape[1] * (tile(0).shape[2] if len(tile(0).shape) == 3 else 1)]
                if len(tile(0).shape) == 3:
                    r = r.rearrange("p (a w) -> p a w", a=tile(0).shape[1])
                own.done(nc.vector.tensor_tensor(r, bank, tile(0), ALU.subtract))
                own.after()
                own.done(nc.vector.tensor_copy(tile(1), r))
                own.after()
                nc.vector.tensor_tensor(tile(2), r, tile(1), ALU.subtract).then_inc(parts_ready, 1)

            def mask(i, s):
                tile = att[s % 4]
                dve.wait_ge(squares_ready, i * (2 * STEPS) + 2 * s + 2)
                nc.vector.scalar_tensor_tensor(tile[:, :, MASKED], tile[:, :, MASKED], HALF,
                                               consts["causal"][:, :].unsqueeze(1).broadcast_to([P, 2, 2 * P]),
                                               ALU.add, ALU.mult).then_inc(att_ready, 1)
                nc.vector.tensor_scalar(tile[:, :, WHOLE], tile[:, :, WHOLE], HALF, None,
                                        ALU.add).then_inc(att_ready, 1)

            def invert(i, a):
                dve.wait_ge(den_ready, i * 2 + a + 1)
                nc.vector.reciprocal(z[a][:, :], den[a][:, :]).then_inc(z_ready, 1)

            def values_enc(i):
                for a in range(HALVES):
                    dve.wait_ge(v_psum, i * (VN + HALVES) + a + 1)
                    for w in range(2):
                        rows = slice(ENC * w, ENC * w + ENC)
                        nc.vector.tensor_copy(v_enc[rows, a, :, HD * w:HD * w + HD],
                                              PR[a][rows, :].rearrange("p (g e) -> p g e", e=HD)
                                              ).then_inc(v_enc_ready, 1)

            def residual(i, a):
                dve.wait_ge(x_res_in[a], i * 16 + 16)
                dve.wait_ge(out_psum, i * 2 + a + 1)
                nc.vector.tensor_tensor(x_new[:, 2 * a:2 * a + 2, :], TR[:, 0:2 * D].rearrange("p (t d) -> p t d", d=D),
                                        x_res[:, 2 * a:2 * a + 2, :], ALU.add).then_inc(x_new_ready, 1)

            def round_(i, first, more):
                for s in range(STEPS):
                    mask(i, s)
                    if more and s == LN_STEP:
                        layernorm_a(i + 1)
                    if more and s == SQRT_STEP:
                        layernorm_b(i + 1)
                    if more and 0 <= s - QK_STEP < NQK:
                        split(i + 1, s - QK_STEP)
                    if s == INVERT_STEP:
                        invert(i, 0)
                    for a in range(HALVES):
                        if s == RESIDUAL_STEP[a] and not first:
                            residual(i - 1, a)
                if more:
                    dve.wait_ge(y_psum, i * STEPS + STEPS)
                    values_enc(i + 1)
                invert(i, 1)

            layernorm_a(0)
            layernorm_b(0)
            for j in range(NQK):
                split(0, j)
            dve.wait_ge(v_enc_clear, 1)
            values_enc(0)
            round_(0, True, True)
            with dve.Fori(1, ROUNDS - 1) as i:
                round_(i, False, True)
            round_(ROUNDS - 1, False, False)
            for a in range(HALVES):
                residual(ROUNDS - 1, a)

        @block.scalar
        def _(act):
            def square_root(i):
                act.wait_ge(var_ready, i + 1)
                nc.scalar.activation(std[:, :], var[:, :], ACT.Sqrt).then_inc(std_ready, 1)

            def turn(i):
                act.wait_ge(turned, i + 1)
                nc.scalar.copy(xnT[:, :], TR[:, :]).then_inc(xnT_ready, 1)

            def first_part(i, j):
                tile, bank = qk_tile(j)
                act.wait_ge(qk_psum, i * NQK + j + 1)
                nc.scalar.copy(tile(0), bank).then_inc(part1_ready, 1)

            def square(i, s):
                n = i * (2 * STEPS) + 2 * s
                for w in range(2):
                    act.wait_ge(scores_psum, n + w + 1)
                    nc.scalar.activation(att[s % 4][:, w, :], S[w][:, :], ACT.Square, bias=HEAD_SHIFT,
                                         scale=HEAD_SCALE).then_inc(squares_ready, 1)

            def copy_y(i, s):
                act.wait_ge(y_psum, i * STEPS + s + 1)
                nc.scalar.copy(yT[s // PAIRS][:, s % PAIRS, :], Y[s % 2][:, 0:N]).then_inc(y_copied, 1)

            def denominators(i, a):
                act.wait_ge(den_psum, i * 2 + a + 1)
                nc.scalar.activation(den[a][:, :], DEN[:, 0:N], ACT.Identity, bias=Z_EPS).then_inc(den_ready, 1)

            def values(i):
                for m in range(VN):
                    act.wait_ge(v_psum, i * (VN + HALVES) + HALVES + m + 1)
                    nc.scalar.copy(v[:, m // 2, 512 * (m % 2):512 * (m % 2) + 512], PR[m % 2][:, :]
                                   ).then_inc(v_ready, 1)

            def round_(i, first, more):
                for s in range(STEPS):
                    square(i, s)
                    if s >= LAG:
                        copy_y(i, s - LAG)
                    if s == PAIRS + LAG - 1:
                        denominators(i, 0)
                    if more and s == LN_STEP:
                        square_root(i + 1)
                    if more and s == TURN_STEP:
                        turn(i + 1)
                    if more and 0 <= s - QK_STEP < NQK:
                        if s == QK_STEP:
                            act.wait_ge(parts_out, i * 32 + 32)
                        first_part(i + 1, s - QK_STEP)
                for s in range(STEPS - LAG, STEPS):
                    copy_y(i, s)
                denominators(i, 1)
                if more:
                    values(i + 1)

            square_root(0)
            turn(0)
            for j in range(NQK):
                first_part(0, j)
            values(0)
            round_(0, True, True)
            with act.Fori(1, ROUNDS - 1) as i:
                round_(i, False, True)
            round_(ROUNDS - 1, False, False)

        @block.tensor
        def _(pe):
            def turn(i):
                pe.wait_ge(xn_ready, i * TILES + TILES)
                for t in range(TILES):
                    mm = nc.tensor.transpose(TR[:, P * t:P * t + P], xn[:, t, :], consts["ident"][:, :])
                mm.then_inc(turned, 1)

            def project(i, j):
                if j >= 2:
                    pe.wait_ge(parts_ready, i * NQK + j - 1)
                bank = PR[j % 2]
                if j < 2 * NCH:
                    w, c = ("wq", "wk")[j // NCH], j % NCH
                    mm = nc.tensor.matmul(bank[:, :], wT[w][:, P * c:P * c + P], xnT[:, :], start=True, stop=True)
                else:
                    enc = xnT[:, :].rearrange("d (a n) -> d a n", a=HALVES)[:, :, 0:ENC]
                    for c in range(NCH):
                        mm = nc.tensor.matmul(bank[:, P * c:P * c + P], wT["wke"][:, P * c:P * c + P], enc,
                                              start=True, stop=True)
                mm.then_inc(qk_psum, 1)

            def values_of_encoder(i):
                heads = wT["wve"][:, :].rearrange("d (g w e) -> d w g e", w=2, e=HD)
                for a in range(HALVES):
                    for w in range(2):
                        mm = nc.tensor.matmul(PR[a][ENC * w:ENC * w + ENC, :], xnT[:, N * a:N * a + ENC],
                                              heads[:, w], start=True, stop=True)
                    mm.then_inc(v_psum, 1)

            def values(i):
                for m in range(VN):
                    t, w = m // 2, m % 2
                    if t == 0:
                        pe.wait_ge(v_enc_ready, i * (2 * HALVES) + 2 * w + 2)
                    else:
                        pe.wait_ge(v_ready, i * VN + m - 1)
                    nc.tensor.matmul(PR[m % 2][:, :], xnT[:, P * t:P * t + P], wT["wv"][:, 512 * w:512 * w + 512],
                                     start=True, stop=True).then_inc(v_psum, 1)

            def scores(i, s):
                a, p = s // PAIRS, s % PAIRS
                if p == 0:
                    pe.wait_ge(stack_in[a], i * (32 * SLOTS) + 32 * SLOTS)
                for w in range(2):
                    h = 2 * p + w
                    if s >= 1:
                        pe.wait_ge(squares_ready, i * (2 * STEPS) + 2 * s + w - 1)
                    nc.tensor.matmul(S[w][:, LATE], k_stack[a][:, h, P:2 * P], q_stack[a][:, h, P:2 * P],
                                     start=True, stop=True)
                    nc.tensor.matmul(S[w][:, EARLY], k_stack[a][:, h, 0:P], q_stack[a][:, h, :],
                                     start=True, stop=True)
                    for x in range(2):
                        mm = nc.tensor.matmul(S[w][ENC * x:ENC * x + ENC, ENC_KEYS], k_stack[a][:, 2 * p + x, N:KW],
                                              q_stack[a][:, 2 * p + x, P * w:P * w + P], start=True, stop=True)
                    mm.then_inc(scores_psum, 1)

            def weighted(i, s):
                u, a, p = s % 2, s // PAIRS, s % PAIRS
                tile = att[s % 4]
                pe.wait_ge(att_ready, i * (2 * STEPS) + 2 * s + 2)
                if s == 0:
                    pe.wait_ge(v_ready, i * VN + VN)
                    pe.wait_ge(v_enc_ready, i * (2 * HALVES) + 2 * HALVES)
                if s >= 2:
                    pe.wait_ge(y_copied, i * STEPS + s - 1)
                for late in range(2):
                    for w in range(2):
                        h = 2 * p + w
                        nc.tensor.matmul(Y[u][HD * w:HD * w + HD, P * late:N], v[:, 2 * a + late, HD * h:HD * h + HD],
                                         tile[:, w, LATE if late else EARLY], start=(late == 0), stop=False,
                                         skip_group_check=True)
                nc.tensor.matmul(Y[u][:, 0:N], v_enc[:, a, p, :], tile[:, :, ENC_KEYS], start=False,
                                 stop=True, skip_group_check=True).then_inc(y_psum, 1)

            def denominators(i, s):
                a, j = s // PAIRS, s % PAIRS // 2
                for late in range(2):
                    for g in range(4):
                        tile = att[(s + g // 2) % 4]
                        nc.tensor.matmul(DEN[ROW_GROUP * g:ROW_GROUP * g + ROW_GROUP, P * late:N],
                                         consts["sum_rows"][:, j, :], tile[:, g % 2, LATE if late else EARLY],
                                         start=(j == 0 and late == 0), stop=False, skip_group_check=True)
                for g in range(4):
                    tile = att[(s + g // 2) % 4]
                    mm = nc.tensor.matmul(DEN[ROW_GROUP * g:ROW_GROUP * g + ROW_GROUP, 0:N],
                                          consts["sum_enc_rows"][:, g % 2, j, :], tile[:, :, ENC_KEYS], start=False,
                                          stop=(j == PAIRS // 2 - 1), skip_group_check=True)
                if j == PAIRS // 2 - 1:
                    mm.then_inc(den_psum, 1)

            def project_out(i, a):
                pe.wait_ge(yT_ready, (i * 2 + a) * 2 + 2)
                for t in range(2):
                    for p in range(PAIRS):
                        mm = nc.tensor.matmul(TR[:, D * t:D * t + D], yT[a][:, p, P * t:P * t + P],
                                              wT["wout"][:, D * p:D * p + D], start=(p == 0), stop=(p == PAIRS - 1))
                mm.then_inc(out_psum, 1)

            def round_(i, first, more):
                for s in range(STEPS):
                    scores(i, s)
                    if s >= LAG:
                        weighted(i, s - LAG)
                    if s >= LAG and (s - LAG) % 2:
                        denominators(i, s - LAG - 1)
                    if more and s == TURN_STEP:
                        if not first:
                            pe.wait_ge(x_new_ready, i * 2 - 1)
                        turn(i + 1)
                    if more and 0 <= s - QK_STEP < NQK:
                        if s == QK_STEP:
                            pe.wait_ge(xnT_ready, i + 2)
                        project(i + 1, s - QK_STEP)
                    for a in range(HALVES):
                        if s == OUT_STEP[a] and not first:
                            project_out(i - 1, a)
                weighted(i, STEPS - 2)
                if more:
                    pe.wait_ge(parts_ready, (i + 1) * NQK + NQK)
                    values_of_encoder(i + 1)
                weighted(i, STEPS - 1)
                denominators(i, STEPS - 2)
                if more:
                    values(i + 1)

            turn(0)
            pe.wait_ge(xnT_ready, 1)
            for j in range(NQK):
                project(0, j)
            pe.wait_ge(parts_ready, NQK)
            values_of_encoder(0)
            values(0)
            round_(0, True, True)
            with pe.Fori(1, ROUNDS - 1) as i:
                round_(i, False, True)
            round_(ROUNDS - 1, False, False)
            project_out(ROUNDS - 1, 0)
            pe.wait_ge(x_new_ready, ROUNDS * 2 - 1)
            project_out(ROUNDS - 1, 1)

        @block.gpsimd
        def _(pool):
            nc.gpsimd.memset(v_enc[:], 0.0).then_inc(v_enc_clear, 1)

            def spread_z(i, a):
                n = i * 2 + a
                pool.wait_ge(z_ready, n + 1)
                pool.sem_inc(pool_turn, 1)
                for w in range(2):
                    for odd in range(2):
                        row = ROW_GROUP * (2 * odd + w)
                        pool.dma_start(z_dram[w].rearrange("(j o) n -> j o n", o=2)[:, odd, :],
                                     z[a][row:row + PAIRS // 2, :]).then_inc(z_out, 16)
                pool.wait_ge(z_out, n * 64 + 64)
                pool.sem_inc(pool_turn, 1)
                for w in range(2):
                    pool.dma_start(z_wide[a][HD * w:HD * w + HD, :],
                                 z_dram[w].rearrange("p n -> (p n)").unsqueeze(0).broadcast_to([HD, PAIRS * N])
                                 ).then_inc(z_wide_in, 16)

            def scale(i, a):
                pool.wait_ge(z_wide_in, (i * 2 + a) * 32 + 32)
                pool.wait_ge(y_copied, i * STEPS + PAIRS * (a + 1))
                for w in range(2):
                    part = yT[a][:, PAIRS // 2 * w:PAIRS // 2 * w + PAIRS // 2, :].rearrange("p g n -> p (g n)")
                    nc.gpsimd.tensor_tensor(part, part, z_wide[a][:, PAIRS // 2 * N * w:PAIRS // 2 * N * (w + 1)],
                                            ALU.mult).then_inc(yT_ready, 1)

            with pool.Fori(0, ROUNDS) as i:
                for a in range(HALVES):
                    spread_z(i, a)
                    scale(i, a)


def make_constants(nc, consts, raw, psum, weights, stage, inputs, tokens, turn):
    with ExitStack() as ctx:
        def sem(n):
            return ctx.enter_context(nc.semaphore(f"setup_{n}"))
        pool_step = sem("pool_step")
        iota_ready = sem("iota_ready")
        masks_ready = sem("masks_ready")
        converted = sem("converted")
        wr_clear = sem("wr_clear")
        b1_in = sem("b1_in")
        b1T_psum = sem("b1T_psum")
        block = ctx.enter_context(nc.Block())

        @block.sync
        def _(sp):
            sp.dma_start(stage["b1"][:, :], inputs["b1"].rearrange("e (k p) -> (e k) p", p=P)).then_inc(b1_in, 16)
            load_tokens(sp, tokens[0], inputs["x"].rearrange("(c p) d -> p c d", p=P), tokens[1])
            sp.wait_ge(wr_clear, 1)
            sp.dma_start(weights["wr"][:, 0:E], inputs["wr"]).then_inc(weights["wr_in"], 16)
            for rows, source in turn["sources"]:
                sp.dma_start(rows, source).then_inc(turn["loaded"], 16)
            sp.dma_start(weights["w2"][:, :].rearrange("p (e k d) -> p e k d", e=E, k=HC),
                         inputs["w2"].rearrange("e (k p) d -> p e k d", p=P)).then_inc(weights["w2_in"], 16)
            sp.dma_start(weights["b2"][:, :], inputs["b2"].rearrange("e d -> (e d)").unsqueeze(0)
                         .broadcast_to([P, E * D])).then_inc(weights["b2_in"], 16)

        @block.gpsimd
        def _(pool):
            own = Steps(pool, pool_step)
            nc.gpsimd.memset(weights["wr"][:, :], 0.0).then_inc(wr_clear, 1)
            own.done(nc.gpsimd.memset(raw["ones"][:, :], 1.0))
            own.done(nc.gpsimd.iota(raw["column"][:, :], pattern=[[1, P]], base=0, channel_multiplier=0))
            own.done(nc.gpsimd.iota(raw["row"][:, :], pattern=[[0, 1]], base=0, channel_multiplier=1))
            own.done(nc.gpsimd.iota(raw["shift"][:, :], pattern=[[-1, BITS]], base=BITS - 1, channel_multiplier=0))
            own.done(nc.gpsimd.iota(raw["distance"][:, :], pattern=[[1, P]], base=P, channel_multiplier=-1))
            own.done(nc.gpsimd.memset(raw["one_i"][:, :], 1))
            own.after()
            nc.gpsimd.affine_select(out=consts["tri_f"][:, :], in_=raw["ones"][:, :], compare_op=ALU.is_ge, fill=0.0,
                                    base=0, pattern=[[1, P]], channel_multiplier=-1).then_inc(masks_ready, 1)
            nc.gpsimd.affine_select(out=consts["ident"][:, :], in_=raw["ones"][:, :], compare_op=ALU.is_equal,
                                    fill=0.0, base=0, pattern=[[1, P]], channel_multiplier=-1
                                    ).then_inc(masks_ready, 1)

        @block.vector
        def _(dve):
            own = Steps(dve, converted)
            dve.wait_ge(pool_step, 6)
            own.done(nc.vector.tensor_copy(consts["iota_f"][:, :], raw["column"][:, :]))
            own.done(nc.vector.tensor_copy(consts["part"][:, :], raw["row"][:, :]))
            own.done(nc.vector.tensor_copy(consts["ones"][:, :], raw["ones"][:, :]))
            own.done(nc.vector.tensor_tensor(consts["bits_i"][:, 0:BITS], raw["one_i"][:, :], raw["shift"][:, :],
                                             ALU.logical_shift_left))
            own.done(nc.vector.memset(consts["bits_i"][:, BITS:BITS + 1], 0))
            own.done(nc.vector.memset(consts["restart"][:, :], 1.0))
            own.done(nc.vector.tensor_scalar(raw["phase"][:, :], raw["distance"][:, :], E - 1, None, ALU.bitwise_and))
            own.after()
            own.done(nc.vector.tensor_copy(consts["bits_f"][:, :], consts["bits_i"][:, 0:BITS]))
            own.done(nc.vector.memset(consts["restart"][:, :].rearrange("p (e c) -> p e c", e=E)[:, :, 0:1], 0.0))
            own.done(nc.vector.tensor_scalar(consts["same_expert"][:, :], raw["phase"][:, :], 0.0, None,
                                             ALU.is_equal))
            G = PAIRS // 2
            own.done(nc.vector.memset(consts["sum_rows"][:, :, 0:G], 0.0))
            own.done(nc.vector.memset(consts["sum_rows"][:, :, G:ROW_GROUP], 1.0))
            own.done(nc.vector.memset(consts["sum_enc_rows"][:, :, :, :], 0.0))
            own.after()
            for j in range(G):
                own.done(nc.vector.memset(consts["sum_rows"][:, j, j:j + 1], 1.0))
            own.after()
            for w in range(2):
                half = slice(ENC * w, ENC * w + ENC)
                own.done(nc.vector.tensor_copy(consts["sum_enc_rows"][half, w, :, :], consts["sum_rows"][half, :, :]))
            dve.wait_ge(masks_ready, 2)
            for w in range(2):
                own.done(nc.vector.tensor_copy(consts["causal"][:, P * w:P * w + P], consts["tri_f"][:, :]))
            own.done(nc.vector.tensor_copy(consts["tri"][:, :], consts["tri_f"][:, :]))
            dve.wait_ge(b1T_psum, 1)
            own.done(nc.vector.tensor_copy(weights["b1"][:, :], psum[0][:, 0:E * HC]))

        @block.tensor
        def _(pe):
            pe.wait_ge(b1_in, 16)
            pe.wait_ge(masks_ready, 2)
            nc.tensor.transpose(psum[0][:, 0:E * HC], stage["b1"][:, :], consts["ident"][0:E * HC, 0:E * HC]
                                ).then_inc(b1T_psum, 1)


def build(nc, x, wq, wk, wv, wke, wve, wout, wr, w1, b1, w2, b2, out):
    with ExitStack() as ctx:
        def sb(name, shape, dt=F32):
            return ctx.enter_context(nc.sbuf_tensor(name, shape, dt))

        psum = [ctx.enter_context(nc.psum_tensor(f"bank{i}", [P, 512], F32)) for i in range(8)]
        consts = {
            "tri_f": sb("tri_f", [P, P]), "ident": sb("ident", [P, P]), "iota_f": sb("iota_f", [P, P], BF16),
            "part": sb("part", [P, 1]), "ones": sb("ones", [P, P], BF16), "bits_i": sb("bits_i", [P, BITS + 1], I32),
            "bits_f": sb("bits_f", [P, BITS]), "restart": sb("restart", [P, C * E]),
            "same_expert": sb("same_expert", [P, P], BF16), "tri": sb("tri", [P, P], BF16),
            "causal": sb("causal", [P, 2 * P]), "sum_rows": sb("sum_rows", [P, PAIRS // 2, ROW_GROUP]),
            "sum_enc_rows": sb("sum_enc_rows", [P, 2, PAIRS // 2, ROW_GROUP])}
        weights = {"wr": sb("wr", [D, ROW_GROUP]), "w1": [sb(f"w1_{u}", [D, HID]) for u in range(2)], "w1_dram": w1,
                   "w2": sb("w2", [P, E * HC * D]), "b2": sb("b2", [P, E * D]), "b1": sb("b1", [P, E * HC])}
        table = nc.dram_tensor("dispatch_table", [T, ROW], F32, kind="Internal").ap()
        q_dram = nc.dram_tensor("q_parts_dram", [3, NCH, P, RT], BF16, kind="Internal").ap()
        k_dram = nc.dram_tensor("k_parts_dram", [3, NCH, P, HALVES * KW], BF16, kind="Internal").ap()
        z_dram = nc.dram_tensor("z_dram", [2, PAIRS, N], F32, kind="Internal").ap()
        wT = {"wq": sb("wqT", [D, H * FD]), "wk": sb("wkT", [D, H * FD]), "wke": sb("wkeT", [D, H * FD]),
              "wv": sb("wvT", [D, H * HD]), "wve": sb("wveT", [D, H * HD]), "wout": sb("woutT", [P, PAIRS * D])}
        weights.update({n: ctx.enter_context(nc.semaphore(n)) for n in ("wr_in", "w2_in", "b2_in")})
        x_flat = x.rearrange("b n d -> (b n) d")
        out_flat = out.rearrange("b n d -> (b n) d")
        with ExitStack() as first:
            def raw_sb(name, shape, dt=F32):
                return first.enter_context(nc.sbuf_tensor(name, shape, dt))

            raw = {
                "ones": raw_sb("raw_ones", [P, P]), "column": raw_sb("raw_column", [P, P], I32),
                "row": raw_sb("raw_row", [P, 1], I32), "shift": raw_sb("raw_shift", [P, BITS], I32),
                "distance": raw_sb("raw_distance", [P, P], I32), "one_i": raw_sb("raw_one_i", [P, BITS], I32),
                "phase": raw_sb("raw_phase", [P, P], I32)}
            tokens = (raw_sb("first_tokens", [P, C, D]),
                      [first.enter_context(nc.semaphore(f"first_tokens_in{i}")) for i in range(4)])
            turn = {"sources": [], "blocks": [], "loaded": first.enter_context(nc.semaphore("attn_weights_in"))}
            for n, w in (("wq", wq), ("wk", wk), ("wke", wke), ("wv", wv), ("wve", wve)):
                tiles = w.shape[0] // P
                rows = raw_sb(f"{n}_rows", [P, tiles, D])
                turn["sources"].append((rows[:], w.rearrange("(c p) d -> p c d", p=P)))
                turn["blocks"] += [(rows[:, i, :], wT[n], P * i) for i in range(tiles)]
            rows = raw_sb("wout_rows", [D, H * HD])
            turn["sources"].append((rows[:, :], wout))
            turn["blocks"] += [(rows[:, P * i:P * i + P], wT["wout"], P * i) for i in range(PAIRS)]
            turn["loads"] = len(turn["sources"])
            make_constants(nc, consts, raw, psum, weights, {"b1": raw_sb("b1_rows", [E * HC, P])},
                           {"x": x_flat, "wr": wr, "w1": w1, "b1": b1, "w2": w2, "b2": b2}, tokens, turn)
            ffn_stage(nc, "ffn1", consts, weights, psum, x_flat, out_flat, table, tokens, turn)
        attention(nc, psum, consts, wT, out_flat, (q_dram, k_dram, z_dram))
        ffn_stage(nc, "ffn2", consts, weights, psum, out_flat, out_flat, table)

_INS = ['L0_attn_x', 'L0_attn_Wq', 'L0_attn_Wk', 'L0_attn_Wv', 'L0_attn_Wk_enc', 'L0_attn_Wv_enc', 'L0_attn_Wout',
        'L0_ffn_Wr', 'L0_ffn_W1', 'L0_ffn_b1', 'L0_ffn_W2', 'L0_ffn_b2']
_OUTS = [((16, 256, 128), 'float32')]


def kernel(**inputs):
    import numpy as _np
    import concourse.bacc as _bacc
    from concourse import mybir as _mybir
    from concourse.bass_utils import run_bass_kernel_spmd as _run

    nc = _bacc.Bacc("TRN2", target_bir_lowering=False, num_devices=1)
    arrays, args = {}, []
    for name in _INS:
        a = _np.ascontiguousarray(inputs[name])
        arrays[f"in_{name}_dram"] = a
        args.append(nc.dram_tensor(f"in_{name}_dram", a.shape, _mybir.dt.from_np(a.dtype), kind="ExternalInput").ap())
    for i, (shape, dtype) in enumerate(_OUTS):
        dt = _mybir.dt.from_np(_np.dtype(dtype))
        args.append(nc.dram_tensor(f"out_{i}_dram", shape, dt, kind="ExternalOutput").ap())
    build(nc, *args)
    r = _run(nc, [arrays], core_ids=[0])
    got = tuple(r.results[0][f"out_{i}_dram"] for i in range(len(_OUTS)))
    return got[0]
```

```python
from contextlib import ExitStack

import concourse.bass as bass
from concourse import mybir

F32 = mybir.dt.float32
BF16 = mybir.dt.bfloat16
F32R = mybir.dt.float32r
I32 = mybir.dt.int32
ALU = mybir.AluOpType
ACT = mybir.ActivationFunctionType
AX_X = mybir.AxisListType.X

P = 128
B, N, D = 16, 256, 128
T = B * N
C = T // P
E = 8
K = T * 2 // E
HID = 512
HC = HID // P
SL = K // P
ROW = D + E
H, FD, HD = 16, 16, 64
ENC = 64
PAIRS = H // 2
LN_EPS = 1e-5
Z_EPS = 1e-12
HEAD_SCALE = 1.0 / (2 * 4.0 ** 2) ** 0.5
HEAD_SHIFT = 0.25 / (2 * HEAD_SCALE)
HALF = 1.0 - HEAD_SHIFT ** 2
BITS = 30

DIGITS = BITS // 2
UNROLL = 5


class Steps:

    def __init__(self, engine, sem, start=0):
        self.engine, self.sem, self.n = engine, sem, start

    def done(self, instruction):
        instruction.then_inc(self.sem, 1)
        self.n = self.n + 1
        return self.n

    def after(self, value=None):
        self.engine.wait_ge(self.sem, self.n if value is None else value)



def wait_unless_first(engine, sem, value):
    if not (isinstance(value, int) and value == 0):
        engine.wait_ge(sem, value)


def load_tokens(sp, xt, src, x_in):
    for i in range(4):
        part = slice(8 * i, 8 * i + 8)
        sp.dma_start(xt[:, part, :], src[:, part, :]).then_inc(x_in[i], 16)


def ffn_stage(nc, name, consts, weights, psum, x_acc, table, xt, x_in, rows=None, turn=None):
    acc = x_acc.rearrange("(c p) d -> p c d", p=P)
    QT = 4
    ident = consts["ident"]

    with ExitStack() as ctx:
        def sem(n):
            return ctx.enter_context(nc.semaphore(f"{name}_{n}"))

        def sb(n, shape, dt=F32):
            return ctx.enter_context(nc.sbuf_tensor(f"{name}_{n}", shape, dt))

        flat = C * E

        def by_pool(c):
            return c % QT == QT - 1 and c < 3 * C // 4

        buf = {
            "rstd": sb("rstd", [P, C]), "unused": sb("unused", [P, 2]), "std": sb("std", [P, C]),
            "tmp32": sb("tmp32", [P, 4, C]), "logitsT": sb("logitsT", [P, 2, 512]), "scores": sb("scores", [P, flat]),
            "work": sb("work", [P, 4, flat]), "sT": sb("sT", [P, flat]), "thr": sb("thr", [P, 1], I32),
            "cand": sb("cand", [P, 3], I32), "terms": sb("terms", [P, 3], I32), "low": sb("low", [P, 1], I32),
            "cmp": sb("cmp", [P, 3, flat]),
            "count": sb("count", [P, 3], BF16), "thr_wide": sb("thr_wide", [P, P]), "thr_row": sb("thr_row", [P, E]),
            "gt": sb("gt", [P, flat], BF16), "eq": sb("eq", [P, flat], BF16), "sel": sb("sel", [P, flat], BF16),
            "before": sb("before", [P, flat], BF16), "need": sb("need", [P, E]), "need2": sb("need2", [P, E]),
            "need3": sb("need3", [P, E]), "slot_i": sb("slot_i", [P, flat], I32), "hi_i": sb("hi_i", [P, flat], I32),
            "lo_i": sb("lo_i", [P, flat], I32), "hi": sb("hi", [P, flat], BF16), "lo": sb("lo", [P, flat], BF16),
            "hi_hot": sb("hi_hot", [P, C, P], BF16), "lo_hot": sb("lo_hot", [P, C, SL], BF16),
            "lo_val": sb("lo_val", [P, C, 2 * SL], BF16), "list": sb("list", [P, 2 * SL]),
            "idx": sb("idx", [P, E * SL], I32), "gather_idx": [sb(f"gather_idx{u}", [P, SL], I32) for u in range(2)],
            "scatter_idx": [sb(f"scatter_idx{u}", [P, SL], I32) for u in range(2)],
            "tok": [sb(f"tok{u}", [P, SL, ROW]) for u in range(2)], "tokT": sb("tokT", [D, K]),
            "hidden": sb("hidden", [P, HC, K]), "yb": sb("yb", [P, SL, D]), "gate": [sb(f"gate{u}", [P, SL]) for u in range(2)],
            "y": [sb(f"y{u}", [P, SL, D]) for u in range(2)]}
        scores, xnT = buf["scores"], buf["hidden"][:, :, :].rearrange("p k t -> p (k t)")
        rstd, tmp32 = buf["rstd"], buf["tmp32"]
        buf["rows"] = rows or sb("rows", [P, C, ROW])
        if x_in:
            residual_out, var_ready, std_ready = sem("residual_out"), sem("var_ready"), sem("std_ready")
            xn_ready, xn_pool_ready, rstd_ready = sem("xn_ready"), sem("xn_pool_ready"), sem("rstd_ready")
            stats, mv = sb("stats", [P, C, 6]), sb("mv", [P, C, 2])
        table_out = sem("table_out")
        logitsT_psum = sem("logitsT_psum")
        logitsT_ready = sem("logitsT_ready")
        xnT_psum = sem("xnT_psum")
        xnT_ready = sem("xnT_ready")
        logits_ready = sem("logits_ready")
        shifted_ready = sem("shifted_ready")
        exp_ready = sem("exp_ready")
        scores_ready = sem("scores_ready")
        scoresT_psum = sem("scoresT_psum")
        counts_ready = sem("counts_ready")
        total_ready = sem("total_ready")
        thr_ready = sem("thr_ready")
        thrT_ready = sem("thrT_ready")
        gt_ready = sem("gt_ready")
        gt_count = sem("gt_count")
        eq_ready = sem("eq_ready")
        eq_rank = sem("eq_rank")
        sel_ready = sem("sel_ready")
        sel_rank = sem("sel_rank")
        dve_step = sem("dve_step")
        onehot_ready = sem("onehot_ready")
        list_ready = sem("list_ready")
        idx_ready = sem("idx_ready")
        w1_in = [sem("w1_in0"), sem("w1_in1")]
        gathered = [[sem(f"gathered{u}{half}") for half in range(2)] for u in range(2)]
        gather_idx_ready = sem("gather_idx_ready")
        scatter_idx_ready = sem("scatter_idx_ready")
        gate_ready = sem("gate_ready")
        act_turn = sem("act_turn")
        pool_turn = sem("pool_turn")
        tokT_psum = sem("tokT_psum")
        tokT_ready = sem("tokT_ready")
        hidden_psum = sem("hidden_psum")
        hidden_ready = sem("hidden_ready")
        y_psum = sem("y_psum")
        y_biased = sem("y_biased")
        y_ready = sem("y_ready")
        scattered = sem("scattered")
        if turn:
            weights_turned, weights_ready, split_step = sem("weights_turned"), sem("weights_ready"), sem("split_step")
        block = ctx.enter_context(nc.Block())

        logitsT = psum[2:4]
        logits = [bank[:, :].rearrange("p (q g r) -> p g q r", q=4, g=4)[:, :, :, 0:E] for bank in (psum[7], psum[4])]
        scoresT = psum[6][:, 0:2 * P]
        total = psum[5][:, 0:3]
        thr_psum = psum[5][:, 0:P]
        rank_psum = psum[4][:, 0:C * E]
        list_psum = psum[7][:, 0:2 * SL]
        hidden_bank = [psum[2], psum[3], psum[6]]

        @block.sync
        def _(sp):
            def load_w1(e, u):
                sp.dma_start(weights["w1"][u][:, :], weights["w1_dram"][bass.ds(e, 1), :, :]
                             .rearrange("e d h -> d (e h)")).then_inc(w1_in[u], 16)

            for u in range(2):
                load_w1(u, u)
            if x_in:
                for i in range(4):
                    sp.wait_ge(x_in[i], 16)
                sp.dma_start(acc, xt[:]).then_inc(residual_out, 16)
                sp.wait_ge(residual_out, 16)
            sp.wait_ge(scores_ready, 2)
            sp.dma_start(table.rearrange("(c p) r -> p c r", p=P), buf["rows"][:]).then_inc(table_out, 16)
            sp.wait_ge(table_out, 16)
            with sp.Fori(0, E // 2 - 1) as g:
                for u in range(2):
                    sp.wait_ge(hidden_psum, (g * 2 + u) * (2 * HC) + 2 * HC)
                    load_w1(g * 2 + (2 + u), u)

        @block.vector
        def _(dve):
            own = Steps(dve, dve_step)
            rows = buf["rows"]
            if x_in:
                for i in range(4):
                    dve.wait_ge(x_in[i], 16)
                    for c in range(8 * i, 8 * i + 8):
                        last = own.done(nc.vector.bn_stats(stats[:, c, :], xt[:, c, :]))
                own.after(last)
                for c in range(C):
                    last = own.done(nc.vector.bn_aggr(mv[:, c, :], stats[:, c, :]))
                own.after(last)
                var = mv[:, :, 1]
                own.done(nc.vector.tensor_scalar(tmp32[:, 0, :], var, LN_EPS, None, ALU.add))
                own.after()
                nc.vector.tensor_copy(tmp32[:, 1, :], tmp32[:, 0, :]).then_inc(var_ready, 1)
                dve.wait_ge(std_ready, 1)
                own.done(nc.vector.reciprocal(tmp32[:, 2, :], buf["std"][:, :]))
                own.after()
                own.done(nc.vector.tensor_tensor(tmp32[:, 3, :], tmp32[:, 0, :], tmp32[:, 2, :], ALU.mult))
                own.after()
                own.done(nc.vector.tensor_tensor(tmp32[:, 2, :], tmp32[:, 3, :], buf["std"][:, :], ALU.add))
                own.after()
                own.done(nc.vector.tensor_scalar(tmp32[:, 3, :], tmp32[:, 2, :], 0.5, None, ALU.mult))
                own.after()
                nc.vector.reciprocal(rstd[:, :], tmp32[:, 3, :]).then_inc(rstd_ready, 1)
                dve.wait_ge(rstd_ready, 1)
                for c in range(C):
                    if not by_pool(c):
                        nc.vector.tensor_scalar(rows[:, c, 0:D], xt[:, c, :], mv[:, c, 0:1], rstd[:, c:c + 1],
                                                ALU.subtract, ALU.mult).then_inc(xn_ready, 1)
            work = buf["work"]
            w3 = [work[:, i, :].rearrange("p (c e) -> p c e", e=E) for i in range(4)]
            for half in range(2):
                dve.wait_ge(logits_ready, half + 1)
                tiles = slice(C // 2 * half, C // 2 * half + C // 2)
                highest = tmp32[:, 0, tiles].rearrange("p (g q) -> p g q", g=4)
                own.done(nc.vector.tensor_reduce(highest, logits[half], AX_X, ALU.max))
                own.after()
                nc.vector.tensor_tensor(w3[0][:, tiles, :].rearrange("p (g q) e -> p g q e", g=4), logits[half],
                                        highest.unsqueeze(3).broadcast_to([P, 4, 4, E]),
                                        ALU.subtract).then_inc(shifted_ready, 1)
            dve.wait_ge(exp_ready, 2)
            own.done(nc.vector.tensor_reduce(tmp32[:, 1, :], w3[1], AX_X, ALU.add))
            own.after()
            own.done(nc.vector.reciprocal(tmp32[:, 2, :], tmp32[:, 1, :]))
            own.after()
            inv = tmp32[:, 2, :].unsqueeze(2).broadcast_to([P, C, E])
            s3 = scores[:, :].rearrange("p (c e) -> p c e", e=E)
            nc.vector.tensor_tensor(s3, w3[1], inv, ALU.mult).then_inc(scores_ready, 1)
            nc.vector.tensor_tensor(rows[:, :, D:ROW], w3[1], inv, ALU.mult).then_inc(scores_ready, 1)
            sT = buf["sT"]
            thr, cand, terms, low = buf["thr"], buf["cand"], buf["terms"], buf["low"]
            own.done(nc.vector.memset(thr[:, :], 0))
            own.done(nc.vector.memset(low[:, :], 0))
            own.done(nc.vector.memset(terms[:, :], 0))
            own.done(nc.vector.tensor_copy(cand[:, :], consts["digits"][:, 0, :]))
            dve.wait_ge(scoresT_psum, 1)
            own.done(nc.vector.tensor_copy(sT[:, :], scoresT))
            own.after()
            start = own.n
            PER_DIGIT = 4
            with dve.Fori(0, DIGITS // UNROLL) as r:
                for b in range(UNROLL):
                    i = r * UNROLL + b
                    digit = Steps(dve, dve_step, i * PER_DIGIT + start)
                    for j in range(3):
                        nc.vector.tensor_scalar(buf["cmp"][:, j, :], sT[:, :], cand[:, j:j + 1].bitcast(F32), 0.0,
                                                ALU.is_ge, ALU.add, accum_out=buf["count"][:, j:j + 1]
                                                ).then_inc(counts_ready, 1)
                    digit.done(nc.vector.tensor_tensor(thr[:, :], low[:, :], terms[:, 2:3], ALU.bitwise_xor))
                    digit.after()
                    dve.wait_ge(total_ready, i + 1)
                    digit.done(nc.vector.scalar_tensor_tensor(
                        terms[:, :], total, float(K), consts["digit_terms"][:, bass.ds(i, 1), :]
                        .rearrange("p o j -> p (o j)"), ALU.is_ge, ALU.mult))
                    digit.after()
                    digit.done(nc.vector.scalar_tensor_tensor(low[:, :], terms[:, 0:1], terms[:, 1:2], thr[:, :],
                                                              ALU.bitwise_xor, ALU.bitwise_xor))
                    digit.after()
                    digit.done(nc.vector.scalar_tensor_tensor(
                        cand[:, :], consts["digits"][:, bass.ds(i + 1, 1), :].rearrange("p o j -> p (o j)"),
                        terms[:, 2:3], low[:, :].broadcast_to([P, 3]), ALU.bitwise_xor, ALU.bitwise_xor))
                    digit.after()
            own = Steps(dve, dve_step, start + DIGITS * PER_DIGIT)
            own.after()
            thr = cand[:, 0:1].bitcast(F32)
            nc.vector.tensor_copy(buf["thr_wide"][:, :], thr.broadcast_to([P, P])).then_inc(thr_ready, 1)
            dve.wait_ge(thrT_ready, 1)
            own.done(nc.vector.tensor_copy(buf["thr_row"][:, :], thr_psum[:, 0:E]))
            own.after()
            s_ec = scores[:, :].rearrange("p (c e) -> p e c", e=E)
            thr_ec = buf["thr_row"][:, :].unsqueeze(2).broadcast_to([P, E, C])

            def ec(t):
                return t[:, :].rearrange("p (e c) -> p e c", e=E)

            nc.vector.tensor_tensor(ec(buf["gt"]), s_ec, thr_ec, ALU.is_gt).then_inc(gt_ready, 1)
            own.done(nc.vector.tensor_tensor(ec(buf["eq"]), s_ec, thr_ec, ALU.is_equal))
            own.after()

            def ec_psum(t):
                return t.rearrange("p (e c) -> p e c", e=E)

            def earlier_tiles(mask):
                own.done(nc.vector.tensor_tensor_scan(work[:, 0, :], consts["restart"][:, :], mask[:, :], 0.0,
                                                      ALU.mult, ALU.add))
                own.after()
                return nc.vector.tensor_tensor(buf["before"][:, :], work[:, 0, :], mask[:, :], ALU.subtract)

            earlier_tiles(buf["eq"]).then_inc(eq_ready, 1)
            dve.wait_ge(gt_count, 1)
            own.done(nc.vector.tensor_reduce(buf["need"][:, :], ec_psum(rank_psum), AX_X, ALU.add))
            own.after()
            own.done(nc.vector.tensor_scalar(buf["need2"][:, :], buf["need"][:, :], -1.0, float(K), ALU.mult, ALU.add))
            own.after()
            nc.vector.tensor_copy(buf["need3"][:, :], buf["need2"][:, :]).then_inc(eq_ready, 1)
            dve.wait_ge(eq_rank, 1)
            own.done(nc.vector.tensor_tensor(work[:, 1, :].rearrange("p (e c) -> p e c", e=E), ec_psum(rank_psum),
                                             buf["need2"][:, :].unsqueeze(2).broadcast_to([P, E, C]), ALU.is_le))
            own.after()
            own.done(nc.vector.tensor_tensor(work[:, 2, :], work[:, 1, :], buf["eq"][:, :], ALU.mult))
            own.after()
            own.done(nc.vector.tensor_tensor(buf["sel"][:, :], work[:, 2, :], buf["gt"][:, :], ALU.add))
            own.after()
            earlier_tiles(buf["sel"]).then_inc(sel_ready, 1)
            dve.wait_ge(sel_rank, 1)
            own.done(nc.vector.tensor_tensor(work[:, 1, :], rank_psum, buf["sel"][:, :], ALU.mult))
            own.after()
            own.done(nc.vector.tensor_scalar(buf["slot_i"][:, :], work[:, 1, :], -1.0, None, ALU.add))
            own.after()
            own.done(nc.vector.tensor_scalar(buf["hi_i"][:, :], buf["slot_i"][:, :], 3, None, ALU.arith_shift_right))
            own.done(nc.vector.tensor_scalar(buf["lo_i"][:, :], buf["slot_i"][:, :], SL - 1, None, ALU.bitwise_and))
            own.after()
            own.done(nc.vector.tensor_copy(buf["hi"][:, :], buf["hi_i"][:, :]))
            own.done(nc.vector.tensor_copy(buf["lo"][:, :], buf["lo_i"][:, :]))
            own.after()
            start = own.n
            PER_LIST = 2

            def build_list(e):
                own = Steps(dve, dve_step, e * PER_LIST + start)
                hi = buf["hi"][:, bass.ds(e * C, C)].unsqueeze(2).broadcast_to([P, C, P])
                lo = buf["lo"][:, bass.ds(e * C, C)].unsqueeze(2).broadcast_to([P, C, SL])
                own.done(nc.vector.tensor_tensor(buf["lo_hot"][:, :, :], consts["iota_f"][:, 0:SL].unsqueeze(1)
                                                 .broadcast_to([P, C, SL]), lo, ALU.is_equal))
                nc.vector.tensor_tensor(buf["hi_hot"][:, :, :], consts["iota_f"][:, :].unsqueeze(1)
                                        .broadcast_to([P, C, P]), hi, ALU.is_equal).then_inc(onehot_ready, 1)
                own.after()
                nc.vector.tensor_scalar(buf["lo_val"][:, :, 0:SL], buf["lo_hot"][:, :, :], consts["part"][:, 0:1],
                                        None, ALU.mult).then_inc(onehot_ready, 1)
                nc.vector.tensor_tensor(buf["lo_val"][:, :, SL:2 * SL], buf["lo_hot"][:, :, :],
                                        consts["iota_f"][:, 0:C].unsqueeze(2).broadcast_to([P, C, SL]),
                                        ALU.mult).then_inc(onehot_ready, 1)
                dve.wait_ge(list_ready, e + 1)
                own.done(nc.vector.tensor_copy(buf["list"][:, :], list_psum))
                own.after()
                nc.vector.scalar_tensor_tensor(buf["idx"][:, bass.ds(e * SL, SL)], buf["list"][:, SL:2 * SL], float(P),
                                               buf["list"][:, 0:SL], ALU.mult, ALU.add).then_inc(idx_ready, 1)

            def take_tokens(e, u):
                for half in range(2):
                    dve.wait_ge(tokT_psum, e * 2 + half + 1)
                    nc.vector.tensor_copy(buf["tokT"][:, 512 * half:512 * half + 512],
                                          psum[half][:, :]).then_inc(tokT_ready, 1)
                if not isinstance(e, int) or e >= 2:
                    dve.wait_ge(y_ready, e * 2 - 2)
                nc.vector.tensor_scalar(buf["gate"][u][:, :], buf["tok"][u][:, :, bass.ds(e + D, 1)]
                                        .rearrange("p j o -> p (j o)"), 0.5, None, ALU.mult).then_inc(gate_ready, 1)

            def expert(e, u, lists, takes):
                if lists:
                    build_list(e + lists)
                if takes:
                    take_tokens(e + 1, 1 - u)
                for half in range(2):
                    slots = slice(4 * half, 4 * half + 4)
                    dve.wait_ge(y_psum, e * 2 + half + 1)
                    y4 = psum[4 + half][:, :].rearrange("p (j d) -> p j d", d=D)
                    bias = weights["b2"][:, bass.ds(e * D, D)].unsqueeze(1).broadcast_to([P, 4, D])
                    nc.vector.tensor_tensor(buf["yb"][:, slots, :], y4, bias, ALU.add).then_inc(y_biased, 1)
                    dve.wait_ge(y_biased, e * 2 + half + 1)
                    if half == 0:
                        if not isinstance(e, int) or e >= 2:
                            dve.wait_ge(scattered, (e - 1) * (16 * SL))
                        dve.wait_ge(gate_ready, e + 1)
                    gate = buf["gate"][u][:, slots].unsqueeze(2).broadcast_to([P, 4, D])
                    nc.vector.tensor_tensor(buf["y"][u][:, slots, :], buf["yb"][:, slots, :], gate,
                                            ALU.mult).then_inc(y_ready, 1)

            build_list(0)
            build_list(1)
            build_list(2)
            take_tokens(0, 0)
            own_split = Steps(dve, split_step) if turn else None

            def split_weights(names):
                for n in names:
                    whole, (high, low) = turn["whole"][n], turn["parts"][n]
                    own_split.done(nc.vector.tensor_copy(high[:, :], whole[:, :]))
                    own_split.after()
                    own_split.done(nc.vector.tensor_tensor(low[:, :], whole[:, :], high[:, :].bitcast(F32), ALU.subtract))

            dve.wait_ge(weights["b2_in"], 16)
            expert(0, 0, 3, True)
            if turn:
                split_weights(("wq", "wk", "wke"))
            expert(1, 1, None, True)
            if turn:
                split_weights(("wv",))
            with dve.Fori(1, E // 2 - 1) as g:
                expert(g * 2, 0, 2, True)
                expert(g * 2 + 1, 1, 2, True)
            expert(E - 2, 0, None, True)
            expert(E - 1, 1, None, False)

        @block.scalar
        def _(act):
            if x_in:
                act.wait_ge(var_ready, 1)
                nc.scalar.activation(buf["std"][:, :], tmp32[:, 1, :], ACT.Sqrt).then_inc(std_ready, 1)
            nc.scalar.activation(buf["unused"][:, 0:1], ident[:, 0:1], ACT.Exp).then_inc(act_turn, 1)
            for i in range(C // QT):
                act.wait_ge(xnT_psum, i + 1)
                nc.scalar.copy(xnT[:, 512 * i:512 * i + 512], psum[i % 2][:, :]).then_inc(xnT_ready, 1)
                if i % 4 == 3:
                    act.wait_ge(logitsT_psum, i // 4 + 1)
                    nc.scalar.copy(buf["logitsT"][:, i // 4, :], logitsT[i // 4][:, :]).then_inc(logitsT_ready, 1)
            for half in range(2):
                act.wait_ge(shifted_ready, half + 1)
                columns = slice(flat // 2 * half, flat // 2 * half + flat // 2)
                nc.scalar.activation(buf["work"][:, 1, columns], buf["work"][:, 0, columns], ACT.Exp
                                     ).then_inc(exp_ready, 1)
            act.wait_ge(act_turn, 1)
            nc.scalar.activation(buf["unused"][:, 1:2], buf["unused"][:, 0:1], ACT.Gelu).then_inc(act_turn, 1)

            if turn:
                for i, (_, destination, column) in enumerate(turn["blocks"]):
                    if i % 2 == 0:
                        act.wait_ge(weights_turned, i // 2 + 1)
                        nc.scalar.copy(destination[:, column:column + 2 * P], psum[i // 2 % 4][:, 0:2 * P]
                                       ).then_inc(weights_ready, 1)

            def expert(e):
                for n in range(2 * HC):
                    half, k = n // HC, n % HC
                    act.wait_ge(hidden_psum, e * (2 * HC) + (n + 1))
                    act.sem_inc(act_turn, 1)
                    nc.scalar.activation(buf["hidden"][:, k, 512 * half:512 * half + 512], hidden_bank[n % 3][:, :],
                                         ACT.Gelu, bias=weights["b1"][:, bass.ds(e * HC + k, 1)]
                                         ).then_inc(hidden_ready, 1)

            expert(0)
            with act.Fori(1, E) as e:
                expert(e)

        @block.tensor
        def _(pe):
            def route(half):
                pe.wait_ge(xnT_ready, 4 * half + 4)
                for g in range(4):
                    i = 4 * half + g
                    mm = nc.tensor.matmul(logitsT[half][32 * g:32 * g + 32, :], weights["wr"][:, :],
                                          xnT[:, 512 * i:512 * i + 512], start=True, stop=True)
                mm.then_inc(logitsT_psum, 1)

            def turn_logits(half):
                pe.wait_ge(logitsT_ready, half + 1)
                bank = (psum[7], psum[4])[half]
                for q in range(4):
                    mm = nc.tensor.transpose(bank[:, P * q:P * q + P], buf["logitsT"][:, half, P * q:P * q + P],
                                             ident[:, :])
                mm.then_inc(logits_ready, 1)

            pe.wait_ge(weights["wr_in"], 16)
            for i in range(C // QT):
                if i >= 2:
                    pe.wait_ge(xnT_ready, i - 1)
                for q in range(QT):
                    c = QT * i + q
                    before = sum(by_pool(n) for n in range(c))
                    if x_in and by_pool(c):
                        pe.wait_ge(xn_pool_ready, before + 1)
                    elif x_in:
                        pe.wait_ge(xn_ready, c - before + 1)
                    mm = nc.tensor.transpose(psum[i % 2][:, P * q:P * q + P], buf["rows"][:, QT * i + q, 0:D],
                                             ident[:, :])
                mm.then_inc(xnT_psum, 1)
                if i == 4:
                    route(0)
                if i == 6:
                    turn_logits(0)
            route(1)
            turn_logits(1)
            pe.wait_ge(scores_ready, 1)
            for half in range(2):
                mm = nc.tensor.transpose(scoresT[:, P * half:P * half + P], scores[:, P * half:P * half + P],
                                         ident[:, :])
            mm.then_inc(scoresT_psum, 1)
            with pe.Fori(0, DIGITS // UNROLL) as r:
                for b in range(UNROLL):
                    pe.wait_ge(counts_ready, (r * UNROLL + b) * 3 + 3)
                    nc.tensor.matmul(total, consts["same_expert"][:, :], buf["count"][:, :], start=True,
                                     stop=True).then_inc(total_ready, 1)
            pe.wait_ge(thr_ready, 1)
            nc.tensor.transpose(thr_psum, buf["thr_wide"][:, :], ident[:, :]).then_inc(thrT_ready, 1)
            pe.wait_ge(gt_ready, 1)
            nc.tensor.matmul(rank_psum, consts["ones"][:, :], buf["gt"][:, :], start=True,
                             stop=True).then_inc(gt_count, 1)
            pe.wait_ge(eq_ready, 2)
            nc.tensor.matmul(rank_psum, consts["tri"][:, :], buf["eq"][:, :], start=True, stop=False)
            nc.tensor.matmul(rank_psum, consts["ones"][:, :], buf["before"][:, :], start=False,
                             stop=True).then_inc(eq_rank, 1)
            pe.wait_ge(sel_ready, 1)
            nc.tensor.matmul(rank_psum, consts["tri"][:, :], buf["sel"][:, :], start=True, stop=False)
            nc.tensor.matmul(rank_psum, consts["ones"][:, :], buf["before"][:, :], start=False,
                             stop=True).then_inc(sel_rank, 1)

            def token_list(e):
                pe.wait_ge(onehot_ready, e * 3 + 3)
                for c in range(C):
                    mm = nc.tensor.matmul(list_psum, buf["hi_hot"][:, c, :], buf["lo_val"][:, c, :],
                                          start=(c == 0), stop=(c == C - 1))
                mm.then_inc(list_ready, 1)

            def turn_tokens(e, u):
                for half in range(2):
                    pe.wait_ge(gathered[u][half], (e - u) * (4 * SL) + 8 * SL)
                    for q in range(4):
                        mm = nc.tensor.transpose(psum[half][:, P * q:P * q + P], buf["tok"][u][:, 4 * half + q, 0:D],
                                                 ident[:, :])
                    mm.then_inc(tokT_psum, 1)

            def expert(e, u, lists, turns):
                pe.wait_ge(w1_in[u], (e - u) * 8 + 16)
                for n in range(2 * HC):
                    half, k = n // HC, n % HC
                    if k == 0:
                        pe.wait_ge(tokT_ready, e * 2 + half + 1)
                    if n >= 3:
                        pe.wait_ge(hidden_ready, e * (2 * HC) + (n - 2))
                    nc.tensor.matmul(hidden_bank[n % 3][:, :], weights["w1"][u][:, P * k:P * k + P],
                                     buf["tokT"][:, 512 * half:512 * half + 512], start=True,
                                     stop=True).then_inc(hidden_psum, 1)
                if lists:
                    token_list(e + lists)
                if turns:
                    turn_tokens(e + 1, 1 - u)
                wait_unless_first(pe, y_biased, e * 2)
                for half in range(2):
                    pe.wait_ge(hidden_ready, e * (2 * HC) + HC * (half + 1))
                    for q in range(4):
                        for k in range(HC):
                            mm = nc.tensor.matmul(psum[4 + half][:, P * q:P * q + P],
                                                  buf["hidden"][:, k, 512 * half + P * q:512 * half + P * q + P],
                                                  weights["w2"][:, bass.ds(e * HID + k * P, P)],
                                                  start=(k == 0), stop=(k == HC - 1))
                    mm.then_inc(y_psum, 1)

            def turn_weights(first, last):
                for i, (source, _, _) in enumerate(turn["blocks"]):
                    if first <= i < last:
                        if i >= 8 and i % 2 == 0:
                            pe.wait_ge(weights_ready, i // 2 - 3)
                        mm = nc.tensor.transpose(psum[i // 2 % 4][:, P * (i % 2):P * (i % 2) + P], source, ident[:, :])
                        if i % 2:
                            mm.then_inc(weights_turned, 1)

            if turn:
                pe.wait_ge(turn["loaded"], turn["loads"] * 16)
                turn_weights(0, 8)
            token_list(0)
            if turn:
                turn_weights(8, 24)
            token_list(1)
            if turn:
                turn_weights(24, len(turn["blocks"]))
                pe.wait_ge(weights_ready, len(turn["blocks"]) // 2)
            token_list(2)
            turn_tokens(0, 0)
            pe.wait_ge(weights["w2_in"], 16)
            expert(0, 0, 3, True)
            expert(1, 1, None, True)
            with pe.Fori(1, E // 2 - 1) as g:
                expert(g * 2, 0, 2, True)
                expert(g * 2 + 1, 1, 2, True)
            expert(E - 2, 0, None, True)
            expert(E - 1, 1, None, False)

        @block.gpsimd
        def _(pool):
            if x_in:
                pool.wait_ge(rstd_ready, 1)
            for c in range(C):
                if x_in and by_pool(c):
                    nc.gpsimd.tensor_scalar(buf["rows"][:, c, 0:D], xt[:, c, :], mv[:, c, 0:1], rstd[:, c:c + 1],
                                            ALU.subtract, ALU.mult).then_inc(xn_pool_ready, 1)
            pool.wait_ge(table_out, 16)
            if x_in:
                pool.wait_ge(residual_out, 16)

            def gather(e, u):
                pool.wait_ge(idx_ready, e + 1)
                if not isinstance(e, int) or e >= 2:
                    pool.wait_ge(gate_ready, e - 1)
                nc.gpsimd.tensor_copy(buf["gather_idx"][u][:, :], buf["idx"][:, bass.ds(e * SL, SL)]
                                      ).then_inc(gather_idx_ready, 1)
                pool.wait_ge(gather_idx_ready, e + 1)
                pool.sem_inc(pool_turn, 1)
                for j in range(SL):
                    nc.gpsimd.indirect_dma_start(
                        out=buf["tok"][u][:, j, :], out_offset=None, in_=table,
                        in_offset=bass.IndirectOffsetOnAxis(ap=buf["gather_idx"][u][:, j:j + 1], axis=0)
                    ).then_inc(gathered[u][2 * j // SL], 16)

            def expert(e, u, gathers):
                if gathers:
                    gather(e + 2, u)
                nc.gpsimd.tensor_copy(buf["scatter_idx"][u][:, :], buf["idx"][:, bass.ds(e * SL, SL)]
                                      ).then_inc(scatter_idx_ready, 1)
                pool.wait_ge(scatter_idx_ready, e + 1)
                wait_unless_first(pool, scattered, e * (16 * SL))
                for half in range(2):
                    pool.wait_ge(y_ready, e * 2 + half + 1)
                    pool.sem_inc(pool_turn, 1)
                    for j in range(4 * half, 4 * half + 4):
                        nc.gpsimd.indirect_dma_start(
                            out=x_acc, out_offset=bass.IndirectOffsetOnAxis(ap=buf["scatter_idx"][u][:, j:j + 1], axis=0),
                            in_=buf["y"][u][:, j, :], in_offset=None, compute_op=ALU.add).then_inc(scattered, 16)

            gather(0, 0)
            gather(1, 1)
            expert(0, 0, True)
            expert(1, 1, True)
            with pool.Fori(1, E // 2 - 1) as g:
                expert(g * 2, 0, True)
                expert(g * 2 + 1, 1, True)
            expert(E - 2, 0, False)
            expert(E - 1, 1, False)
            pool.wait_ge(scattered, E * 16 * SL)



Q_PART = [0, 0, 1, 1, 0, 2, 1, 2]
K_PART = [0, 1, 0, 1, 2, 0, 2, 1]
SLOTS = len(Q_PART)
HALVES = 2
ROUNDS = B // HALVES
RT = HALVES * N
TILES = RT // P
KW = N + ENC
ROW_GROUP = 32
NCH = H * FD // P
STEPS = HALVES * PAIRS
LN_STEP, TURN_STEP, QK_STEP = 0, 2, 3
LAG = 2
INVERT_STEP = PAIRS + 2
SCALE_STEP = 3
OUT_STEP, RESIDUAL_STEP = (0, 7), (2, 8)


PART_PAIRS = [(0, 0), (0, 1), (1, 0)]


def attention(nc, psum, consts, wT, parts, x, rows, scratch):
    with ExitStack() as ctx:
        def sem(n):
            return ctx.enter_context(nc.semaphore(f"attn_{n}"))

        def sb(n, shape, dt=F32):
            return ctx.enter_context(nc.sbuf_tensor(f"attn_{n}", shape, dt))

        x_ln, xn, x_res = sb("x_ln", [P, TILES, D]), sb("xn", [P, TILES, D]), sb("x_res", [P, TILES, D])
        xnT = [sb(f"xnT_{part}", [D, RT], F32R) for part in ("high", "low")]
        xnT_enc = sb("xnT_enc", [D, HALVES, ENC])
        x_new = [sb(f"x_new{a}", [P, 2, D]) for a in range(HALVES)]
        new_stats, new_mv = sb("new_stats", [P, 2, 6]), sb("new_mv", [P, 2, 2])
        new_var, new_std, new_tmp = sb("new_var", [P, 2]), sb("new_std", [P, 2]), sb("new_tmp", [P, 4, 2])
        stats, mv = sb("stats", [P, TILES, 6]), sb("mv", [P, TILES, 2])
        var, std = sb("var", [P, TILES]), sb("std", [P, TILES])
        ln_tmp, rstd = sb("ln_tmp", [P, 3, TILES]), sb("rstd", [P, TILES])
        q_parts = sb("q_parts", [P, 3, NCH, RT], BF16)
        k_parts = sb("k_parts", [P, 3, NCH, HALVES, KW], BF16)
        rest = [sb(f"rest{u}", [P, RT]) for u in range(2)]
        q_stack = [sb(f"q_stack{a}", [P, H, N], BF16) for a in range(HALVES)]
        k_stack = [sb(f"k_stack{a}", [P, H, KW], BF16) for a in range(HALVES)]
        v = sb("v", [P, TILES, H * HD])
        v_enc = sb("v_enc", [P, HALVES, PAIRS, P])
        att = [sb(f"att{u}", [P, 2, 4 * P]) for u in range(4)]
        sums = [sb(f"sums{u}", [P, 2, P]) for u in range(4)]
        den, z = ([sb(f"{n}{a}", [P, N]) for a in range(HALVES)] for n in ("den", "z"))
        z_wide = sb("z_wide", [P, PAIRS * N])
        yT = [sb(f"yT{a}", [P, PAIRS, N]) for a in range(HALVES)]
        q_dram, k_dram, z_dram = scratch

        x_ln_in = sem("x_ln_in")
        x_res_in = [sem(f"x_res_in{a}") for a in range(HALVES)]
        var_ready = sem("var_ready")
        std_ready = sem("std_ready")
        xn_ready = sem("xn_ready")
        turned = sem("turned")
        xnT_ready = sem("xnT_ready")
        qk_psum = sem("qk_psum")
        part1_ready = sem("part1_ready")
        parts_ready = sem("parts_ready")
        parts_out = sem("parts_out")
        stack_in = [sem(f"stack_in{a}") for a in range(HALVES)]
        v_psum = sem("v_psum")
        v_ready = sem("v_ready")
        v_enc_ready = sem("v_enc_ready")
        scores_psum = sem("scores_psum")
        squares_ready = sem("squares_ready")
        att_ready = sem("att_ready")
        y_psum = sem("y_psum")
        y_copied = sem("y_copied")
        den_psum = sem("den_psum")
        den_ready = sem("den_ready")
        z_ready = sem("z_ready")
        z_out = sem("z_out")
        z_wide_in = sem("z_wide_in")
        sums_step = sem("sums_step")
        z_rows_ready = sem("z_rows_ready")
        last_z_psum = sem("last_z_psum")
        last_yT_ready = sem("last_yT_ready")
        sums_ready = sem("sums_ready")
        yT_ready = sem("yT_ready")
        out_psum = sem("out_psum")
        x_new_ready = sem("x_new_ready")
        x_out = [sem(f"x_out{a}") for a in range(HALVES)]
        new_var_ready = sem("new_var_ready")
        new_std_ready = sem("new_std_ready")
        dve_step = sem("dve_step")
        dve_turn = sem("dve_turn")
        sp_turn = sem("sp_turn")
        split_step = sem("split_step")
        stats_step = sem("stats_step")
        xnT_high_ready = sem("xnT_high_ready")
        v_enc_clear = sem("v_enc_clear")
        block = ctx.enter_context(nc.Block())

        S, DEN, Y, PR, OUT = psum[0:2], psum[2], psum[3:5], psum[5:7], psum[7]
        last_z = S + Y
        z_rows = q_stack[0][:, :, :].rearrange("p h n -> p (h n)").bitcast(F32)[:, 0:PAIRS * P].rearrange(
            "p (g m) -> p g m", m=P)
        VB = [OUT, PR[0], PR[1]]
        TURN = PR[1]
        NQK = 2 * NCH + 1
        LN_STEPS = 2 * TILES + 5
        VN = TILES * 2

        def x_round(i):
            return x[bass.ds(i * RT, RT), :].rearrange("(t p) d -> p t d", p=P)

        LATE, EARLY, ENC_KEYS = slice(0, P), slice(P, 3 * P), slice(3 * P, 4 * P)
        MASKED, WHOLE = slice(0, 2 * P), slice(2 * P, 4 * P)

        def qk_tile(j):
            bank = PR[j % 2]
            if j < NCH:
                return (lambda s: q_parts[:, s, j, :]), bank[:, :]
            if j < 2 * NCH:
                return ((lambda s: k_parts[:, s, j - NCH, :, 0:N]),
                        bank[:, :].rearrange("p (a n) -> p a n", a=HALVES))
            return ((lambda s: k_parts[:, s, :, :, N:KW].rearrange("p c a n -> p (c a) n")),
                    bank[:, 0:NCH * HALVES * ENC].rearrange("p (g n) -> p g n", n=ENC))

        @block.sync
        def _(sp):
            def load_ln(i):
                sp.dma_start(x_ln[:], x_round(i)).then_inc(x_ln_in, 16)

            def store_q(i):
                sp.wait_ge(part1_ready, i * NQK + NCH)
                sp.wait_ge(parts_ready, i * NQK + NCH)
                sp.dma_start(q_dram.rearrange("s c p t -> p s c t"), q_parts[:]).then_inc(parts_out, 16)

            def store_k(i):
                sp.wait_ge(part1_ready, i * NQK + NQK)
                sp.wait_ge(parts_ready, i * NQK + NQK)
                sp.dma_start(k_dram.rearrange("s c p t -> p s c t"),
                             k_parts[:].rearrange("p s c a w -> p s c (a w)")).then_inc(parts_out, 16)
                sp.wait_ge(parts_out, i * 32 + 32)
                sp.sem_inc(sp_turn, 1)

            def spread_z(i, a):
                n = i * 2 + a
                first = isinstance(n, int) and n == 0
                sp.wait_ge(z_ready, n + 1)
                sp.sem_inc(sp_turn, 1)
                if not first:
                    sp.wait_ge(z_wide_in, n * 32)
                for w in range(2):
                    for odd in range(2):
                        row = ROW_GROUP * (2 * odd + w)
                        sp.dma_start(z_dram[w].rearrange("(j o) n -> j o n", o=2)[:, odd, :],
                                     z[a][row:row + PAIRS // 2, :]).then_inc(z_out, 16)
                sp.wait_ge(z_out, n * 64 + 64)
                sp.sem_inc(sp_turn, 1)
                if not first:
                    sp.wait_ge(yT_ready, n * 2)
                for w in range(2):
                    sp.dma_start(z_wide[HD * w:HD * w + HD, :],
                                 z_dram[w].rearrange("p n -> (p n)").unsqueeze(0).broadcast_to([HD, PAIRS * N])
                                 ).then_inc(z_wide_in, 16)

            def load_stack(a):
                for s in range(SLOTS):
                    sp.dma_start(q_stack[a][FD * s:FD * s + FD, :, :],
                                 q_dram[Q_PART[s]].rearrange("c (h f) t -> f (c h) t", f=FD)[:, :, N * a:N * a + N]
                                 ).then_inc(stack_in[a], 16)
                    sp.dma_start(k_stack[a][FD * s:FD * s + FD, :, :],
                                 k_dram[K_PART[s]].rearrange("c (h f) t -> f (c h) t", f=FD)[:, :, KW * a:KW * a + KW]
                                 ).then_inc(stack_in[a], 16)

            def load_res(i, a):
                sp.dma_start(x_res[:, 2 * a:2 * a + 2, :], x_round(i)[:, 2 * a:2 * a + 2, :]
                             ).then_inc(x_res_in[a], 16)

            def store_out(i, a):
                sp.wait_ge(x_new_ready, i * 2 + a + 1)
                sp.sem_inc(sp_turn, 1)
                sp.dma_start(x_round(i)[:, 2 * a:2 * a + 2, :], x_new[a][:]).then_inc(x_out[a], 16)

            def round_(i, first, more, more_after):
                if first:
                    sp.wait_ge(xn_ready, TILES)
                    load_ln(1)
                    load_stack(1)
                else:
                    store_out(i - 1, 0)
                if more:
                    sp.wait_ge(stack_in[1], i * (32 * SLOTS) + 32 * SLOTS)
                    store_q(i + 1)
                    store_k(i + 1)
                if not first:
                    store_out(i - 1, 1)
                if more:
                    sp.wait_ge(scores_psum, i * (2 * STEPS) + STEPS)
                    load_stack(0)
                spread_z(i, 0)
                if more_after:
                    sp.wait_ge(xn_ready, i * TILES + 2 * TILES)
                    sp.sem_inc(sp_turn, 1)
                    load_ln(i + 2)
                for a in range(HALVES):
                    load_res(i, a)
                if more:
                    spread_z(i, 1)
                    sp.wait_ge(scores_psum, i * (2 * STEPS) + 2 * STEPS)
                    load_stack(1)

            load_ln(0)
            store_q(0)
            store_k(0)
            load_stack(0)
            round_(0, True, True, True)
            with sp.Fori(1, ROUNDS - 2) as i:
                round_(i, False, True, True)
            round_(ROUNDS - 2, False, True, False)
            round_(ROUNDS - 1, False, False, False)
            for a in range(HALVES):
                store_out(ROUNDS - 1, a)
            for a in range(HALVES):
                sp.wait_ge(x_out[a], ROUNDS * 16)

        @block.vector
        def _(dve):
            def layernorm_a(i):
                own = Steps(dve, dve_step, i * LN_STEPS)
                dve.wait_ge(x_ln_in, i * 16 + 16)
                for t in range(TILES):
                    own.done(nc.vector.bn_stats(stats[:, t, :], x_ln[:, t, :]))
                own.after()
                dve.sem_inc(dve_turn, 1)
                for t in range(TILES):
                    own.done(nc.vector.bn_aggr(mv[:, t, :], stats[:, t, :]))
                own.after()
                nc.vector.tensor_scalar(var[:, :], mv[:, :, 1], LN_EPS, None, ALU.add).then_inc(var_ready, 1)

            def layernorm_b(i):
                own = Steps(dve, dve_step, i * LN_STEPS + 2 * TILES)
                dve.wait_ge(std_ready, i + 1)
                own.done(nc.vector.reciprocal(ln_tmp[:, 0, :], std[:, :]))
                own.after()
                own.done(nc.vector.tensor_tensor(ln_tmp[:, 1, :], var[:, :], ln_tmp[:, 0, :], ALU.mult))
                own.after()
                own.done(nc.vector.tensor_tensor(ln_tmp[:, 2, :], ln_tmp[:, 1, :], std[:, :], ALU.add))
                own.after()
                own.done(nc.vector.tensor_scalar(ln_tmp[:, 0, :], ln_tmp[:, 2, :], 0.5, None, ALU.mult))
                own.after()
                own.done(nc.vector.reciprocal(rstd[:, :], ln_tmp[:, 0, :]))
                own.after()
                for t in range(TILES):
                    nc.vector.tensor_scalar(xn[:, t, :], x_ln[:, t, :], mv[:, t, 0:1], rstd[:, t:t + 1],
                                            ALU.subtract, ALU.mult).then_inc(xn_ready, 1)

            def split(i, j):
                own = Steps(dve, split_step, i * (2 * NQK) + 2 * j)
                tile, bank = qk_tile(j)
                dve.wait_ge(part1_ready, i * NQK + j + 1)
                r = rest[j % 2][:, 0:tile(0).shape[1] * (tile(0).shape[2] if len(tile(0).shape) == 3 else 1)]
                if len(tile(0).shape) == 3:
                    r = r.rearrange("p (a w) -> p a w", a=tile(0).shape[1])
                own.done(nc.vector.tensor_tensor(r, bank, tile(0), ALU.subtract))
                own.after()
                own.done(nc.vector.tensor_copy(tile(1), r))
                own.after()
                nc.vector.tensor_tensor(tile(2), r, tile(1), ALU.subtract).then_inc(parts_ready, 1)

            def mask(i, s):
                tile = att[s % 4]
                dve.wait_ge(squares_ready, i * (2 * STEPS) + 2 * s + 2)
                nc.vector.scalar_tensor_tensor(tile[:, :, MASKED], tile[:, :, MASKED], HALF,
                                               consts["causal"][:, :].unsqueeze(1).broadcast_to([P, 2, 2 * P]),
                                               ALU.add, ALU.mult).then_inc(att_ready, 1)
                nc.vector.tensor_scalar(tile[:, :, WHOLE], tile[:, :, WHOLE], HALF, None,
                                        ALU.add).then_inc(att_ready, 1)

            def invert(i, a):
                dve.wait_ge(den_ready, i * 2 + a + 1)
                nc.vector.reciprocal(z[a][:, :], den[a][:, :]).then_inc(z_ready, 1)

            def values_enc(i):
                for a in range(HALVES):
                    dve.wait_ge(v_psum, i * (VN + HALVES) + a + 1)
                    for w in range(2):
                        rows = slice(ENC * w, ENC * w + ENC)
                        nc.vector.tensor_copy(v_enc[rows, a, :, HD * w:HD * w + HD],
                                              PR[a][rows, :].rearrange("p (g e) -> p g e", e=HD)
                                              ).then_inc(v_enc_ready, 1)

            def residual(i, a):
                own = Steps(dve, stats_step, (i * 2 + a) * 11)
                dve.wait_ge(x_res_in[a], i * 16 + 16)
                dve.wait_ge(out_psum, i * 2 + a + 1)
                wait_unless_first(dve, x_out[a], i * 16)
                nc.vector.tensor_tensor(x_new[a][:], OUT[:, 0:2 * D].rearrange("p (t d) -> p t d", d=D),
                                        x_res[:, 2 * a:2 * a + 2, :], ALU.add).then_inc(x_new_ready, 1)
                dve.wait_ge(x_new_ready, i * 2 + a + 1)
                for t in range(2):
                    own.done(nc.vector.bn_stats(new_stats[:, t, :], x_new[a][:, t, :]))
                own.after()
                dve.sem_inc(dve_turn, 1)
                for t in range(2):
                    own.done(nc.vector.bn_aggr(new_mv[:, t, :], new_stats[:, t, :]))
                own.after()
                nc.vector.tensor_scalar(new_var[:, :], new_mv[:, :, 1], LN_EPS, None, ALU.add
                                        ).then_inc(new_var_ready, 1)

            def normalise_new(i, a):
                own = Steps(dve, stats_step, (i * 2 + a) * 11 + 4)
                dve.wait_ge(new_std_ready, i * 2 + a + 1)
                own.done(nc.vector.reciprocal(new_tmp[:, 0, :], new_std[:, :]))
                own.after()
                own.done(nc.vector.tensor_tensor(new_tmp[:, 1, :], new_var[:, :], new_tmp[:, 0, :], ALU.mult))
                own.after()
                own.done(nc.vector.tensor_tensor(new_tmp[:, 2, :], new_tmp[:, 1, :], new_std[:, :], ALU.add))
                own.after()
                own.done(nc.vector.tensor_scalar(new_tmp[:, 0, :], new_tmp[:, 2, :], 0.5, None, ALU.mult))
                own.after()
                own.done(nc.vector.reciprocal(new_tmp[:, 3, :], new_tmp[:, 0, :]))
                own.after()
                dve.sem_inc(dve_turn, 1)
                for t in range(2):
                    own.done(nc.vector.tensor_scalar(
                        rows[:, bass.ds(i * TILES + (2 * a + t), 1), 0:D].rearrange("p o d -> p (o d)"),
                        x_new[a][:, t, :], new_mv[:, t, 0:1], new_tmp[:, 3, t:t + 1], ALU.subtract, ALU.mult))
                own.after()

            def split_tokens(i):
                dve.wait_ge(xnT_high_ready, i + 1)
                nc.vector.tensor_tensor(xnT[1][:, :], TURN[:, :], xnT[0][:, :].bitcast(F32), ALU.subtract
                                        ).then_inc(xnT_ready, 1)

            def round_(i, first, more):
                for s in range(STEPS):
                    if more and s == LN_STEP:
                        layernorm_a(i + 1)
                    mask(i, s)
                    if more and s == LN_STEP:
                        layernorm_b(i + 1)
                    if more and s == TURN_STEP:
                        split_tokens(i + 1)
                    if more and 0 <= s - QK_STEP < NQK:
                        split(i + 1, s - QK_STEP)
                    if s == INVERT_STEP:
                        invert(i, 0)
                    for a in range(HALVES):
                        if s == RESIDUAL_STEP[a] and not first:
                            residual(i - 1, a)
                        if s == RESIDUAL_STEP[a] + 1 and not first:
                            normalise_new(i - 1, a)
                if not more:
                    dve.wait_ge(scores_psum, i * (2 * STEPS) + STEPS)
                    for p in range(PAIRS):
                        for w in range(2):
                            row = ROW_GROUP * (2 * (p % 2) + w) + p // 2
                            nc.vector.tensor_copy(z_rows[:, p, HD * w:HD * w + HD], consts["ident"][:, row:row + 1]
                                                  .broadcast_to([P, HD])).then_inc(z_rows_ready, 1)
                if more:
                    dve.wait_ge(y_psum, i * STEPS + STEPS)
                    values_enc(i + 1)
                invert(i, 1)

            layernorm_a(0)
            layernorm_b(0)
            split_tokens(0)
            for j in range(NQK):
                split(0, j)
            dve.wait_ge(v_enc_clear, 1)
            values_enc(0)
            round_(0, True, True)
            with dve.Fori(1, ROUNDS - 1) as i:
                round_(i, False, True)
            round_(ROUNDS - 1, False, False)
            dve.wait_ge(y_copied, ROUNDS * STEPS)
            for g in range(PAIRS // 2):
                dve.wait_ge(last_z_psum, g + 1)
                part = yT[1][:, 2 * g:2 * g + 2, :].rearrange("p g n -> p (g n)")
                nc.vector.tensor_tensor(part, part, last_z[g][:, :], ALU.mult).then_inc(last_yT_ready, 1)
            for a in range(HALVES):
                residual(ROUNDS - 1, a)
                normalise_new(ROUNDS - 1, a)

        @block.scalar
        def _(act):
            def square_root(i):
                act.wait_ge(var_ready, i + 1)
                nc.scalar.activation(std[:, :], var[:, :], ACT.Sqrt).then_inc(std_ready, 1)

            def root_new(i, a):
                act.wait_ge(new_var_ready, i * 2 + a + 1)
                nc.scalar.activation(new_std[:, :], new_var[:, :], ACT.Sqrt).then_inc(new_std_ready, 1)

            def turn(i):
                act.wait_ge(turned, i + 1)
                nc.scalar.copy(xnT_enc[:], TURN[:, :].rearrange("d (a n) -> d a n", a=HALVES)[:, :, 0:ENC])
                nc.scalar.copy(xnT[0][:, :], TURN[:, :]).then_inc(xnT_high_ready, 1)

            def first_part(i, j):
                tile, bank = qk_tile(j)
                act.wait_ge(qk_psum, i * NQK + j + 1)
                nc.scalar.copy(tile(0), bank).then_inc(part1_ready, 1)

            def square(i, s):
                n = i * (2 * STEPS) + 2 * s
                for w in range(2):
                    act.wait_ge(scores_psum, n + w + 1)
                    nc.scalar.activation(att[s % 4][:, w, :], S[w][:, :], ACT.Square, bias=HEAD_SHIFT,
                                         scale=HEAD_SCALE).then_inc(squares_ready, 1)

            def copy_y(i, s):
                act.wait_ge(y_psum, i * STEPS + s + 1)
                nc.scalar.copy(yT[s // PAIRS][:, s % PAIRS, :], Y[s % 2][:, 0:N]).then_inc(y_copied, 1)

            def denominators(i, a):
                act.wait_ge(den_psum, i * 2 + a + 1)
                nc.scalar.activation(den[a][:, :], DEN[:, 0:N], ACT.Identity, bias=Z_EPS).then_inc(den_ready, 1)

            def values(i):
                for m in range(VN):
                    act.wait_ge(v_psum, i * (VN + HALVES) + HALVES + m + 1)
                    nc.scalar.copy(v[:, m // 2, 512 * (m % 2):512 * (m % 2) + 512], VB[m % 3][:, :]
                                   ).then_inc(v_ready, 1)

            def round_(i, first, more):
                for s in range(STEPS):
                    square(i, s)
                    if s >= LAG:
                        copy_y(i, s - LAG)
                    if s == PAIRS + LAG - 1:
                        denominators(i, 0)
                    for a in range(HALVES):
                        if s == RESIDUAL_STEP[a] + 1 and not first:
                            root_new(i - 1, a)
                    if more and s == LN_STEP:
                        square_root(i + 1)
                    if more and s == TURN_STEP:
                        turn(i + 1)
                    if more and 0 <= s - QK_STEP < NQK:
                        if s == QK_STEP:
                            act.wait_ge(parts_out, i * 32 + 32)
                        first_part(i + 1, s - QK_STEP)
                for s in range(STEPS - LAG, STEPS):
                    copy_y(i, s)
                denominators(i, 1)
                if more:
                    values(i + 1)

            square_root(0)
            turn(0)
            for j in range(NQK):
                first_part(0, j)
            values(0)
            round_(0, True, True)
            with act.Fori(1, ROUNDS - 1) as i:
                round_(i, False, True)
            round_(ROUNDS - 1, False, False)
            for a in range(HALVES):
                root_new(ROUNDS - 1, a)

        @block.tensor
        def _(pe):
            def turn(i):
                pe.wait_ge(xn_ready, i * TILES + TILES)
                for t in range(TILES):
                    mm = nc.tensor.transpose(TURN[:, P * t:P * t + P], xn[:, t, :], consts["ident"][:, :])
                mm.then_inc(turned, 1)

            def project(i, j):
                if j >= 2:
                    pe.wait_ge(parts_ready, i * NQK + j - 1)
                bank = PR[j % 2]
                if j < 2 * NCH:
                    w, c = parts[("wq", "wk")[j // NCH]], j % NCH
                    for m, (k, l) in enumerate(PART_PAIRS):
                        mm = nc.tensor.matmul(bank[:, :], w[k][:, P * c:P * c + P], xnT[l][:, :], start=(m == 0),
                                              stop=(m == 2))
                else:
                    enc = [x[:, :].rearrange("d (a n) -> d a n", a=HALVES)[:, :, 0:ENC] for x in xnT]
                    for c in range(NCH):
                        for m, (k, l) in enumerate(PART_PAIRS):
                            mm = nc.tensor.matmul(bank[:, P * c:P * c + P], parts["wke"][k][:, P * c:P * c + P],
                                                  enc[l], start=(m == 0), stop=(m == 2))
                mm.then_inc(qk_psum, 1)

            def values_of_encoder(i):
                heads = wT["wve"][:, :].rearrange("d (g w e) -> d w g e", w=2, e=HD)
                for a in range(HALVES):
                    for w in range(2):
                        mm = nc.tensor.matmul(PR[a][ENC * w:ENC * w + ENC, :], xnT_enc[:, a, :],
                                              heads[:, w], start=True, stop=True)
                    mm.then_inc(v_psum, 1)

            def values(i):
                for m in range(VN):
                    t, w = m // 2, m % 2
                    if 1 <= m < 3:
                        pe.wait_ge(v_enc_ready, i * (2 * HALVES) + 2 * m)
                    elif m >= 3:
                        pe.wait_ge(v_ready, i * VN + m - 2)
                    for n, (k, l) in enumerate(PART_PAIRS):
                        mm = nc.tensor.matmul(VB[m % 3][:, :], xnT[k][:, P * t:P * t + P],
                                              parts["wv"][l][:, 512 * w:512 * w + 512], start=(n == 0), stop=(n == 2))
                    mm.then_inc(v_psum, 1)

            def scores(i, s):
                a, p = s // PAIRS, s % PAIRS
                if p == 0:
                    pe.wait_ge(stack_in[a], i * (32 * SLOTS) + 32 * SLOTS)
                for w in range(2):
                    h = 2 * p + w
                    if s >= 1:
                        pe.wait_ge(squares_ready, i * (2 * STEPS) + 2 * s + w - 1)
                    nc.tensor.matmul(S[w][:, LATE], k_stack[a][:, h, P:2 * P], q_stack[a][:, h, P:2 * P],
                                     start=True, stop=True)
                    nc.tensor.matmul(S[w][:, EARLY], k_stack[a][:, h, 0:P], q_stack[a][:, h, :],
                                     start=True, stop=True)
                    for x in range(2):
                        mm = nc.tensor.matmul(S[w][ENC * x:ENC * x + ENC, ENC_KEYS], k_stack[a][:, 2 * p + x, N:KW],
                                              q_stack[a][:, 2 * p + x, P * w:P * w + P], start=True, stop=True)
                    mm.then_inc(scores_psum, 1)

            def weighted(i, s):
                u, a, p = s % 2, s // PAIRS, s % PAIRS
                tile = att[s % 4]
                pe.wait_ge(att_ready, i * (2 * STEPS) + 2 * s + 2)
                if s == 0:
                    pe.wait_ge(v_ready, i * VN + VN)
                    pe.wait_ge(v_enc_ready, i * (2 * HALVES) + 2 * HALVES)
                if s >= 2:
                    pe.wait_ge(y_copied, i * STEPS + s - 1)
                for late in range(2):
                    for w in range(2):
                        h = 2 * p + w
                        nc.tensor.matmul(Y[u][HD * w:HD * w + HD, P * late:N], v[:, 2 * a + late, HD * h:HD * h + HD],
                                         tile[:, w, LATE if late else EARLY], start=(late == 0), stop=False,
                                         skip_group_check=True)
                nc.tensor.matmul(Y[u][:, 0:N], v_enc[:, a, p, :], tile[:, :, ENC_KEYS], start=False,
                                 stop=True, skip_group_check=True).then_inc(y_psum, 1)

            def denominators(i, s):
                a, j = s // PAIRS, s % PAIRS // 2
                heads = [(slice(ROW_GROUP * g, ROW_GROUP * g + ROW_GROUP), (s + g // 2) % 4, g % 2) for g in range(4)]
                for rows, u, w in heads:
                    nc.tensor.matmul(DEN[rows, 0:P], consts["sum_rows"][:, j, :], att[u][:, w, P:2 * P],
                                     start=(j == 0), stop=False, skip_group_check=True)
                for rows, u, w in heads:
                    nc.tensor.matmul(DEN[rows, 0:P], consts["sum_enc_rows"][:, w, j, :], att[u][:, 0, ENC_KEYS],
                                     start=False, stop=False, skip_group_check=True)
                pe.wait_ge(sums_ready, (i * STEPS + s) * 2 + 4)
                for rows, u, w in heads:
                    mm = nc.tensor.matmul(DEN[rows, P:N], consts["sum_rows"][:, j, :], sums[u][:, w, :],
                                          start=False, stop=(j == PAIRS // 2 - 1), skip_group_check=True)
                if j == PAIRS // 2 - 1:
                    mm.then_inc(den_psum, 1)

            def project_out(i, a, tiles=(0, 1), scaled=False):
                if not scaled:
                    pe.wait_ge(yT_ready, (i * 2 + a) * 2 + 2)
                for t in tiles:
                    for p in range(PAIRS):
                        mm = nc.tensor.matmul(OUT[:, D * t:D * t + D], yT[a][:, p, P * t:P * t + P],
                                              wT["wout"][:, D * p:D * p + D], start=(p == 0), stop=(p == PAIRS - 1))
                if 1 in tiles:
                    mm.then_inc(out_psum, 1)

            def round_(i, first, more):
                for s in range(STEPS):
                    scores(i, s)
                    if s >= LAG:
                        weighted(i, s - LAG)
                    if s >= LAG and (s - LAG) % 2:
                        denominators(i, s - LAG - 1)
                    if more and s == TURN_STEP:
                        pe.wait_ge(v_ready, i * VN + VN)
                        turn(i + 1)
                    if more and 0 <= s - QK_STEP < NQK:
                        if s == QK_STEP:
                            pe.wait_ge(xnT_ready, i + 2)
                        project(i + 1, s - QK_STEP)
                    if not first:
                        if s == OUT_STEP[0]:
                            pe.wait_ge(v_ready, i * VN + VN - 1)
                            project_out(i - 1, 0, (0,))
                        if s == OUT_STEP[0] + 1:
                            project_out(i - 1, 0, (1,))
                        if s == OUT_STEP[1]:
                            pe.wait_ge(x_new_ready, i * 2 - 1)
                            project_out(i - 1, 1)
                weighted(i, STEPS - 2)
                if more:
                    pe.wait_ge(parts_ready, (i + 1) * NQK + NQK)
                    values_of_encoder(i + 1)
                weighted(i, STEPS - 1)
                denominators(i, STEPS - 2)
                if more:
                    values(i + 1)

            turn(0)
            pe.wait_ge(xnT_ready, 1)
            for j in range(NQK):
                project(0, j)
            pe.wait_ge(parts_ready, NQK)
            values_of_encoder(0)
            values(0)
            round_(0, True, True)
            with pe.Fori(1, ROUNDS - 1) as i:
                round_(i, False, True)
            round_(ROUNDS - 1, False, False)
            pe.wait_ge(z_ready, ROUNDS * 2)
            pe.wait_ge(z_rows_ready, 2 * PAIRS)
            pe.wait_ge(squares_ready, ROUNDS * (2 * STEPS))
            pe.wait_ge(y_copied, ROUNDS * STEPS)
            for p in range(PAIRS):
                mm = nc.tensor.matmul(last_z[p // 2][:, N * (p % 2):N * (p % 2) + N], z_rows[:, p, :], z[1][:, :],
                                      start=True, stop=True)
                if p % 2:
                    mm.then_inc(last_z_psum, 1)
            project_out(ROUNDS - 1, 0)
            pe.wait_ge(x_new_ready, ROUNDS * 2 - 1)
            pe.wait_ge(last_yT_ready, PAIRS // 2)
            project_out(ROUNDS - 1, 1, scaled=True)

        @block.gpsimd
        def _(pool):
            nc.gpsimd.memset(v_enc[:], 0.0).then_inc(v_enc_clear, 1)

            def add_keys(i, s):
                tile, total = att[s % 4], sums[s % 4]
                pool.wait_ge(att_ready, i * (2 * STEPS) + 2 * s + 2)
                nc.gpsimd.tensor_tensor(total[:, :, :], tile[:, :, 2 * P:3 * P], tile[:, :, LATE], ALU.add
                                        ).then_inc(sums_step, 1)
                pool.wait_ge(sums_step, i * STEPS + s + 1)
                for x in range(2):
                    rows = slice(ENC * x, ENC * x + ENC)
                    nc.gpsimd.tensor_tensor(total[rows, x, :], total[rows, x, :], tile[rows, 1, ENC_KEYS], ALU.add
                                            ).then_inc(sums_ready, 1)
                pool.wait_ge(sums_ready, (i * STEPS + s) * 2 + 2)

            def scale(i, a, w):
                if w == 0:
                    pool.wait_ge(z_wide_in, (i * 2 + a) * 32 + 32)
                    pool.wait_ge(y_copied, i * STEPS + PAIRS * (a + 1))
                part = yT[a][:, PAIRS // 2 * w:PAIRS // 2 * w + PAIRS // 2, :].rearrange("p g n -> p (g n)")
                nc.gpsimd.tensor_tensor(part, part, z_wide[:, PAIRS // 2 * N * w:PAIRS // 2 * N * (w + 1)],
                                        ALU.mult).then_inc(yT_ready, 1)

            def round_(i, first):
                for s in range(STEPS):
                    add_keys(i, s)
                    if 0 <= s - SCALE_STEP < 2 and not first:
                        scale(i - 1, 1, s - SCALE_STEP)
                for w in range(2):
                    scale(i, 0, w)

            round_(0, True)
            with pool.Fori(1, ROUNDS) as i:
                round_(i, False)


def make_constants(nc, consts, raw, psum, weights, stage, inputs, tokens, turn):
    with ExitStack() as ctx:
        def sem(n):
            return ctx.enter_context(nc.semaphore(f"setup_{n}"))
        pool_step = sem("pool_step")
        masks_ready = sem("masks_ready")
        converted = sem("converted")
        wr_clear = sem("wr_clear")
        b1_in = sem("b1_in")
        b1T_psum = sem("b1T_psum")
        block = ctx.enter_context(nc.Block())

        @block.sync
        def _(sp):
            sp.dma_start(stage["b1"][:, :], inputs["b1"].rearrange("e (k p) -> (e k) p", p=P)).then_inc(b1_in, 16)
            load_tokens(sp, tokens[0], inputs["x"].rearrange("(c p) d -> p c d", p=P), tokens[1])
            sp.wait_ge(wr_clear, 1)
            sp.dma_start(weights["wr"][:, 0:E], inputs["wr"]).then_inc(weights["wr_in"], 16)
            for rows, source in turn["sources"]:
                sp.dma_start(rows, source).then_inc(turn["loaded"], 16)
            sp.dma_start(weights["w2"][:, :].rearrange("p (e k d) -> p e k d", e=E, k=HC),
                         inputs["w2"].rearrange("e (k p) d -> p e k d", p=P)).then_inc(weights["w2_in"], 16)
            sp.dma_start(weights["b2"][:, :], inputs["b2"].rearrange("e d -> (e d)").unsqueeze(0)
                         .broadcast_to([P, E * D])).then_inc(weights["b2_in"], 16)

        @block.gpsimd
        def _(pool):
            own = Steps(pool, pool_step)
            nc.gpsimd.memset(weights["wr"][:, :], 0.0).then_inc(wr_clear, 1)
            own.done(nc.gpsimd.memset(raw["ones"][:, :], 1.0))
            own.done(nc.gpsimd.iota(raw["column"][:, :], pattern=[[1, P]], base=0, channel_multiplier=0))
            own.done(nc.gpsimd.iota(raw["row"][:, :], pattern=[[0, 1]], base=0, channel_multiplier=1))
            own.done(nc.gpsimd.iota(raw["shift"][:, :], pattern=[[-2, DIGITS]], base=BITS - 2, channel_multiplier=0))
            own.done(nc.gpsimd.iota(raw["distance"][:, :], pattern=[[1, P]], base=P, channel_multiplier=-1))
            for j in range(3):
                own.done(nc.gpsimd.memset(raw["digit"][:, j, :], j + 1))
            own.after()
            nc.gpsimd.affine_select(out=consts["tri_f"][:, :], in_=raw["ones"][:, :], compare_op=ALU.is_ge, fill=0.0,
                                    base=0, pattern=[[1, P]], channel_multiplier=-1).then_inc(masks_ready, 1)
            nc.gpsimd.affine_select(out=consts["ident"][:, :], in_=raw["ones"][:, :], compare_op=ALU.is_equal,
                                    fill=0.0, base=0, pattern=[[1, P]], channel_multiplier=-1
                                    ).then_inc(masks_ready, 1)

        @block.vector
        def _(dve):
            own = Steps(dve, converted)
            dve.wait_ge(pool_step, 8)
            own.done(nc.vector.tensor_copy(consts["iota_f"][:, :], raw["column"][:, :]))
            own.done(nc.vector.tensor_copy(consts["part"][:, :], raw["row"][:, :]))
            own.done(nc.vector.tensor_copy(consts["ones"][:, :], raw["ones"][:, :]))
            for j in range(3):
                own.done(nc.vector.tensor_tensor(consts["digits"][:, 0:DIGITS, j], raw["digit"][:, j, :],
                                                 raw["shift"][:, :], ALU.logical_shift_left))
            own.done(nc.vector.memset(consts["digits"][:, DIGITS, :], 0))
            own.done(nc.vector.memset(consts["restart"][:, :], 1.0))
            own.done(nc.vector.tensor_scalar(raw["phase"][:, :], raw["distance"][:, :], E - 1, None, ALU.bitwise_and))
            own.after()
            for j, value in enumerate((1, 3, 1)):
                own.done(nc.vector.tensor_copy(consts["digit_terms"][:, :, j],
                                               consts["digits"][:, 0:DIGITS, value - 1]))
            own.done(nc.vector.memset(consts["restart"][:, :].rearrange("p (e c) -> p e c", e=E)[:, :, 0:1], 0.0))
            own.done(nc.vector.tensor_scalar(consts["same_expert"][:, :], raw["phase"][:, :], 0.0, None,
                                             ALU.is_equal))
            G = PAIRS // 2
            own.done(nc.vector.memset(consts["sum_rows"][:, :, 0:G], 0.0))
            own.done(nc.vector.memset(consts["sum_rows"][:, :, G:ROW_GROUP], 1.0))
            own.done(nc.vector.memset(consts["sum_enc_rows"][:, :, :, :], 0.0))
            own.after()
            for j in range(G):
                own.done(nc.vector.memset(consts["sum_rows"][:, j, j:j + 1], 1.0))
            own.after()
            for w in range(2):
                half = slice(ENC * w, ENC * w + ENC)
                own.done(nc.vector.tensor_copy(consts["sum_enc_rows"][half, w, :, :], consts["sum_rows"][half, :, :]))
            dve.wait_ge(masks_ready, 2)
            for w in range(2):
                own.done(nc.vector.tensor_copy(consts["causal"][:, P * w:P * w + P], consts["tri_f"][:, :]))
            own.done(nc.vector.tensor_copy(consts["tri"][:, :], consts["tri_f"][:, :]))
            dve.wait_ge(b1T_psum, 1)
            own.done(nc.vector.tensor_copy(weights["b1"][:, :], psum[0][:, 0:E * HC]))

        @block.tensor
        def _(pe):
            pe.wait_ge(b1_in, 16)
            pe.wait_ge(masks_ready, 2)
            nc.tensor.transpose(psum[0][:, 0:E * HC], stage["b1"][:, :], consts["ident"][0:E * HC, 0:E * HC]
                                ).then_inc(b1T_psum, 1)


def build(nc, x, wq, wk, wv, wke, wve, wout, wr, w1, b1, w2, b2, out):
    with ExitStack() as ctx:
        def sb(name, shape, dt=F32):
            return ctx.enter_context(nc.sbuf_tensor(name, shape, dt))

        psum = [ctx.enter_context(nc.psum_tensor(f"bank{i}", [P, 512], F32)) for i in range(8)]
        consts = {
            "tri_f": sb("tri_f", [P, P]), "ident": sb("ident", [P, P]), "iota_f": sb("iota_f", [P, P], BF16),
            "part": sb("part", [P, 1]), "ones": sb("ones", [P, P], BF16), "digits": sb("digits", [P, DIGITS + 1, 3], I32),
            "digit_terms": sb("digit_terms", [P, DIGITS, 3]), "restart": sb("restart", [P, C * E]),
            "same_expert": sb("same_expert", [P, P], BF16), "tri": sb("tri", [P, P], BF16),
            "causal": sb("causal", [P, 2 * P]), "sum_rows": sb("sum_rows", [P, PAIRS // 2, ROW_GROUP]),
            "sum_enc_rows": sb("sum_enc_rows", [P, 2, PAIRS // 2, ROW_GROUP])}
        weights = {"wr": sb("wr", [D, ROW_GROUP]), "w1": [sb(f"w1_{u}", [D, HID]) for u in range(2)], "w1_dram": w1,
                   "w2": sb("w2", [P, E * HC * D]), "b2": sb("b2", [P, E * D]), "b1": sb("b1", [P, E * HC])}
        table = nc.dram_tensor("dispatch_table", [T, ROW], F32, kind="Internal").ap()
        q_dram = nc.dram_tensor("q_parts_dram", [3, NCH, P, RT], BF16, kind="Internal").ap()
        k_dram = nc.dram_tensor("k_parts_dram", [3, NCH, P, HALVES * KW], BF16, kind="Internal").ap()
        z_dram = nc.dram_tensor("z_dram", [2, PAIRS, N], F32, kind="Internal").ap()
        wT = {"wve": sb("wveT", [D, H * HD]), "wout": sb("woutT", [P, PAIRS * D])}
        parts = {n: [sb(f"{n}T_{part}", [D, width], F32R) for part in ("high", "low")]
                 for n, width in (("wq", H * FD), ("wk", H * FD), ("wke", H * FD), ("wv", H * HD))}
        weights.update({n: ctx.enter_context(nc.semaphore(n)) for n in ("wr_in", "w2_in", "b2_in")})
        x_flat = x.rearrange("b n d -> (b n) d")
        out_flat = out.rearrange("b n d -> (b n) d")
        with ExitStack() as first:
            def raw_sb(name, shape, dt=F32):
                return first.enter_context(nc.sbuf_tensor(name, shape, dt))

            raw = {
                "ones": raw_sb("raw_ones", [P, P]), "column": raw_sb("raw_column", [P, P], I32),
                "row": raw_sb("raw_row", [P, 1], I32), "shift": raw_sb("raw_shift", [P, DIGITS], I32),
                "distance": raw_sb("raw_distance", [P, P], I32), "digit": raw_sb("raw_digit", [P, 3, DIGITS], I32),
                "phase": raw_sb("raw_phase", [P, P], I32)}
            tokens = (raw_sb("first_tokens", [P, C, D]),
                      [first.enter_context(nc.semaphore(f"first_tokens_in{i}")) for i in range(4)])
            whole = {n: raw_sb(f"{n}T", [D, parts[n][0].shape[1]]) for n in parts}
            turn = {"whole": whole, "parts": parts, "sources": [], "blocks": [], "loaded": first.enter_context(nc.semaphore("attn_weights_in"))}
            for n, w in (("wq", wq), ("wk", wk), ("wke", wke), ("wv", wv), ("wve", wve)):
                tiles = w.shape[0] // P
                rows = raw_sb(f"{n}_rows", [P, tiles, D])
                turn["sources"].append((rows[:], w.rearrange("(c p) d -> p c d", p=P)))
                turn["blocks"] += [(rows[:, i, :], {**wT, **whole}[n], P * i) for i in range(tiles)]
            rows = raw_sb("wout_rows", [D, H * HD])
            turn["sources"].append((rows[:, :], wout))
            turn["blocks"] += [(rows[:, P * i:P * i + P], wT["wout"], P * i) for i in range(PAIRS)]
            turn["loads"] = len(turn["sources"])
            make_constants(nc, consts, raw, psum, weights, {"b1": raw_sb("b1_rows", [E * HC, P])},
                           {"x": x_flat, "wr": wr, "w1": w1, "b1": b1, "w2": w2, "b2": b2}, tokens, turn)
            ffn_stage(nc, "ffn1", consts, weights, psum, out_flat, table, tokens[0], tokens[1], turn=turn)
        rows = sb("rows", [P, C, ROW])
        attention(nc, psum, consts, wT, parts, out_flat, rows, (q_dram, k_dram, z_dram))
        ffn_stage(nc, "ffn2", consts, weights, psum, out_flat, table, None, None, rows=rows)

_INS = ['L0_attn_x', 'L0_attn_Wq', 'L0_attn_Wk', 'L0_attn_Wv', 'L0_attn_Wk_enc', 'L0_attn_Wv_enc', 'L0_attn_Wout',
        'L0_ffn_Wr', 'L0_ffn_W1', 'L0_ffn_b1', 'L0_ffn_W2', 'L0_ffn_b2']
_OUTS = [((16, 256, 128), 'float32')]


def kernel(**inputs):
    import numpy as _np
    import concourse.bacc as _bacc
    from concourse import mybir as _mybir
    from concourse.bass_utils import run_bass_kernel_spmd as _run

    nc = _bacc.Bacc("TRN2", target_bir_lowering=False, num_devices=1)
    arrays, args = {}, []
    for name in _INS:
        a = _np.ascontiguousarray(inputs[name])
        arrays[f"in_{name}_dram"] = a
        args.append(nc.dram_tensor(f"in_{name}_dram", a.shape, _mybir.dt.from_np(a.dtype), kind="ExternalInput").ap())
    for i, (shape, dtype) in enumerate(_OUTS):
        dt = _mybir.dt.from_np(_np.dtype(dtype))
        args.append(nc.dram_tensor(f"out_{i}_dram", shape, dt, kind="ExternalOutput").ap())
    build(nc, *args)
    r = _run(nc, [arrays], core_ids=[0])
    got = tuple(r.results[0][f"out_{i}_dram"] for i in range(len(_OUTS)))
    return got[0]
```
